# Optimizing a Trainium2 kernel written in Bass

```python
import numpy as np
import jax
import jax.numpy as jnp

def _softmax(x, axis=-1):
    return jax.nn.softmax(x, axis=axis)

def _gelu(x):
    return jax.nn.gelu(x, approximate=True)

def _silu(x):
    return jax.nn.silu(x)

def _sigmoid(x):
    return jax.nn.sigmoid(x)

def _layernorm(x, axis=-1, eps=1e-05):
    m = jnp.mean(x, axis=axis, keepdims=True)
    v = jnp.var(x, axis=axis, keepdims=True)
    return (x - m) / jnp.sqrt(v + eps)

def _scatter_add(tgt, idx, src, axis=0):
    return tgt.at[idx].add(src)

def _segment_sum(src, seg, n):
    return jax.ops.segment_sum(src, seg, n)
kernel_name = 'mk_gnn_resnorm_d2_gnn_r32_025537'

def setup_inputs(seed: int=0):
    np.random.seed(seed)
    _w = jnp.asarray

    def _rec_inputs():
        import jax
        import jax.numpy as jnp
        _gk = jax.random.key(seed)
        x = -0.000202 + 1 * jax.random.normal(jax.random.fold_in(_gk, 1), (3125, 64), jnp.float32)
        src = jax.random.randint(jax.random.fold_in(_gk, 2), (100000,), 0, 3125, jnp.int32)
        dst = jax.random.randint(jax.random.fold_in(_gk, 3), (100000,), 0, 3125, jnp.int32)
        _o = jnp.argsort(dst, stable=True)
        src = src[_o]
        dst = dst[_o]
        edge_attr_64 = -8.16379e-05 + 0.999858 * jax.random.normal(jax.random.fold_in(_gk, 11), (100000, 64), jnp.float32)
        edge_type_500 = jax.random.randint(jax.random.fold_in(_gk, 13), (100000,), 0, 500, jnp.int32)
        return (x, src, dst, edge_attr_64, edge_type_500)
    x, src, dst, edge_attr_64, edge_type_500 = _rec_inputs()

    def _L0_gnn_setup():
        import jax, jax.numpy as jnp
        import numpy as np
        N = 3125
        E = 50000
        D = 64
        key = jax.random.key(seed)
        ks = jax.random.split(key, 6)
        scale = 1.0 / np.sqrt(3 * D)
        return {'h_e': jax.random.normal(ks[0], (N, D), dtype=jnp.float32), 'h_r': jax.random.normal(ks[1], (E, D), dtype=jnp.float32), 'W1': jax.random.normal(ks[2], (3 * D, D), dtype=jnp.float32) * scale, 'b1': jnp.zeros((D,), dtype=jnp.float32), 'W2': jax.random.normal(ks[3], (3 * D, D), dtype=jnp.float32) * scale, 'b2': jnp.zeros((D,), dtype=jnp.float32), 'edge_index': jax.random.randint(ks[4], (2, E), 0, N, dtype=jnp.int64)}
    _L0_gnn_all = _L0_gnn_setup()
    _L0_gnn_in = {k: v for k, v in _L0_gnn_all.items() if k in ('W1', 'b1', 'W2', 'b2')}
    del _L0_gnn_all

    def _L1_gnn_setup():
        import jax, jax.numpy as jnp
        import numpy as np
        N_ENT, N_REL, N_EDGE = (50000, 500, 15625)
        L_LAYERS, HEADS, DIM = (2, 2, 64)
        POW_ITER, ALPHA, LN_EPS = (3, 0.15, 1e-05)

        def _layernorm(x, g, b):
            mu = jnp.mean(x, axis=-1, keepdims=True)
            var = jnp.mean(jnp.square(x - mu), axis=-1, keepdims=True)
            return (x - mu) * jax.lax.rsqrt(var + LN_EPS) * g + b

        def _node_scores(h, W, att):
            t = jnp.tanh((h @ W).reshape(h.shape[0], HEADS, DIM))
            return jnp.einsum('mhd,hd->mh', t, att)

        def _segment_softmax(scores, seg, num_segments):
            m = jax.ops.segment_max(scores, seg, num_segments=num_segments)
            e = jnp.exp(scores - m[seg])
            z = jax.ops.segment_sum(e, seg, num_segments=num_segments)
            return e / z[seg]
        key = jax.random.key(seed)
        ks = jax.random.split(key, 13)
        s = 1.0 / np.sqrt(DIM)
        return {'entity_embed': jax.random.normal(ks[0], (N_ENT, DIM), jnp.float32) * 0.05, 'relation_embed': jax.random.normal(ks[1], (N_REL, DIM), jnp.float32) * 0.05, 'edge_index': jax.random.randint(ks[2], (2, N_EDGE), 0, N_ENT, jnp.int32), 'edge_type': jax.random.randint(ks[3], (N_EDGE,), 0, N_REL, jnp.int32), 'ln_gamma': jnp.ones((L_LAYERS, DIM), jnp.float32), 'ln_beta': jnp.zeros((L_LAYERS, DIM), jnp.float32), 'W_h': jax.random.normal(ks[4], (L_LAYERS, DIM, HEADS * DIM), jnp.float32) * s, 'W_t': jax.random.normal(ks[5], (L_LAYERS, DIM, HEADS * DIM), jnp.float32) * s, 'W_r': jax.random.normal(ks[6], (L_LAYERS, DIM, HEADS * DIM), jnp.float32) * s, 'att_h': jax.random.normal(ks[7], (L_LAYERS, HEADS, DIM), jnp.float32) * s, 'att_t': jax.random.normal(ks[8], (L_LAYERS, HEADS, DIM), jnp.float32) * s, 'att_r': jax.random.normal(ks[9], (L_LAYERS, HEADS, DIM), jnp.float32) * s, 'W_o': jax.random.normal(ks[10], (L_LAYERS, HEADS * DIM, DIM), jnp.float32) * s}
    _L1_gnn_all = _L1_gnn_setup()
    _L1_gnn_in = {k: v for k, v in _L1_gnn_all.items() if k in ('relation_embed', 'ln_gamma', 'ln_beta', 'W_h', 'W_t', 'W_r', 'att_h', 'att_t', 'att_r', 'W_o')}
    del _L1_gnn_all
    return {'x': x, 'src': src, 'dst': dst, 'edge_attr_64': edge_attr_64, 'edge_type_500': edge_type_500, 'L0_gnn_W1': _L0_gnn_in['W1'], 'L0_gnn_b1': _L0_gnn_in['b1'], 'L0_gnn_W2': _L0_gnn_in['W2'], 'L0_gnn_b2': _L0_gnn_in['b2'], 'L1_gnn_relation_embed': _L1_gnn_in['relation_embed'], 'L1_gnn_ln_gamma': _L1_gnn_in['ln_gamma'], 'L1_gnn_ln_beta': _L1_gnn_in['ln_beta'], 'L1_gnn_W_h': _L1_gnn_in['W_h'], 'L1_gnn_W_t': _L1_gnn_in['W_t'], 'L1_gnn_W_r': _L1_gnn_in['W_r'], 'L1_gnn_att_h': _L1_gnn_in['att_h'], 'L1_gnn_att_t': _L1_gnn_in['att_t'], 'L1_gnn_att_r': _L1_gnn_in['att_r'], 'L1_gnn_W_o': _L1_gnn_in['W_o']}

def reference(x, src, dst, edge_attr_64, edge_type_500, L0_gnn_W1, L0_gnn_b1, L0_gnn_W2, L0_gnn_b2, L1_gnn_relation_embed, L1_gnn_ln_gamma, L1_gnn_ln_beta, L1_gnn_W_h, L1_gnn_W_t, L1_gnn_W_r, L1_gnn_att_h, L1_gnn_att_t, L1_gnn_att_r, L1_gnn_W_o):
    import jax
    import jax.numpy as jnp

    def _L0_gnn_ref(h_e, h_r, W1, b1, W2, b2, edge_index):
        import jax, jax.numpy as jnp
        import numpy as np
        N = 3125
        E = 50000
        D = 64
        src = edge_index[0]
        dst = edge_index[1]
        n = h_e.shape[0]
        deg = jax.ops.segment_sum(jnp.ones((src.shape[0],), h_e.dtype), dst, num_segments=n)
        inv_deg = (1.0 / jnp.maximum(deg, 1.0))[:, None]
        nbr_r = jax.ops.segment_sum(h_r, dst, num_segments=n) * inv_deg

        def layer(h, W, b):
            nbr_x = jax.ops.segment_sum(h[src], dst, num_segments=n) * inv_deg
            z = jnp.concatenate([h, nbr_x, nbr_r], axis=1)
            return jax.nn.relu(z @ W + b)
        h = layer(h_e, W1, b1)
        h = layer(h, W2, b2)
        return h

    def _L1_gnn_ref(entity_embed, relation_embed, edge_index, edge_type, ln_gamma, ln_beta, W_h, W_t, W_r, att_h, att_t, att_r, W_o):
        import jax, jax.numpy as jnp
        import numpy as np
        N_ENT, N_REL, N_EDGE = (50000, 500, 15625)
        L_LAYERS, HEADS, DIM = (2, 2, 64)
        POW_ITER, ALPHA, LN_EPS = (3, 0.15, 1e-05)

        def _layernorm(x, g, b):
            mu = jnp.mean(x, axis=-1, keepdims=True)
            var = jnp.mean(jnp.square(x - mu), axis=-1, keepdims=True)
            return (x - mu) * jax.lax.rsqrt(var + LN_EPS) * g + b

        def _node_scores(h, W, att):
            t = jnp.tanh((h @ W).reshape(h.shape[0], HEADS, DIM))
            return jnp.einsum('mhd,hd->mh', t, att)

        def _segment_softmax(scores, seg, num_segments):
            m = jax.ops.segment_max(scores, seg, num_segments=num_segments)
            e = jnp.exp(scores - m[seg])
            z = jax.ops.segment_sum(e, seg, num_segments=num_segments)
            return e / z[seg]
        src, dst = (edge_index[0], edge_index[1])
        n = entity_embed.shape[0]
        ent = entity_embed
        for l in range(L_LAYERS):
            x = ent
            h = _layernorm(x, ln_gamma[l], ln_beta[l])
            s_h = _node_scores(h, W_h[l], att_h[l])
            s_t = _node_scores(h, W_t[l], att_t[l])
            s_r = _node_scores(relation_embed, W_r[l], att_r[l])
            scores = jax.nn.leaky_relu(s_h[src] + s_t[dst] + s_r[edge_type])
            w = _segment_softmax(scores, src, n)
            A = (1.0 - ALPHA) * w
            Z = jnp.broadcast_to(h[:, None, :], (n, HEADS, DIM))
            aZ0 = ALPHA * h[:, None, :]
            for _ in range(POW_ITER):
                msg = A[:, :, None] * Z[dst]
                Z = jax.ops.segment_sum(msg, src, num_segments=n) + aZ0
            conv = Z.reshape(n, HEADS * DIM) @ W_o[l]
            ent = conv + x
        return ent
    edge_index = jnp.stack([src, dst])
    x = _layernorm(x + _L0_gnn_ref(x, edge_attr_64, L0_gnn_W1, L0_gnn_b1, L0_gnn_W2, L0_gnn_b2, edge_index), axis=-1)
    x = _layernorm(x + _L1_gnn_ref(x, L1_gnn_relation_embed, edge_index, edge_type_500, L1_gnn_ln_gamma, L1_gnn_ln_beta, L1_gnn_W_h, L1_gnn_W_t, L1_gnn_W_r, L1_gnn_att_h, L1_gnn_att_t, L1_gnn_att_r, L1_gnn_W_o), axis=-1)
    return x

_drawn_inputs = setup_inputs


def setup_inputs(seed=0):
    import zlib

    import numpy as np

    out = dict(_drawn_inputs(seed))
    spreads = {'L0_gnn_b1': (0.0, 0.1),
     'L0_gnn_b2': (0.0, 0.1),
     'L1_gnn_ln_gamma': (1.0, 0.2),
     'L1_gnn_ln_beta': (0.0, 0.1)}
    factors = {'L1_gnn_relation_embed': 8.0,
     'L1_gnn_W_h': 8.0,
     'L1_gnn_W_r': 8.0,
     'L1_gnn_att_h': 8.0,
     'L1_gnn_att_r': 8.0}
    for name, (base, spread) in spreads.items():
        noise = np.random.default_rng([zlib.crc32(name.encode()), seed]).standard_normal(out[name].shape)
        drawn = base * np.exp(spread * noise) if base else spread * noise
        out[name] = jnp.asarray(drawn.astype(out[name].dtype))
    for name, factor in factors.items():
        out[name] = (out[name] * factor).astype(out[name].dtype)
    return out
```

```python
import concourse.bass as bass
from concourse import mybir
from contextlib import ExitStack

F32 = mybir.dt.float32
BF16 = mybir.dt.bfloat16
I32 = mybir.dt.int32
U32 = mybir.dt.uint32
ALU = mybir.AluOpType
ACT = mybir.ActivationFunctionType
AX = mybir.AxisListType

N = 3125
E = 100000
D = 64
H = 2
R = 500
L = 2
T = 128
NT = -(-N // T)
LAST = N - (NT - 1) * T
EP = 125
EC = E // EP
NBLK = NT * NT
GC = 8
NCH = -(-((E + NBLK * (T - 1)) // T) // (2 * GC)) * 2 * GC
NG = NCH // GC
NQ = NCH // 4
RW = 72
R_ONE, R_SRC, R_DST, R_REL = 64, 65, 66, 68
ALPHA = 0.15
POW_ITER = 3
LN_EPS = 1e-5
RP = 125
RT = R // RP


def wait_value(eng, sem, value):
    eng.wait_ge(sem, value)
    eng.nop(nofuse=True)


class Chain:

    def __init__(self, eng, sem):
        self.eng, self.sem, self.base, self.n = eng, sem, 0, 0

    def step(self, ins):
        self.n += 1
        ins.then_inc(self.sem, 1)
        self.eng.wait_ge(self.sem, self.base + self.n)


def layernorm_steps(nc, ln, x, y, tmp, st, sqrt_in, sqrt_out, dve, gamma=None, beta=None):
    nt = x.shape[1]
    bc = lambda a: a.unsqueeze(2).to_broadcast([T, nt, D])
    ln.step(nc.vector.tensor_reduce(st[:, 0, :], x, AX.X, ALU.add))
    ln.step(nc.vector.tensor_scalar(st[:, 1, :], st[:, 0, :], 1.0 / D, None, ALU.mult))
    ln.step(nc.vector.tensor_tensor(y, x, bc(st[:, 1, :]), ALU.subtract))
    ln.step(nc.vector.tensor_tensor(tmp, y, y, ALU.mult))
    ln.step(nc.vector.tensor_reduce(st[:, 2, :], tmp, AX.X, ALU.add))
    nc.vector.tensor_scalar(st[:, 3, :], st[:, 2, :], 1.0 / D, LN_EPS, ALU.mult, ALU.add).then_inc(sqrt_in, 1)
    dve.wait_ge(sqrt_out, 1)
    ln.step(nc.vector.reciprocal(st[:, 5, :], st[:, 4, :]))
    ln.step(nc.vector.tensor_tensor(y, y, bc(st[:, 5, :]), ALU.mult))
    if gamma is not None:
        row = lambda a: a.unsqueeze(1).to_broadcast([T, nt, D])
        ln.step(nc.vector.tensor_tensor(y, y, row(gamma), ALU.mult))
        ln.step(nc.vector.tensor_tensor(y, y, row(beta), ALU.add))


def split_steps(nc, ln, parts, src, rest):
    ln.step(nc.vector.tensor_copy(parts[:, :, 0, :], src))
    ln.step(nc.vector.tensor_tensor(rest, src, parts[:, :, 0, :], ALU.subtract))
    ln.step(nc.vector.tensor_copy(parts[:, :, 1, :], rest))
    ln.step(nc.vector.tensor_tensor(parts[:, :, 2, :], rest, parts[:, :, 1, :], ALU.subtract))


def gnn_program(nc, x_in, src_in, dst_in, attr_in, type_in, W1, b1, W2, b2, rel, ln_g, ln_b,
                W_h, W_t, W_r, att_h, att_t, att_r, W_o, out):
    top = ExitStack()

    taken_sems = {}

    def take_sem(stack, name):
        if id(stack) not in taken_sems:
            taken_sems[id(stack)] = []

            def give_back():
                nc.clear_and_free_semaphores(taken_sems.pop(id(stack)))
                nc.all_engine_barrier()
            stack.callback(give_back)
        taken_sems[id(stack)].append(nc.alloc_semaphore(name))
        return taken_sems[id(stack)][-1]

    def sb(name, shape, dt, stack=top):
        return stack.enter_context(nc.sbuf_tensor(name, shape, dt))

    records = nc.dram_tensor("records", (NCH * T, RW), F32).ap()
    onehots = nc.dram_tensor("onehots", (2, NG, T, GC * T), BF16).ap()
    rel_scores = nc.dram_tensor("rel_scores", (R, 2 * L), F32).ap()
    rec_groups = records.rearrange("(g p c) w -> g p (c w)", p=T, c=GC)

    with top:
        iota1 = sb("iota1", [T, T], F32)
        ident = sb("ident", [T, T], F32)
        identb = sb("identb", [T, T], BF16)
        below = sb("below", [T, T], F32)
        ones = sb("ones", [T, T], F32)
        x = sb("x", [T, NT, D], F32)
        src_lo = sb("src_lo", [T, NCH], F32)
        dst_lo = sb("dst_lo", [T, NCH], F32)
        s_rel = sb("s_rel", [T, NCH, 2 * L], F32)
        src_tile = sb("src_tile", [1, NCH], I32)
        dst_tile = sb("dst_tile", [1, NCH], I32)

        def score_phase(name, table, nt, rows, w_ap, att_ap, result):
            with ExitStack() as ctx:
                stage = sb(name + "_stage", [T, D], F32, ctx)
                tT = sb(name + "_tT", [D, T], F32, ctx)
                act = sb(name + "_act", [T, 4 * D], F32, ctx)
                prod = sb(name + "_prod", [T, 4, D], F32, ctx)
                psT = ctx.enter_context(nc.psum_tensor(name + "_psT", [D, T], F32))
                psW = ctx.enter_context(nc.psum_tensor(name + "_psW", [T, 4 * D], F32))
                sem = lambda n: take_sem(ctx, f"{name}_{n}")
                staged, turned, copied, multiplied, squashed = map(sem, ["staged", "turned", "copied", "multiplied", "squashed"])
                chain = sem("chain")
                block = ctx.enter_context(nc.Block())

                @block.vector
                def _(dve):
                    ln = Chain(dve, chain)
                    with dve.Fori(0, nt) as t:
                        nc.vector.tensor_scalar(stage[0:rows, :], table[0:rows, bass.ds(t, 1), :].rearrange("p a d -> p (a d)"),
                                                1.0, None, ALU.mult).then_inc(staged, 1)
                        dve.wait_ge(squashed, t + 1)
                        ln.base, ln.n = t * 2, 0
                        ln.step(nc.vector.tensor_tensor(prod[0:rows, :, :].rearrange("p k d -> p (k d)"), act[0:rows, :],
                                                        att_ap[0:rows, :], ALU.mult))
                        ln.step(nc.vector.tensor_reduce(result[0:rows, bass.ds(t, 1), :].rearrange("p a k -> p (a k)"),
                                                        prod[0:rows, :, :], AX.X, ALU.add))

                @block.tensor
                def _(pe):
                    with pe.Fori(0, nt) as t:
                        wait_value(pe, staged, t + 1)
                        nc.tensor.transpose(psT[:, 0:rows], stage[0:rows, :], ident[0:rows, 0:rows]).then_inc(turned, 1)
                        pe.wait_ge(copied, t + 1)
                        nc.tensor.matmul(psW[0:rows, :], tT[:, 0:rows], w_ap, start=True, stop=True).then_inc(multiplied, 1)

                @block.scalar
                def _(act_e):
                    with act_e.Fori(0, nt) as t:
                        act_e.wait_ge(turned, t + 1)
                        nc.scalar.activation(tT[:, 0:rows], psT[:, 0:rows], ACT.Copy).then_inc(copied, 1)
                        act_e.wait_ge(multiplied, t + 1)
                        nc.scalar.activation(act[0:rows, :], psW[0:rows, :], ACT.Tanh).then_inc(squashed, 1)

        with ExitStack() as ctx:
            zeros = sb("zeros", [T, GC * RW], F32, ctx)
            sem = lambda n: take_sem(ctx, n)
            s_zero, s_clear, s_load, s_set, s_xz = map(sem, ["zero_ready", "cleared", "x_loaded", "const_set", "x_zeroed"])
            block = ctx.enter_context(nc.Block())

            @block.vector
            def _(dve):
                nc.vector.memset(zeros[:, :], 0.0).then_inc(s_zero, 1)
                nc.vector.memset(x[:, NT - 1, :], 0.0).then_inc(s_xz, 1)

            @block.sync
            def _(sp):
                sp.wait_ge(s_xz, 1)
                sp.dma_start(x[:, 0:NT - 1, :], x_in[0:(NT - 1) * T, :].rearrange("(t p) d -> p t d", p=T)).then_inc(s_load, 16)
                sp.dma_start(x[0:LAST, NT - 1, :], x_in[(NT - 1) * T:N, :]).then_inc(s_load, 16)
                sp.wait_ge(s_zero, 1)
                with sp.Fori(0, NG) as g:
                    sp.dma_start(rec_groups[bass.ds(g, 1), :, :].rearrange("a p w -> (a p) w"), zeros[:, :]).then_inc(s_clear, 16)
                sp.wait_ge(s_load, 32)
                sp.wait_ge(s_clear, NG * 16)

            @block.gpsimd
            def _(pool):
                nc.gpsimd.iota(iota1[:, :], [[1, T]], base=1, channel_multiplier=0, allow_small_or_imprecise_dtypes=True)
                nc.gpsimd.memset(ident[:, :], 0.0).then_inc(s_set, 1)
                nc.gpsimd.memset(identb[:, :], 0.0).then_inc(s_set, 1)
                nc.gpsimd.memset(ones[:, :], 1.0).then_inc(s_set, 1)
                pool.wait_ge(s_set, 3)
                for m in (ident, identb):
                    nc.gpsimd.affine_select(out=m[:, :], in_=m[:, :], compare_op=ALU.not_equal, fill=1.0,
                                            base=0, pattern=[[-1, T]], channel_multiplier=1)
                nc.gpsimd.affine_select(out=below[:, :], in_=ones[:, :], compare_op=ALU.is_gt, fill=0.0,
                                        base=0, pattern=[[1, T]], channel_multiplier=-1)

        with ExitStack() as ctx:
            rel_sb = sb("rel_sb", [T, RT, D], F32, ctx)
            wr = sb("wr", [D, 4 * D], F32, ctx)
            ar = sb("ar", [T, 4 * D], F32, ctx)
            rs = sb("rs", [T, RT, 4], F32, ctx)
            with ExitStack() as c2:
                s_load = take_sem(c2, "rel_loaded")
                block = c2.enter_context(nc.Block())

                @block.sync
                def _(sp):
                    sp.dma_start(rel_sb[0:RP, :, :], rel.rearrange("(t p) d -> p t d", p=RP)).then_inc(s_load, 16)
                    sp.dma_start(wr[:, :].rearrange("p (l n) -> p l n", l=L), W_r.rearrange("l p n -> p l n")).then_inc(s_load, 16)
                    sp.dma_start(ar[:, :], att_r.rearrange("l h d -> (l h d)").partition_broadcast(T)).then_inc(s_load, 16)
                    sp.wait_ge(s_load, 48)
            score_phase("rel", rel_sb, RT, RP, wr[:, :], ar, rs)
            with ExitStack() as c2:
                s_store = take_sem(c2, "rel_stored")
                block = c2.enter_context(nc.Block())

                @block.sync
                def _(sp):
                    sp.dma_start(rel_scores.rearrange("(t p) k -> p t k", p=RP), rs[0:RP, :, :]).then_inc(s_store, 16)
                    sp.wait_ge(s_store, 16)

        with ExitStack() as slot_ctx:
            row_idx = sb("row_idx", [EP, EC], I32, slot_ctx)
            slo = sb("slo", [EP, EC], F32, slot_ctx)
            dlo = sb("dlo", [EP, EC], F32, slot_ctx)
            typ = sb("typ", [EP, EC], I32, slot_ctx)
            with ExitStack() as ctx:
                s_hi = sb("s_hi", [EP, EC], F32, ctx)
                d_hi = sb("d_hi", [EP, EC], F32, ctx)
                iota_t = sb("iota_t", [EP, NT], F32, ctx)
                counts = sb("counts", [NT, EC + 1, NT], F32, ctx)
                rank = sb("rank", [EP, EC], F32, ctx)

                with ExitStack() as c2:
                    src_i = sb("src_i", [EP, EC], I32, c2)
                    dst_i = sb("dst_i", [EP, EC], I32, c2)
                    hi_i = sb("hi_i", [EP, 4, EC], I32, c2)
                    s_load = take_sem(c2, "edges_loaded")
                    chain = take_sem(c2, "cut_chain")
                    block = c2.enter_context(nc.Block())

                    @block.sync
                    def _(sp):
                        for to, frm in ((src_i, src_in), (dst_i, dst_in), (typ, type_in)):
                            sp.dma_start(to[:, :], frm.rearrange("(p c) -> p c", p=EP)).then_inc(s_load, 16)
                        sp.wait_ge(s_load, 48)

                    @block.gpsimd
                    def _(pool):
                        nc.gpsimd.iota(iota_t[:, :], [[1, NT]], base=0, channel_multiplier=0, allow_small_or_imprecise_dtypes=True)

                    @block.vector
                    def _(dve):
                        dve.wait_ge(s_load, 48)
                        nc.vector.memset(counts[:, 0, :], 0.0)
                        for i, (a, hi, lo) in enumerate(((src_i, s_hi, slo), (dst_i, d_hi, dlo))):
                            nc.vector.tensor_scalar(hi_i[:, 2 * i, :], a[:, :], 7, None, ALU.logical_shift_right).then_inc(chain, 1)
                            nc.vector.tensor_scalar(hi_i[:, 2 * i + 1, :], a[:, :], T - 1, None, ALU.bitwise_and).then_inc(chain, 1)
                            dve.wait_ge(chain, 2 * i + 2)
                            nc.vector.tensor_copy(hi[:, :], hi_i[:, 2 * i, :])
                            nc.vector.tensor_scalar(lo[:, :], hi_i[:, 2 * i + 1, :], 1.0, None, ALU.add)

                BC = 20
                with ExitStack() as c2:
                    oa = sb("oa", [EP, 2, BC, NT], BF16, c2)
                    ob = sb("ob", [EP, 2, BC, NT], BF16, c2)
                    psH = c2.enter_context(nc.psum_tensor("psH", [NT, 2, 512], F32))
                    sem = lambda n: take_sem(c2, n)
                    marked, counted, kept = map(sem, ["cols_marked", "cols_counted", "counts_kept"])
                    block = c2.enter_context(nc.Block())

                    def mark(n, c0):
                        for o, hi in ((oa, s_hi), (ob, d_hi)):
                            last = nc.vector.tensor_tensor(
                                o[:, n, :, :], hi[:, bass.ds(c0, BC)].unsqueeze(2).to_broadcast([EP, BC, NT]),
                                iota_t[:, :].unsqueeze(1).to_broadcast([EP, BC, NT]), ALU.is_equal)
                        last.then_inc(marked, 1)

                    ROUNDS = EC // BC // 2

                    @block.vector
                    def _(dve):
                        mark(0, 0)
                        mark(1, BC)
                        with dve.Fori(1, ROUNDS) as t:
                            for n in range(2):
                                dve.wait_ge(counted, t * 2 + (n - 1))
                                mark(n, t * (2 * BC) + n * BC)

                    @block.tensor
                    def _(pe):
                        def count(n):
                            for j in range(BC):
                                last = nc.tensor.matmul(psH[:, n, j * NT:(j + 1) * NT], oa[:, n, j, :], ob[:, n, j, :],
                                                        start=True, stop=True, skip_group_check=True)
                            last.then_inc(counted, 1)
                        for n in range(2):
                            pe.wait_ge(marked, n + 1)
                            count(n)
                        with pe.Fori(1, ROUNDS) as t:
                            for n in range(2):
                                pe.wait_ge(marked, t * 2 + (n + 1))
                                pe.wait_ge(kept, t * 2 + (n - 1))
                                count(n)

                    @block.scalar
                    def _(act):
                        with act.Fori(0, ROUNDS) as t:
                            for n in range(2):
                                wait_value(act, counted, t * 2 + (n + 1))
                                nc.scalar.activation(counts[:, bass.ds(t * (2 * BC) + (n * BC + 1), BC), :].rearrange("p c b -> p (c b)"),
                                                     psH[:, n, 0:BC * NT], ACT.Copy).then_inc(kept, 1)

                with ExitStack() as c2:
                    small = sb("small", [NT, 6, NT], F32, c2)
                    small_i = sb("small_i", [NT, 2, NT], I32, c2)
                    row_base = sb("row_base", [NT, 1], F32, c2)
                    iota_c = sb("iota_c", [NT, NCH], F32, c2)
                    passed = sb("passed", [NT, NCH], F32, c2)
                    rows_passed = sb("rows_passed", [NT, NCH], F32, c2)
                    kf = sb("kf", [1, 2, NCH], F32, c2)
                    psB = c2.enter_context(nc.psum_tensor("psB", [NT, 512], F32))
                    psK = c2.enter_context(nc.psum_tensor("psK", [1, 3, 512], F32))
                    psR = c2.enter_context(nc.psum_tensor("psR", [1, 3, 512], F32))
                    sem = lambda n: take_sem(c2, n)
                    chain, totals, based, compared, summed, s_iota = map(sem, ["slot_chain", "row_totals", "row_bases", "ends_passed", "chunk_keys", "iota_set"])
                    block = c2.enter_context(nc.Block())
                    spans = [(i * 512, min(512, NCH - i * 512)) for i in range(-(-NCH // 512))]

                    @block.gpsimd
                    def _(pool):
                        nc.gpsimd.iota(iota_c[:, :], [[1, NCH]], base=0, channel_multiplier=0,
                                       allow_small_or_imprecise_dtypes=True).then_inc(s_iota, 1)

                    @block.tensor
                    def _(pe):
                        pe.wait_ge(totals, 1)
                        nc.tensor.matmul(psB[:, 0:1], below[0:NT, 0:NT], small[:, 2, NT - 1:NT], start=True, stop=True).then_inc(based, 1)
                        pe.wait_ge(compared, 1)
                        for i, (o, w) in enumerate(spans):
                            nc.tensor.matmul(psK[:, i, 0:w], ones[0:NT, 0:1], passed[:, o:o + w], start=True, stop=True)
                            last = nc.tensor.matmul(psR[:, i, 0:w], ones[0:NT, 0:1], rows_passed[:, o:o + w], start=True, stop=True)
                        last.then_inc(summed, 1)

                    @block.vector
                    def _(dve):
                        ln = Chain(dve, chain)
                        for b in range(NT):
                            c = counts[:, 1:EC + 1, b]
                            last = nc.vector.tensor_tensor_scan(c, c, c, 0.0, ALU.add, ALU.max)
                        ln.step(last)
                        ln.step(nc.vector.tensor_scalar(small_i[:, 0, :], counts[:, EC, :], float(T - 1), None, ALU.add))
                        ln.step(nc.vector.tensor_scalar(small_i[:, 1, :], small_i[:, 0, :], 7, None, ALU.logical_shift_right))
                        ln.step(nc.vector.tensor_copy(small[:, 1, :], small_i[:, 1, :]))
                        nc.vector.tensor_tensor_scan(small[:, 2, :], small[:, 1, :], small[:, 1, :], 0.0, ALU.add, ALU.max).then_inc(totals, 1)
                        dve.wait_ge(based, 1)
                        ln.step(nc.vector.tensor_copy(row_base[:, :], psB[:, 0:1]))
                        ln.step(nc.vector.tensor_scalar(small[:, 3, :], small[:, 2, :], row_base[:, :], None, ALU.add))
                        ln.step(nc.vector.tensor_tensor(small[:, 4, :], small[:, 3, :], small[:, 1, :], ALU.subtract))
                        ln.step(nc.vector.tensor_scalar(small[:, 5, :], small[:, 4, :], float(T), None, ALU.mult))
                        ln.step(nc.vector.tensor_tensor(counts[:, 0:EC, :], counts[:, 0:EC, :],
                                                        small[:, 5, :].unsqueeze(1).to_broadcast([NT, EC, NT]), ALU.add))
                        dve.wait_ge(s_iota, 1)
                        ln.step(nc.vector.tensor_scalar(passed[:, :], iota_c[:, :], small[:, 3, 0:1], None, ALU.is_ge))
                        for b in range(1, NT):
                            ln.step(nc.vector.scalar_tensor_tensor(out=passed[:, :], in0=iota_c[:, :], scalar=small[:, 3, b:b + 1],
                                                                   in1=passed[:, :], op0=ALU.is_ge, op1=ALU.add))
                        nc.vector.tensor_scalar(rows_passed[:, :], iota_c[:, :], small[:, 3, NT - 1:NT], None, ALU.is_ge).then_inc(compared, 1)
                        dve.wait_ge(summed, 1)
                        for i, (o, w) in enumerate(spans):
                            nc.vector.tensor_copy(kf[:, 0, o:o + w], psK[:, i, 0:w])
                            last = nc.vector.tensor_copy(kf[:, 1, o:o + w], psR[:, i, 0:w])
                        ln.step(last)
                        nc.vector.scalar_tensor_tensor(out=dst_tile[:, :], in0=kf[:, 1, :], scalar=-float(NT), in1=kf[:, 0, :],
                                                       op0=ALU.mult, op1=ALU.add)
                        nc.vector.tensor_scalar(src_tile[:, :], kf[:, 1, :], float(NT - 1), None, ALU.min)

                BR = 16
                with ExitStack() as c2:
                    oa = sb("oa2", [EP, BR, NT], BF16, c2)
                    ob = sb("ob2", [EP, BR, NT], BF16, c2)
                    oaT = sb("oaT", [NT, BR, 128], BF16, c2)
                    oaTf = sb("oaTf", [NT, BR, 128], F32, c2)
                    before = sb("before", [EP, BR, EP], BF16, c2)
                    pick = sb("pick", [EP, BR, NT], F32, c2)
                    psT = c2.enter_context(nc.psum_tensor("psT", [NT, BR, 128], BF16))
                    psS = c2.enter_context(nc.psum_tensor("psS", [EP, BR, 128], F32))
                    psR = c2.enter_context(nc.psum_tensor("psRk", [EP, 512], F32))
                    sem = lambda n: take_sem(c2, n)
                    marked, turned, copied, alike, masked, ranked, chain = map(
                        sem, ["marked", "turned", "copied", "alike", "masked", "ranked", "rank_chain"])
                    block = c2.enter_context(nc.Block())

                    @block.vector
                    def _(dve):
                        ln = Chain(dve, chain)
                        with dve.Fori(0, EC // BR) as t:
                            ln.base, ln.n = t * 2, 0
                            for o, hi in ((oa, s_hi), (ob, d_hi)):
                                last = nc.vector.tensor_tensor(
                                    o[:, :, :], hi[:, bass.ds(t * BR, BR)].unsqueeze(2).to_broadcast([EP, BR, NT]),
                                    iota_t[:, :].unsqueeze(1).to_broadcast([EP, BR, NT]), ALU.is_equal)
                            last.then_inc(marked, 1)
                            dve.wait_ge(alike, t + 1)
                            for q in range(BR // 4):
                                last = nc.vector.tensor_tensor(before[:, 4 * q:4 * q + 4, :], psS[:, 4 * q:4 * q + 4, 0:EP],
                                                               below[0:EP, 0:EP].unsqueeze(1).to_broadcast([EP, 4, EP]), ALU.mult)
                            last.then_inc(masked, 1)
                            dve.wait_ge(ranked, t + 1)
                            ln.step(nc.vector.tensor_tensor(pick[:, :, :].rearrange("p c b -> p (c b)"), psR[:, 0:BR * NT],
                                                            ob[:, :, :].rearrange("p c b -> p (c b)"), ALU.mult))
                            ln.step(nc.vector.tensor_reduce(rank[:, bass.ds(t * BR, BR)], pick[:, :, :], AX.X, ALU.add))

                    @block.tensor
                    def _(pe):
                        with pe.Fori(0, EC // BR) as t:
                            wait_value(pe, marked, t + 1)
                            for j in range(BR):
                                last = nc.tensor.transpose(psT[:, j, 0:EP], oa[:, j, :], identb[0:EP, 0:EP])
                            last.then_inc(turned, 1)
                            pe.wait_ge(copied, t * 2 + 2)
                            for j in range(BR):
                                last = nc.tensor.matmul(psS[:, j, 0:EP], oaT[:, j, 0:EP], oaT[:, j, 0:EP], start=True, stop=True,
                                                        skip_group_check=True)
                            last.then_inc(alike, 1)
                            pe.wait_ge(masked, t + 1)
                            for j in range(BR):
                                o = psR[:, j * NT:(j + 1) * NT]
                                nc.tensor.matmul(o, oaTf[:, j, 0:EP], counts[:, bass.ds(t * BR + j, 1), :].rearrange("p a b -> p (a b)"),
                                                 start=True, stop=False, skip_group_check=True)
                                last = nc.tensor.matmul(o, before[:, j, :], ob[:, j, :], start=False, stop=True, skip_group_check=True)
                            last.then_inc(ranked, 1)

                    @block.scalar
                    def _(act):
                        with act.Fori(0, EC // BR) as t:
                            act.wait_ge(turned, t + 1)
                            nc.scalar.activation(oaT[:, :, 0:EP], psT[:, :, 0:EP], ACT.Copy).then_inc(copied, 1)
                            nc.scalar.activation(oaTf[:, :, 0:EP], psT[:, :, 0:EP], ACT.Copy).then_inc(copied, 1)

                with ExitStack() as c2:
                    ri = sb("ri", [EP, 4, EC], I32, c2)
                    chain = take_sem(c2, "row_chain")
                    block = c2.enter_context(nc.Block())

                    @block.vector
                    def _(dve):
                        ln = Chain(dve, chain)
                        ln.step(nc.vector.tensor_copy(ri[:, 0, :], rank[:, :]))
                        nc.vector.tensor_scalar(ri[:, 1, :], ri[:, 0, :], -GC * T, None, ALU.bitwise_and)
                        nc.vector.tensor_scalar(ri[:, 2, :], ri[:, 0, :], T - 1, 3, ALU.bitwise_and, ALU.logical_shift_left)
                        ln.step(nc.vector.tensor_scalar(ri[:, 3, :], ri[:, 0, :], 7, GC - 1, ALU.logical_shift_right, ALU.bitwise_and))
                        ln.step(nc.vector.tensor_tensor(row_idx[:, :], ri[:, 1, :], ri[:, 2, :], ALU.bitwise_or))
                        ln.step(nc.vector.tensor_tensor(row_idx[:, :], row_idx[:, :], ri[:, 3, :], ALU.bitwise_or))

            with ExitStack() as ctx:
                HC = 8
                stage = sb("stage", [EP, 2, HC, RW], F32, ctx)
                row_st = sb("row_st", [EP, 2, HC], I32, ctx)
                typ_st = sb("typ_st", [EP, 2, HC], I32, ctx)
                sem = lambda n: take_sem(ctx, n)
                attr_in_stage = [sem(f"attr_in_stage{i}") for i in range(2)]
                fields_set, s_one = sem("fields_set"), sem("ones_set")
                gathered = [sem(f"rel_gathered{i}") for i in range(2)]
                scattered = [sem(f"records_scattered{i}") for i in range(2)]
                block = ctx.enter_context(nc.Block())
                attr_cols = attr_in.rearrange("(p c) d -> p c d", p=EP)
                ROUNDS = EC // (2 * HC)

                @block.sync
                def _(sp):
                    def load(n, c0):
                        sp.dma_start(stage[:, n, :, 0:D], attr_cols[:, bass.ds(c0, HC), :]).then_inc(attr_in_stage[n], 16)
                    load(0, 0)
                    load(1, HC)
                    with sp.Fori(1, ROUNDS) as t:
                        for n in range(2):
                            wait_value(sp, scattered[n], t * (16 * HC))
                            load(n, t * (2 * HC) + n * HC)

                @block.vector
                def _(dve):
                    nc.vector.memset(stage[:, :, :, D:RW], 0.0).then_inc(s_one, 1)
                    dve.wait_ge(s_one, 1)
                    nc.vector.memset(stage[:, :, :, R_ONE:R_ONE + 1], 1.0).then_inc(s_one, 1)

                    def fields(n, c0):
                        cols = bass.ds(c0, HC)
                        nc.vector.tensor_copy(stage[:, n, :, R_SRC], slo[:, cols])
                        nc.vector.tensor_copy(stage[:, n, :, R_DST], dlo[:, cols])
                        nc.vector.tensor_copy(row_st[:, n, :], row_idx[:, cols])
                        nc.vector.tensor_copy(typ_st[:, n, :], typ[:, cols]).then_inc(fields_set, 1)
                    dve.wait_ge(s_one, 2)
                    fields(0, 0)
                    fields(1, HC)
                    with dve.Fori(1, ROUNDS) as t:
                        for n in range(2):
                            wait_value(dve, scattered[n], t * (16 * HC))
                            fields(n, t * (2 * HC) + n * HC)

                @block.gpsimd
                def _(pool):
                    def gather(n):
                        for j in range(HC):
                            pool.indirect_dma_start(
                                out=stage[:, n, j, R_REL:R_REL + 2 * L], out_offset=None, in_=rel_scores,
                                in_offset=bass.IndirectOffsetOnAxis(ap=typ_st[:, n, j:j + 1].bitcast(U32), axis=0)).then_inc(gathered[n], 16)

                    def scatter(n):
                        for j in range(HC):
                            pool.indirect_dma_start(
                                out=records, out_offset=bass.IndirectOffsetOnAxis(ap=row_st[:, n, j:j + 1].bitcast(U32), axis=0),
                                in_=stage[:, n, j, :], in_offset=None).then_inc(scattered[n], 16)

                    pool.wait_ge(fields_set, 1)
                    gather(0)
                    pool.wait_ge(fields_set, 2)
                    gather(1)
                    with pool.Fori(0, ROUNDS - 1) as t:
                        for n in range(2):
                            wait_value(pool, gathered[n], (t + 1) * (16 * HC))
                            wait_value(pool, attr_in_stage[n], (t + 1) * 16)
                            scatter(n)
                        for n in range(2):
                            wait_value(pool, fields_set, t * 2 + (n + 3))
                            gather(n)
                    for n in range(2):
                        pool.wait_ge(gathered[n], ROUNDS * 16 * HC)
                        pool.wait_ge(attr_in_stage[n], ROUNDS * 16)
                        scatter(n)
                    for n in range(2):
                        pool.wait_ge(scattered[n], ROUNDS * 16 * HC)

        with ExitStack() as ctx:
            rec = sb("rec", [T, 2, GC, RW], F32, ctx)
            mark = sb("mark", [T, 2, 2, GC, T], BF16, ctx)
            turn = sb("turn", [T, 2, 2, GC * T], BF16, ctx)
            psT = ctx.enter_context(nc.psum_tensor("psTurn", [T, 2, 2, GC * T], BF16))
            sem = lambda n: take_sem(ctx, n)
            loaded = [sem(f"rec_loaded{i}") for i in range(2)]
            stored = [sem(f"turned_stored{i}") for i in range(2)]
            kept, marked, turned, copied = map(sem, ["places_kept", "slots_marked", "marks_turned", "turned_copied"])
            block = ctx.enter_context(nc.Block())

            def rounds(eng, body):
                body(0, True)
                with eng.Fori(1, NG // 2) as t:
                    body(t, False)

            @block.sync
            def _(sp):
                def body(t, first):
                    for n in range(2):
                        if not first:
                            wait_value(sp, kept, t * 2 + (n - 1))
                        sp.dma_start(rec[:, n, :, :].rearrange("p c w -> p (c w)"),
                                     rec_groups[bass.ds(t * 2 + n, 1), :, :].rearrange("a p w -> (a p) w")).then_inc(loaded[n], 16)
                rounds(sp, body)

            @block.vector
            def _(dve):
                def body(t, first):
                    for n in range(2):
                        cols = bass.ds((t * 2 + n) * GC, GC)
                        wait_value(dve, loaded[n], t * 16 + 16)
                        nc.vector.tensor_copy(src_lo[:, cols], rec[:, n, :, R_SRC])
                        nc.vector.tensor_copy(dst_lo[:, cols], rec[:, n, :, R_DST])
                        if not first:
                            wait_value(dve, turned, t * 2 + (n - 1))
                        for k, r in enumerate((R_SRC, R_DST)):
                            nc.vector.tensor_tensor(mark[:, n, k, :, :], iota1[:, :].unsqueeze(1).to_broadcast([T, GC, T]),
                                                    rec[:, n, :, r:r + 1].to_broadcast([T, GC, T]), ALU.is_equal).then_inc(marked, 1)
                        nc.vector.tensor_copy(s_rel[:, cols, :], rec[:, n, :, R_REL:R_REL + 2 * L]).then_inc(kept, 1)
                rounds(dve, body)

            @block.tensor
            def _(pe):
                def body(t, first):
                    for n in range(2):
                        wait_value(pe, marked, t * 4 + (2 * n + 2))
                        if not first:
                            wait_value(pe, copied, t * 4 + (2 * n - 2))
                        for k in range(2):
                            for j in range(GC):
                                last = nc.tensor.transpose(psT[:, n, k, j * T:(j + 1) * T], mark[:, n, k, j, :], identb[:, :])
                        last.then_inc(turned, 1)
                rounds(pe, body)

            @block.scalar
            def _(act):
                def body(t, first):
                    for n in range(2):
                        wait_value(act, turned, t * 2 + (n + 1))
                        if not first:
                            wait_value(act, stored[n], t * 32)
                        for k in range(2):
                            nc.scalar.activation(turn[:, n, k, :], psT[:, n, k, :], ACT.Copy).then_inc(copied, 1)
                        wait_value(act, copied, t * 4 + (2 * n + 2))
                        for k in range(2):
                            act.dma_start(onehots[k, bass.ds(t * 2 + n, 1), :, :].rearrange("a p w -> (a p) w"),
                                          turn[:, n, k, :]).then_inc(stored[n], 16)
                rounds(act, body)
                for n in range(2):
                    act.wait_ge(stored[n], NG * 16)

        ROUNDS = NCH // (2 * GC)

        def peeled(eng, body):
            body(0, True, False)
            with eng.Fori(1, ROUNDS - 1) as t:
                body(t, False, False)
            body(ROUNDS - 1, False, True)

        def tile_of(eng, tiles, c):
            return eng.value_load(tiles[0:1, bass.ds(c, 1)], min_val=0, max_val=NT - 1)

        def spread_pass(name, turned, g_tiles, F, table, lo, s_tiles, weights, extra, acc):
            GW = F if weights is None else 2 * D
            XW = {None: 0, "record": D + 1, "weight": 2}[extra]
            AW = 128 if GW + XW <= 128 else 256
            with ExitStack() as ctx:
                ot = sb(name + "_ot", [T, 2, GC, T], BF16, ctx)
                gw = sb(name + "_gw", [T, 2, 4, GW], F32, ctx)
                oh = sb(name + "_oh", [T, 2, 4, T], F32, ctx)
                places = sb(name + "_places", [T, 2, 4], F32, ctx)
                placed4 = take_sem(ctx, name + "_places_set")
                rec = sb(name + "_rec", [T, 2, GC, RW], F32, ctx) if extra == "record" else None
                gps = ctx.enter_context(nc.psum_tensor(name + "_gps", [T, 2, 4, 128], F32))
                aps = ctx.enter_context(nc.psum_tensor(name + "_aps", [T, 2, 4, AW], F32))
                sem = lambda n: take_sem(ctx, f"{name}_{n}")
                ot_loaded = [sem(f"ot_loaded{i}") for i in range(2)]
                rec_loaded = [sem(f"rec_loaded{i}") for i in range(2)]
                gathered, weighted, marked, summed, added, cleared = map(
                    sem, ["gathered", "weighted", "marked", "summed", "added", "cleared"])
                block = ctx.enter_context(nc.Block())

                @block.sync
                def _(sp):
                    def body(t, first, last):
                        for n in range(2):
                            g = bass.ds(t * 2 + n, 1)
                            if not first:
                                sp.wait_ge(gathered, t * 4 + (2 * n - 2))
                            sp.dma_start(ot[:, n, :, :].rearrange("p c e -> p (c e)"),
                                         onehots[turned, g, :, :].rearrange("a p w -> (a p) w")).then_inc(ot_loaded[n], 16)
                            if rec is not None:
                                if not first:
                                    sp.wait_ge(summed, t * 4 + (2 * n - 2))
                                sp.dma_start(rec[:, n, :, :].rearrange("p c w -> p (c w)"),
                                             rec_groups[g, :, :].rearrange("a p w -> (a p) w")).then_inc(rec_loaded[n], 16)
                    peeled(sp, body)

                @block.gpsimd
                def _(pool):
                    def marking(t, first, last):
                        for k in range(4):
                            if not (first and k < 2):
                                wait_value(pool, summed, t * 4 + (k - 1))
                            nc.gpsimd.tensor_copy(places[:, k % 2, :], lo[:, bass.ds(t * 16 + 4 * k, 4)]).then_inc(placed4, 1)
                            wait_value(pool, placed4, t * 4 + (k + 1))
                            for j in range(4):
                                last_ = nc.gpsimd.tensor_scalar(oh[:, k % 2, j, :], iota1[:, :], places[:, k % 2, j:j + 1], None,
                                                                ALU.is_equal)
                            last_.then_inc(marked, 1)
                    peeled(pool, marking)

                @block.tensor
                def _(pe):
                    def gather(t, k, first):
                        n, j0 = k // 2, 4 * (k % 2)
                        if k % 2 == 0:
                            pe.wait_ge(ot_loaded[n], t * 16 + 16)
                        if not (first and k < 2):
                            pe.wait_ge(weighted, t * 4 + (k - 1))
                        for j in range(4):
                            tile = tile_of(pe, g_tiles, t * 16 + (4 * k + j))
                            for part in range(3):
                                last = nc.tensor.matmul(gps[:, k % 2, j, 0:F], ot[:, n, j0 + j, :],
                                                        table[:, bass.ds(tile, 1), part, :].rearrange("p a d -> p (a d)"),
                                                        start=(part == 0), stop=(part == 2), skip_group_check=True)
                        last.then_inc(gathered, 1)

                    def add_up(t, k, first):
                        n, j0 = k // 2, 4 * (k % 2)
                        pe.wait_ge(weighted, t * 4 + (k + 1))
                        pe.wait_ge(marked, t * 4 + (k + 1))
                        if rec is not None and k % 2 == 0:
                            pe.wait_ge(rec_loaded[n], t * 16 + 16)
                        if not (first and k < 2):
                            pe.wait_ge(added, t * 16 + 4 * (k - 1))
                        for j in range(4):
                            w = oh[:, k % 2, j, :]
                            last = nc.tensor.matmul(aps[:, k % 2, j, 0:GW], w, gw[:, k % 2, j, :], start=True, stop=True,
                                                    skip_group_check=True)
                            if extra == "record":
                                last = nc.tensor.matmul(aps[:, k % 2, j, GW:GW + XW], w, rec[:, n, j0 + j, 0:XW],
                                                        start=True, stop=True, skip_group_check=True)
                            if extra == "weight":
                                last = nc.tensor.matmul(aps[:, k % 2, j, GW:GW + XW], w,
                                                        weights[:, bass.ds(t * 16 + (4 * k + j), 1), :].rearrange("p a h -> p (a h)"),
                                                        start=True, stop=True, skip_group_check=True)
                        last.then_inc(summed, 1)

                    def body(t, first, last):
                        for k in range(4):
                            if k < 3:
                                gather(t, k + 1, first)
                            elif not last:
                                gather(t + 1, 0, False)
                            add_up(t, k, first)
                    gather(0, 0, True)
                    peeled(pe, body)

                @block.vector
                def _(dve):
                    nc.vector.memset(acc[:, :, :], 0.0).then_inc(cleared, 1)
                    dve.wait_ge(cleared, 1)

                    def weigh(t, k, first):
                        dve.wait_ge(gathered, t * 4 + (k + 1))
                        if not (first and k < 2):
                            dve.wait_ge(summed, t * 4 + (k - 1))
                        g = gps[:, k % 2, :, 0:F]
                        if weights is None:
                            nc.vector.tensor_scalar(gw[:, k % 2, :, :], g, 1.0, None, ALU.mult).then_inc(weighted, 1)
                        elif F == D:
                            w = weights[:, bass.ds(t * 16 + 4 * k, 4), :]
                            for h in range(H):
                                last = nc.vector.tensor_tensor(gw[:, k % 2, :, h * D:(h + 1) * D], g,
                                                               w[:, :, h:h + 1].to_broadcast([T, 4, D]), ALU.mult)
                            last.then_inc(weighted, 1)
                        else:
                            w = weights[:, bass.ds(t * 16 + 4 * k, 4), :].rearrange("p c h -> p (c h)")
                            nc.vector.tensor_tensor(gw[:, k % 2, :, :].rearrange("p c (h d) -> p (c h) d", h=H),
                                                    gps[:, k % 2, :, :].rearrange("p c (h d) -> p (c h) d", h=H),
                                                    w.unsqueeze(2).to_broadcast([T, 4 * H, D]), ALU.mult).then_inc(weighted, 1)

                    def add(t, k, first):
                        dve.wait_ge(summed, t * 4 + (k + 1))
                        for j in range(4):
                            tile = tile_of(dve, s_tiles, t * 16 + (4 * k + j))
                            a = acc[:, bass.ds(tile, 1), :].rearrange("p a w -> p (a w)")
                            if not (first and k == j == 0):
                                dve.wait_ge(added, t * 16 + (4 * k + j))
                            nc.vector.tensor_tensor(a, a, aps[:, k % 2, j, 0:GW + XW], ALU.add).then_inc(added, 1)

                    def body(t, first, last):
                        for k in range(4):
                            if k < 3:
                                weigh(t, k + 1, first)
                            elif not last:
                                weigh(t + 1, 0, False)
                            add(t, k, first)
                    weigh(0, 0, True)
                    peeled(dve, body)

        def pick_pass(name, sides, finish):
            NS = len(sides)
            with ExitStack() as ctx:
                ot = sb(name + "_ot", [T, 2, NS, GC, T], BF16, ctx)
                val = sb(name + "_val", [T, 2, GC, H], F32, ctx)
                ps = ctx.enter_context(nc.psum_tensor(name + "_ps", [T, 2, 512], F32))
                sem = lambda n: take_sem(ctx, f"{name}_{n}")
                loaded = [sem(f"loaded{i}") for i in range(2)]
                picked, taken, chain, ready = map(sem, ["picked", "taken", "chain", "ready"])
                block = ctx.enter_context(nc.Block())

                def groups(eng, body):
                    body(0, True)
                    with eng.Fori(1, ROUNDS) as t:
                        body(t, False)

                @block.sync
                def _(sp):
                    def body(t, first):
                        for n in range(2):
                            if not first:
                                sp.wait_ge(picked, t * 2 + (n - 1))
                            for i, (turned, _, _) in enumerate(sides):
                                sp.dma_start(ot[:, n, i, :, :].rearrange("p c e -> p (c e)"),
                                             onehots[turned, bass.ds(t * 2 + n, 1), :, :].rearrange("a p w -> (a p) w")).then_inc(loaded[n], 16)
                    groups(sp, body)

                @block.tensor
                def _(pe):
                    def body(t, first):
                        for n in range(2):
                            pe.wait_ge(loaded[n], t * (16 * NS) + 16 * NS)
                            if not first:
                                pe.wait_ge(taken, t * 2 + (n - 1))
                            for j in range(GC):
                                for i, (_, tiles, table) in enumerate(sides):
                                    tile = tile_of(pe, tiles, t * (2 * GC) + (n * GC + j))
                                    last = nc.tensor.matmul(ps[:, n, (j * NS + i) * 6:(j * NS + i) * 6 + 6], ot[:, n, i, j, :],
                                                            table[:, bass.ds(tile, 1), :, :].rearrange("p a k h -> p (a k h)"),
                                                            start=True, stop=True, skip_group_check=True)
                            last.then_inc(picked, 1)
                    groups(pe, body)

                @block.vector
                def _(dve):
                    def body(t, first):
                        for n in range(2):
                            dve.wait_ge(picked, t * 2 + (n + 1))
                            nc.vector.tensor_reduce(val[:, n, :, :], ps[:, n, 0:GC * NS * 6].rearrange("p (c k h) -> p c h k", c=GC, h=H),
                                                    AX.X, ALU.add).then_inc(taken, 1)
                            dve.wait_ge(taken, t * 2 + (n + 1))
                            finish(dve, val[:, n, :, :], bass.ds(t * (2 * GC) + n * GC, GC), chain, t * 2 + (n + 1))
                    groups(dve, body)

        def max_pass(name, shifted, top_of):
            with ExitStack() as ctx:
                oh = sb(name + "_oh", [T, 2, 4, T], F32, ctx)
                places = sb(name + "_places", [T, 2, 4], F32, ctx)
                placed4 = take_sem(ctx, name + "_places_set")
                diag = sb(name + "_diag", [T, 2, 4, H, T], F32, ctx)
                best = sb(name + "_best", [T, 2, 4, H], F32, ctx)
                aps = ctx.enter_context(nc.psum_tensor(name + "_aps", [T, 2, 4, H * T], F32))
                sem = lambda n: take_sem(ctx, f"{name}_{n}")
                marked, spread, placed, reduced, cleared, noted = map(sem, ["marked", "spread", "placed", "reduced", "cleared", "noted"])
                block = ctx.enter_context(nc.Block())

                @block.gpsimd
                def _(pool):
                    def marking(t, first, last):
                        for k in range(4):
                            if not (first and k < 2):
                                wait_value(pool, placed, t * 4 + (k - 1))
                            nc.gpsimd.tensor_copy(places[:, k % 2, :], src_lo[:, bass.ds(t * 16 + 4 * k, 4)]).then_inc(placed4, 1)
                            wait_value(pool, placed4, t * 4 + (k + 1))
                            for j in range(4):
                                last_ = nc.gpsimd.tensor_scalar(oh[:, k % 2, j, :], iota1[:, :], places[:, k % 2, j:j + 1], None,
                                                                ALU.is_equal)
                            last_.then_inc(marked, 1)
                    peeled(pool, marking)

                @block.scalar
                def _(act):
                    def spreading(t, first, last):
                        for k in range(4):
                            if not (first and k < 2):
                                wait_value(act, placed, t * 4 + (k - 1))
                            for j in range(4):
                                for h in range(H):
                                    last_ = nc.scalar.activation(
                                        diag[:, k % 2, j, h, :], ident[:, :], ACT.Copy,
                                        scale=shifted[:, bass.ds(t * 16 + (4 * k + j), 1), h:h + 1].rearrange("p a h -> p (a h)"))
                            last_.then_inc(spread, 1)
                    peeled(act, spreading)

                @block.tensor
                def _(pe):
                    def place(t, first, last):
                        for k in range(4):
                            pe.wait_ge(marked, t * 4 + (k + 1))
                            pe.wait_ge(spread, t * 4 + (k + 1))
                            if not (first and k < 2):
                                pe.wait_ge(reduced, t * 4 + (k - 1))
                            for j in range(4):
                                last_ = nc.tensor.matmul(aps[:, k % 2, j, :], oh[:, k % 2, j, :],
                                                         diag[:, k % 2, j, :, :].rearrange("p h e -> p (h e)"), start=True, stop=True,
                                                         skip_group_check=True)
                            last_.then_inc(placed, 1)
                    peeled(pe, place)

                @block.vector
                def _(dve):
                    nc.vector.memset(top_of[:, :, :], 0.0).then_inc(cleared, 1)
                    dve.wait_ge(cleared, 1)

                    def largest(t, first, last):
                        for k in range(4):
                            dve.wait_ge(placed, t * 4 + (k + 1))
                            nc.vector.tensor_reduce(best[:, k % 2, :, :].rearrange("p c h -> p (c h)"),
                                                    aps[:, k % 2, :, :].rearrange("p c (h e) -> p (c h) e", h=H), AX.X, ALU.max).then_inc(reduced, 1)
                            dve.wait_ge(reduced, t * 4 + (k + 1))
                            for j in range(4):
                                tile = tile_of(dve, src_tile, t * 16 + (4 * k + j))
                                m = top_of[:, bass.ds(tile, 1), :].rearrange("p a h -> p (a h)")
                                if not (first and k == j == 0):
                                    dve.wait_ge(noted, t * 16 + (4 * k + j))
                                nc.vector.tensor_tensor(m, m, best[:, k % 2, j, :], ALU.max).then_inc(noted, 1)
                    peeled(dve, largest)

        def dense_phase(name, sources, w_parts, finish, steps):
            K = sum(s.shape[2] for s in sources)
            with ExitStack() as ctx:
                stage = sb(name + "_stage", [T, K], F32, ctx)
                zT = sb(name + "_zT", [T, 2, T], F32, ctx)
                psT = ctx.enter_context(nc.psum_tensor(name + "_psT", [T, 2, T], F32))
                psO = ctx.enter_context(nc.psum_tensor(name + "_psO", [T, D], F32))
                sem = lambda n: take_sem(ctx, f"{name}_{n}")
                staged, turned, copied, multiplied, chain = map(sem, ["staged", "turned", "copied", "multiplied", "chain"])
                cuts = [(0, min(K, T))] + ([(T, K - T)] if K > T else [])
                block = ctx.enter_context(nc.Block())

                @block.vector
                def _(dve):
                    ln = Chain(dve, chain)
                    with dve.Fori(0, NT) as t:
                        o = 0
                        for s in sources:
                            w = s.shape[2]
                            last = nc.vector.tensor_scalar(stage[:, o:o + w], s[:, bass.ds(t, 1), :].rearrange("p a d -> p (a d)"),
                                                           1.0, None, ALU.mult)
                            o += w
                        last.then_inc(staged, 1)
                        dve.wait_ge(multiplied, t + 1)
                        ln.base, ln.n = t * steps, 0
                        finish(ln, bass.ds(t, 1), psO[:, :])
                        assert ln.n == steps

                @block.tensor
                def _(pe):
                    with pe.Fori(0, NT) as t:
                        wait_value(pe, staged, t + 1)
                        for i, (o, w) in enumerate(cuts):
                            last = nc.tensor.transpose(psT[0:w, i, :], stage[:, o:o + w], ident[:, :])
                        last.then_inc(turned, 1)
                        wait_value(pe, copied, t + 1)
                        for i, (o, w) in enumerate(cuts):
                            last = nc.tensor.matmul(psO[:, :], zT[0:w, i, :], w_parts[i], start=(i == 0), stop=(i == len(cuts) - 1))
                        last.then_inc(multiplied, 1)

                @block.scalar
                def _(act):
                    with act.Fori(0, NT) as t:
                        act.wait_ge(turned, t + 1)
                        for i, (o, w) in enumerate(cuts):
                            last = nc.scalar.activation(zT[0:w, i, :], psT[0:w, i, :], ACT.Copy)
                        last.then_inc(copied, 1)

        def vector_steps(name, steps, sqrt=None):
            with ExitStack() as ctx:
                chain = take_sem(ctx, name + "_chain")
                root_in = take_sem(ctx, name + "_root_in")
                root_out = take_sem(ctx, name + "_root_out")
                block = ctx.enter_context(nc.Block())

                @block.vector
                def _(dve):
                    steps(Chain(dve, chain), dve, root_in, root_out)

                if sqrt is not None:
                    @block.scalar
                    def _(act):
                        act.wait_ge(root_in, 1)
                        nc.scalar.activation(sqrt[1], sqrt[0], ACT.Sqrt).then_inc(root_out, 1)

        w1a, w1b = sb("w1a", [T, D], F32), sb("w1b", [D, D], F32)
        w2a, w2b = sb("w2a", [T, D], F32), sb("w2b", [D, D], F32)
        wo = sb("wo", [T, L, D], F32)
        wht = sb("wht", [D, L, 4 * D], F32)
        aht = sb("aht", [T, L, 4 * D], F32)
        rows = sb("rows", [T, 2 + 2 * L, D], F32)
        st = sb("st", [T, 6, NT], F32)
        with ExitStack() as ctx:
            s_load = take_sem(ctx, "weights_loaded")
            block = ctx.enter_context(nc.Block())

            @block.sync
            def _(sp):
                loads = [(w1a[:, :], W1[0:T, :]), (w1b[:, :], W1[T:3 * D, :]), (w2a[:, :], W2[0:T, :]), (w2b[:, :], W2[T:3 * D, :]),
                         (wo[:, :, :], W_o.rearrange("l p d -> p l d")),
                         (wht[:, :, 0:2 * D], W_h.rearrange("l p n -> p l n")), (wht[:, :, 2 * D:], W_t.rearrange("l p n -> p l n")),
                         (rows[:, 0, :], b1.partition_broadcast(T)), (rows[:, 1, :], b2.partition_broadcast(T))]
                for l in range(L):
                    loads += [(aht[:, l, 0:2 * D], att_h[l, :, :].rearrange("h d -> (h d)").partition_broadcast(T)),
                              (aht[:, l, 2 * D:], att_t[l, :, :].rearrange("h d -> (h d)").partition_broadcast(T)),
                              (rows[:, 2 + l, :], ln_g[l, :].partition_broadcast(T)),
                              (rows[:, 2 + L + l, :], ln_b[l, :].partition_broadcast(T))]
                for to, frm in loads:
                    sp.dma_start(to, frm).then_inc(s_load, 16)
                sp.wait_ge(s_load, 16 * len(loads))

        with ExitStack() as ctx:
            parts = sb("parts0", [T, NT, 3, D], BF16, ctx)
            rest = sb("rest0", [T, NT, D], F32, ctx)
            acc0 = sb("acc0", [T, NT, 2 * D + 1], F32, ctx)
            acc1 = sb("acc1", [T, NT, D], F32, ctx)
            inv_deg = sb("inv_deg", [T, NT], F32, ctx)
            hid = sb("hid", [T, NT, D], F32, ctx)
            mean = lambda a: inv_deg[:, :].unsqueeze(2).to_broadcast([T, NT, a.shape[2]])

            vector_steps("split_x", lambda ln, dve, i, o: split_steps(nc, ln, parts, x[:, :, :], rest[:, :, :]))
            spread_pass("near1", 0, src_tile, D, parts, dst_lo, dst_tile, None, "record", acc0)

            def degrees(ln, dve, i, o):
                ln.step(nc.vector.tensor_scalar(st[:, 0, :], acc0[:, :, 2 * D], 1.0, None, ALU.max))
                ln.step(nc.vector.reciprocal(inv_deg[:, :], st[:, 0, :]))
                a = acc0[:, :, 0:2 * D]
                ln.step(nc.vector.tensor_tensor(a, a, mean(a), ALU.mult))
            vector_steps("degrees", degrees)

            def relu_out(to, bias):
                def finish(ln, tile, ps):
                    y = to[:, tile, :].rearrange("p a d -> p (a d)")
                    ln.step(nc.vector.tensor_tensor(y, ps, bias, ALU.add))
                    ln.step(nc.vector.tensor_scalar(y, y, 0.0, None, ALU.max))
                return finish
            dense_phase("layer1", [x, acc0[:, :, 0:D], acc0[:, :, D:2 * D]], [w1a[:, :], w1b[:, :]], relu_out(hid, rows[:, 0, :]), 2)
            vector_steps("split_hid", lambda ln, dve, i, o: split_steps(nc, ln, parts, hid[:, :, :], rest[:, :, :]))
            spread_pass("near2", 0, src_tile, D, parts, dst_lo, dst_tile, None, None, acc1)
            vector_steps("mean2", lambda ln, dve, i, o: ln.step(nc.vector.tensor_tensor(acc1[:, :, :], acc1[:, :, :], mean(acc1), ALU.mult)))
            dense_phase("layer2", [hid, acc1, acc0[:, :, D:2 * D]], [w2a[:, :], w2b[:, :]], relu_out(rest, rows[:, 1, :]), 2)

            def first_norm(ln, dve, i, o):
                ln.step(nc.vector.tensor_tensor(rest[:, :, :], rest[:, :, :], x[:, :, :], ALU.add))
                layernorm_steps(nc, ln, rest[:, :, :], x[:, :, :], hid[:, :, :], st, i, o, dve)
            vector_steps("norm0", first_norm, (st[:, 3, :], st[:, 4, :]))

        def store_nodes(a):
            with ExitStack() as ctx:
                s_out = take_sem(ctx, "out_stored")
                block = ctx.enter_context(nc.Block())

                @block.sync
                def _(sp):
                    sp.dma_start(out[0:(NT - 1) * T, :].rearrange("(t p) d -> p t d", p=T), a[:, 0:NT - 1, :]).then_inc(s_out, 16)
                    sp.dma_start(out[(NT - 1) * T:N, :], a[0:LAST, NT - 1, :]).then_inc(s_out, 16)
                    sp.wait_ge(s_out, 32)
        ent = sb("ent", [T, NT, D], F32)
        h = sb("h", [T, NT, D], F32)
        ah = sb("ah", [T, NT, D], F32)
        Z = sb("Z", [T, NT, 2 * D], F32)
        acc = sb("acc", [T, NT, 2 * D + 2], F32)
        parts = sb("parts", [T, NT, 3, 2 * D], BF16)
        w_edge = sb("w_edge", [T, NCH, H], F32)
        shifted = sb("shifted", [T, NCH, H], F32)
        score4 = sb("score4", [T, NT, 4], F32)
        top_of = sb("top_of", [T, NT, H], F32)
        rest2 = sb("rest2", [T, NT, H], F32)
        pick_src = sb("pick_src", [T, NT, 3, H], BF16)
        pick_dst = sb("pick_dst", [T, NT, 3, H], BF16)
        norm = sb("norm", [T, NT, H], F32)
        least = sb("least", [T, 4], F32)

        vector_steps("ent", lambda ln, dve, i, o: ln.step(nc.vector.tensor_copy(ent[:, :, :], x[:, :, :])))
        for l in range(L):
            nm = f"l{l}"

            def layer_norm(ln, dve, i, o):
                layernorm_steps(nc, ln, ent[:, :, :], h[:, :, :], ah[:, :, :], st, i, o, dve, rows[:, 2 + l, :], rows[:, 2 + L + l, :])
                ln.step(nc.vector.tensor_scalar(ah[:, :, :], h[:, :, :], ALPHA, None, ALU.mult))
            vector_steps(nm + "_norm", layer_norm, (st[:, 3, :], st[:, 4, :]))
            score_phase(nm + "_score", h, NT, T, wht[:, l, :], aht[:, l, :], score4)

            def split_scores(ln, dve, i, o):
                split_steps(nc, ln, pick_src, score4[:, :, 0:2], rest2[:, :, :])
                split_steps(nc, ln, pick_dst, score4[:, :, 2:4], rest2[:, :, :])
            vector_steps(nm + "_split_scores", split_scores)

            def edge_scores(dve, val, cols, chain, n):
                nc.vector.tensor_tensor(val, val, s_rel[:, cols, 2 * l:2 * l + 2], ALU.add).then_inc(chain, 1)
                dve.wait_ge(chain, n)
                nc.vector.scalar_tensor_tensor(out=w_edge[:, cols, :], in0=val, scalar=0.01, in1=val, op0=ALU.mult, op1=ALU.max)
            pick_pass(nm + "_edge", [(0, src_tile, pick_src), (1, dst_tile, pick_dst)], edge_scores)

            with ExitStack() as ctx:
                s_least, s_all = take_sem(ctx, nm + "_least"), take_sem(ctx, nm + "_all_least")
                chain = take_sem(ctx, nm + "_least_chain")
                block = ctx.enter_context(nc.Block())

                @block.vector
                def _(dve):
                    ln = Chain(dve, chain)
                    ln.step(nc.vector.tensor_reduce(least[:, 0:1], w_edge[:, :, :].rearrange("p c h -> p (c h)"), AX.X, ALU.min))
                    nc.vector.tensor_scalar(least[:, 1:2], least[:, 0:1], -1.0, None, ALU.mult).then_inc(s_least, 1)
                    dve.wait_ge(s_all, 1)
                    ln.step(nc.vector.tensor_scalar(least[:, 3:4], least[:, 2:3], 1.0, None, ALU.add))
                    nc.vector.tensor_scalar(shifted[:, :, :], w_edge[:, :, :], least[:, 3:4], None, ALU.add)

                @block.gpsimd
                def _(pool):
                    pool.wait_ge(s_least, 1)
                    nc.gpsimd.partition_all_reduce(least[:, 2:3], least[:, 1:2], T, bass.bass_isa.ReduceOp.max).then_inc(s_all, 1)
            max_pass(nm + "_max", shifted, top_of)

            def unshift(ln, dve, i, o):
                ln.step(nc.vector.tensor_scalar(top_of[:, :, :], top_of[:, :, :], least[:, 3:4], None, ALU.subtract))
                split_steps(nc, ln, pick_src, top_of[:, :, :], rest2[:, :, :])
            vector_steps(nm + "_unshift", unshift)

            def below_top(dve, val, cols, chain, n):
                nc.vector.tensor_tensor(w_edge[:, cols, :], w_edge[:, cols, :], val, ALU.subtract)
            pick_pass(nm + "_under", [(0, src_tile, pick_src)], below_top)
            with ExitStack() as ctx:
                block = ctx.enter_context(nc.Block())

                @block.scalar
                def _(act):
                    nc.scalar.activation(w_edge[:, :, :], w_edge[:, :, :], ACT.Exp)

            vector_steps(nm + "_split_h", lambda ln, dve, i, o: split_steps(nc, ln, parts[:, :, :, 0:D], h[:, :, :], Z[:, :, 0:D]))
            for it in range(POW_ITER):
                first = it == 0
                spread_pass(f"{nm}_spread{it}", 1, dst_tile, D if first else 2 * D, parts[:, :, :, 0:D] if first else parts,
                            src_lo, src_tile, w_edge, "weight" if first else None,
                            acc if first else acc[:, :, 0:2 * D])

                def mix(ln, dve, i, o):
                    if first:
                        ln.step(nc.vector.tensor_scalar(norm[:, :, :], acc[:, :, 2 * D:2 * D + 2], 1e-30, None, ALU.max))
                        ln.step(nc.vector.reciprocal(norm[:, :, :], norm[:, :, :]))
                        ln.step(nc.vector.tensor_scalar(norm[:, :, :], norm[:, :, :], 1.0 - ALPHA, None, ALU.mult))
                    for k in range(H):
                        s = slice(k * D, (k + 1) * D)
                        ln.step(nc.vector.tensor_tensor(Z[:, :, s], acc[:, :, s], norm[:, :, k:k + 1].to_broadcast([T, NT, D]), ALU.mult))
                        ln.step(nc.vector.tensor_tensor(Z[:, :, s], Z[:, :, s], ah[:, :, :], ALU.add))
                    if it < POW_ITER - 1:
                        split_steps(nc, ln, parts, Z[:, :, :], acc[:, :, 0:2 * D])
                vector_steps(f"{nm}_mix{it}", mix)

            def residual(ln, tile, ps):
                y = ent[:, tile, :].rearrange("p a d -> p (a d)")
                ln.step(nc.vector.tensor_tensor(y, y, ps, ALU.add))
            dense_phase(nm + "_conv", [Z], [wo[:, l, :]], residual, 1)

        def last_norm(ln, dve, i, o):
            ln.step(nc.vector.tensor_tensor(ent[:, :, :], ent[:, :, :], x[:, :, :], ALU.add))
            layernorm_steps(nc, ln, ent[:, :, :], h[:, :, :], ah[:, :, :], st, i, o, dve)
        vector_steps("norm_last", last_norm, (st[:, 3, :], st[:, 4, :]))
        store_nodes(h)


_INS = ["x", "src", "dst", "edge_attr_64", "edge_type_500", "L0_gnn_W1", "L0_gnn_b1", "L0_gnn_W2", "L0_gnn_b2",
        "L1_gnn_relation_embed", "L1_gnn_ln_gamma", "L1_gnn_ln_beta", "L1_gnn_W_h", "L1_gnn_W_t", "L1_gnn_W_r",
        "L1_gnn_att_h", "L1_gnn_att_t", "L1_gnn_att_r", "L1_gnn_W_o"]


def kernel(**inputs):
    import numpy as np
    import concourse.bacc as bacc
    from concourse.bass_utils import run_bass_kernel_spmd as run

    nc = bacc.Bacc("TRN2", target_bir_lowering=False, num_devices=1)
    arrays, args = {}, []
    for name in _INS:
        a = np.ascontiguousarray(inputs[name])
        arrays[f"in_{name}"] = a
        args.append(nc.dram_tensor(f"in_{name}", a.shape, mybir.dt.from_np(a.dtype), kind="ExternalInput").ap())
    out = nc.dram_tensor("out_nodes", (N, D), F32, kind="ExternalOutput").ap()
    gnn_program(nc, *args, out)
    return run(nc, [arrays], core_ids=[0]).results[0]["out_nodes"]
```

```python
import concourse.bass as bass
from concourse import mybir
from contextlib import ExitStack

F32 = mybir.dt.float32
BF16 = mybir.dt.bfloat16
F8 = mybir.dt.float8e4
U8 = mybir.dt.uint8
I32 = mybir.dt.int32
U32 = mybir.dt.uint32
ALU = mybir.AluOpType
ACT = mybir.ActivationFunctionType
AX = mybir.AxisListType

N = 3125
E = 100000
D = 64
H = 2
R = 500
L = 2
T = 128
NT = -(-N // T)
LAST = N - (NT - 1) * T
EP = 125
EC = E // EP
NBLK = NT * NT
BCH = 2
CAP = BCH * T
GC = 8
NCH = -(-((E + NBLK * (T - 1)) // T) // (2 * GC)) * 2 * GC
NG = NCH // GC
NQ = NCH // 4
RW = 72
R_ONE, R_SRC, R_DST, R_REL = 64, 65, 66, 68
ALPHA = 0.15
POW_ITER = 3
LN_EPS = 1e-5
RP = 125
RT = R // RP


def wait_value(eng, sem, value):
    eng.wait_ge(sem, value)
    eng.nop(nofuse=True)


class Chain:

    def __init__(self, eng, sem):
        self.eng, self.sem, self.base, self.n = eng, sem, 0, 0

    def step(self, ins):
        self.n += 1
        ins.then_inc(self.sem, 1)
        self.eng.wait_ge(self.sem, self.base + self.n)


def layernorm_steps(nc, ln, x, y, tmp, st, sqrt_in, sqrt_out, dve, gamma=None, beta=None):
    nt = x.shape[1]
    bc = lambda a: a.unsqueeze(2).to_broadcast([T, nt, D])
    ln.step(nc.vector.tensor_reduce(st[:, 0, :], x, AX.X, ALU.add))
    ln.step(nc.vector.tensor_scalar(st[:, 1, :], st[:, 0, :], 1.0 / D, None, ALU.mult))
    ln.step(nc.vector.tensor_tensor(y, x, bc(st[:, 1, :]), ALU.subtract))
    ln.step(nc.vector.tensor_tensor(tmp, y, y, ALU.mult))
    ln.step(nc.vector.tensor_reduce(st[:, 2, :], tmp, AX.X, ALU.add))
    nc.vector.tensor_scalar(st[:, 3, :], st[:, 2, :], 1.0 / D, LN_EPS, ALU.mult, ALU.add).then_inc(sqrt_in, 1)
    dve.wait_ge(sqrt_out, 1)
    ln.step(nc.vector.reciprocal(st[:, 5, :], st[:, 4, :]))
    ln.step(nc.vector.tensor_tensor(y, y, bc(st[:, 5, :]), ALU.mult))
    if gamma is not None:
        row = lambda a: a.unsqueeze(1).to_broadcast([T, nt, D])
        ln.step(nc.vector.tensor_tensor(y, y, row(gamma), ALU.mult))
        ln.step(nc.vector.tensor_tensor(y, y, row(beta), ALU.add))


def split_steps(nc, ln, parts, src, rest):
    ln.step(nc.vector.tensor_copy(parts[:, :, 0, :], src))
    ln.step(nc.vector.tensor_tensor(rest, src, parts[:, :, 0, :], ALU.subtract))
    ln.step(nc.vector.tensor_copy(parts[:, :, 1, :], rest))
    ln.step(nc.vector.tensor_tensor(parts[:, :, 2, :], rest, parts[:, :, 1, :], ALU.subtract))


def gnn_program(nc, x_in, src_in, dst_in, attr_in, type_in, W1, b1, W2, b2, rel, ln_g, ln_b,
                W_h, W_t, W_r, att_h, att_t, att_r, W_o, out):
    top = ExitStack()

    taken_sems = {}

    def take_sem(stack, name):
        if id(stack) not in taken_sems:
            taken_sems[id(stack)] = []

            def give_back():
                nc.clear_and_free_semaphores(taken_sems.pop(id(stack)))
                nc.all_engine_barrier()
            stack.callback(give_back)
        taken_sems[id(stack)].append(nc.alloc_semaphore(name))
        return taken_sems[id(stack)][-1]

    def sb(name, shape, dt, stack=top):
        return stack.enter_context(nc.sbuf_tensor(name, shape, dt))

    records = nc.dram_tensor("records", (NCH * T, RW), F32).ap()
    onehots = nc.dram_tensor("onehots", (2, NG, T, GC * T), BF16).ap()
    onehots8 = nc.dram_tensor("onehots8", (4, NT, T, NT * BCH * T), U8).ap()
    rel_scores = nc.dram_tensor("rel_scores", (R, 2 * L), F32).ap()
    rec_groups = records.rearrange("(g p c) w -> g p (c w)", p=T, c=GC)

    with top:
        iota1 = sb("iota1", [T, T], F32)
        ident = sb("ident", [T, T], F32)
        identb = sb("identb", [T, T], BF16)
        below = sb("below", [T, T], F32)
        ones = sb("ones", [T, T], F32)
        x = sb("x", [T, NT, D], F32)
        block_end = sb("block_end", [NT, NT], F32)
        overfull = sb("overfull", [T, 1], F32)
        overfull_i = sb("overfull_i", [1, 1], I32)
        ar = sb("ar", [T, 4 * D], F32)

        def score_phase(name, table, nt, rows, w_ap, att_ap, result):
            with ExitStack() as ctx:
                stage = sb(name + "_stage", [T, D], F32, ctx)
                tT = sb(name + "_tT", [D, T], F32, ctx)
                act = sb(name + "_act", [T, 4 * D], F32, ctx)
                prod = sb(name + "_prod", [T, 4, D], F32, ctx)
                psT = ctx.enter_context(nc.psum_tensor(name + "_psT", [D, T], F32))
                psW = ctx.enter_context(nc.psum_tensor(name + "_psW", [T, 4 * D], F32))
                sem = lambda n: take_sem(ctx, f"{name}_{n}")
                staged, turned, copied, multiplied, squashed = map(sem, ["staged", "turned", "copied", "multiplied", "squashed"])
                chain = sem("chain")
                block = ctx.enter_context(nc.Block())

                @block.vector
                def _(dve):
                    ln = Chain(dve, chain)
                    with dve.Fori(0, nt) as t:
                        nc.vector.tensor_scalar(stage[0:rows, :], table[0:rows, bass.ds(t, 1), :].rearrange("p a d -> p (a d)"),
                                                1.0, None, ALU.mult).then_inc(staged, 1)
                        dve.wait_ge(squashed, t + 1)
                        ln.base, ln.n = t * 2, 0
                        ln.step(nc.vector.tensor_tensor(prod[0:rows, :, :].rearrange("p k d -> p (k d)"), act[0:rows, :],
                                                        att_ap[0:rows, :], ALU.mult))
                        ln.step(nc.vector.tensor_reduce(result[0:rows, bass.ds(t, 1), :].rearrange("p a k -> p (a k)"),
                                                        prod[0:rows, :, :], AX.X, ALU.add))

                @block.tensor
                def _(pe):
                    with pe.Fori(0, nt) as t:
                        wait_value(pe, staged, t + 1)
                        nc.tensor.transpose(psT[:, 0:rows], stage[0:rows, :], ident[0:rows, 0:rows]).then_inc(turned, 1)
                        pe.wait_ge(copied, t + 1)
                        nc.tensor.matmul(psW[0:rows, :], tT[:, 0:rows], w_ap, start=True, stop=True).then_inc(multiplied, 1)

                @block.scalar
                def _(act_e):
                    with act_e.Fori(0, nt) as t:
                        act_e.wait_ge(turned, t + 1)
                        nc.scalar.activation(tT[:, 0:rows], psT[:, 0:rows], ACT.Copy).then_inc(copied, 1)
                        act_e.wait_ge(multiplied, t + 1)
                        nc.scalar.activation(act[0:rows, :], psW[0:rows, :], ACT.Tanh).then_inc(squashed, 1)

        with ExitStack() as ctx:
            zeros = sb("zeros", [T, GC * RW], F32, ctx)
            sem = lambda n: take_sem(ctx, n)
            s_zero, s_clear, s_load, s_set, s_xz = map(sem, ["zero_ready", "cleared", "x_loaded", "const_set", "x_zeroed"])
            block = ctx.enter_context(nc.Block())

            @block.vector
            def _(dve):
                nc.vector.memset(zeros[:, :], 0.0).then_inc(s_zero, 1)
                nc.vector.memset(x[:, NT - 1, :], 0.0).then_inc(s_xz, 1)

            @block.sync
            def _(sp):
                sp.wait_ge(s_xz, 1)
                sp.dma_start(x[:, 0:NT - 1, :], x_in[0:(NT - 1) * T, :].rearrange("(t p) d -> p t d", p=T)).then_inc(s_load, 16)
                sp.dma_start(x[0:LAST, NT - 1, :], x_in[(NT - 1) * T:N, :]).then_inc(s_load, 16)
                sp.wait_ge(s_zero, 1)
                with sp.Fori(0, NG) as g:
                    sp.dma_start(rec_groups[bass.ds(g, 1), :, :].rearrange("a p w -> (a p) w"), zeros[:, :]).then_inc(s_clear, 16)
                sp.wait_ge(s_load, 32)
                sp.wait_ge(s_clear, NG * 16)

            @block.gpsimd
            def _(pool):
                nc.gpsimd.iota(iota1[:, :], [[1, T]], base=1, channel_multiplier=0, allow_small_or_imprecise_dtypes=True)
                nc.gpsimd.memset(ident[:, :], 0.0).then_inc(s_set, 1)
                nc.gpsimd.memset(identb[:, :], 0.0).then_inc(s_set, 1)
                nc.gpsimd.memset(ones[:, :], 1.0).then_inc(s_set, 1)
                pool.wait_ge(s_set, 3)
                for m in (ident, identb):
                    nc.gpsimd.affine_select(out=m[:, :], in_=m[:, :], compare_op=ALU.not_equal, fill=1.0,
                                            base=0, pattern=[[-1, T]], channel_multiplier=1)
                nc.gpsimd.affine_select(out=below[:, :], in_=ones[:, :], compare_op=ALU.is_gt, fill=0.0,
                                        base=0, pattern=[[1, T]], channel_multiplier=-1)

        with ExitStack() as ctx:
            rel_sb = sb("rel_sb", [T, RT, D], F32, ctx)
            wr = sb("wr", [D, 4 * D], F32, ctx)
            rs = sb("rs", [T, RT, 4], F32, ctx)
            with ExitStack() as c2:
                s_load = take_sem(c2, "rel_loaded")
                block = c2.enter_context(nc.Block())

                @block.sync
                def _(sp):
                    sp.dma_start(rel_sb[0:RP, :, :], rel.rearrange("(t p) d -> p t d", p=RP)).then_inc(s_load, 16)
                    sp.dma_start(wr[:, :].rearrange("p (l n) -> p l n", l=L), W_r.rearrange("l p n -> p l n")).then_inc(s_load, 16)
                    sp.dma_start(ar[:, :], att_r.rearrange("l h d -> (l h d)").partition_broadcast(T)).then_inc(s_load, 16)
                    sp.wait_ge(s_load, 48)
            score_phase("rel", rel_sb, RT, RP, wr[:, :], ar, rs)
            with ExitStack() as c2:
                s_store = take_sem(c2, "rel_stored")
                block = c2.enter_context(nc.Block())

                @block.sync
                def _(sp):
                    sp.dma_start(rel_scores.rearrange("(t p) k -> p t k", p=RP), rs[0:RP, :, :]).then_inc(s_store, 16)
                    sp.wait_ge(s_store, 16)

        with ExitStack() as slot_ctx:
            row_idx = sb("row_idx", [EP, EC], I32, slot_ctx)
            slo = sb("slo", [EP, EC], F32, slot_ctx)
            dlo = sb("dlo", [EP, EC], F32, slot_ctx)
            typ = sb("typ", [EP, EC], I32, slot_ctx)
            edge_rel = sb("edge_rel", [EP, EC, 2 * L], F32, slot_ctx)
            with ExitStack() as ctx:
                s_hi = sb("s_hi", [EP, EC], F32, ctx)
                d_hi = sb("d_hi", [EP, EC], F32, ctx)
                iota_t = sb("iota_t", [EP, NT], F32, ctx)
                counts = sb("counts", [NT, EC + 1, NT], F32, ctx)
                rank = sb("rank", [EP, EC], F32, ctx)

                with ExitStack() as c2:
                    src_i = sb("src_i", [EP, EC], I32, c2)
                    dst_i = sb("dst_i", [EP, EC], I32, c2)
                    hi_i = sb("hi_i", [EP, 4, EC], I32, c2)
                    s_load = take_sem(c2, "edges_loaded")
                    chain = take_sem(c2, "cut_chain")
                    block = c2.enter_context(nc.Block())

                    @block.sync
                    def _(sp):
                        for to, frm in ((src_i, src_in), (dst_i, dst_in), (typ, type_in)):
                            sp.dma_start(to[:, :], frm.rearrange("(p c) -> p c", p=EP)).then_inc(s_load, 16)
                        sp.wait_ge(s_load, 48)

                    @block.gpsimd
                    def _(pool):
                        nc.gpsimd.iota(iota_t[:, :], [[1, NT]], base=0, channel_multiplier=0, allow_small_or_imprecise_dtypes=True)

                    @block.vector
                    def _(dve):
                        dve.wait_ge(s_load, 48)
                        nc.vector.memset(counts[:, 0, :], 0.0)
                        for i, (a, hi, lo) in enumerate(((src_i, s_hi, slo), (dst_i, d_hi, dlo))):
                            nc.vector.tensor_scalar(hi_i[:, 2 * i, :], a[:, :], 7, None, ALU.logical_shift_right).then_inc(chain, 1)
                            nc.vector.tensor_scalar(hi_i[:, 2 * i + 1, :], a[:, :], T - 1, None, ALU.bitwise_and).then_inc(chain, 1)
                            dve.wait_ge(chain, 2 * i + 2)
                            nc.vector.tensor_copy(hi[:, :], hi_i[:, 2 * i, :])
                            nc.vector.tensor_scalar(lo[:, :], hi_i[:, 2 * i + 1, :], 1.0, None, ALU.add)

                BC = 20
                with ExitStack() as c2:
                    oa = sb("oa", [EP, 2, BC, NT], BF16, c2)
                    ob = sb("ob", [EP, 2, BC, NT], BF16, c2)
                    psH = c2.enter_context(nc.psum_tensor("psH", [NT, 2, 512], F32))
                    sem = lambda n: take_sem(c2, n)
                    marked, counted, kept = map(sem, ["cols_marked", "cols_counted", "counts_kept"])
                    block = c2.enter_context(nc.Block())

                    def mark(n, c0):
                        for o, hi in ((oa, s_hi), (ob, d_hi)):
                            last = nc.vector.tensor_tensor(
                                o[:, n, :, :], hi[:, bass.ds(c0, BC)].unsqueeze(2).to_broadcast([EP, BC, NT]),
                                iota_t[:, :].unsqueeze(1).to_broadcast([EP, BC, NT]), ALU.is_equal)
                        last.then_inc(marked, 1)

                    ROUNDS = EC // BC // 2

                    @block.vector
                    def _(dve):
                        mark(0, 0)
                        mark(1, BC)
                        with dve.Fori(1, ROUNDS) as t:
                            for n in range(2):
                                dve.wait_ge(counted, t * 2 + (n - 1))
                                mark(n, t * (2 * BC) + n * BC)

                    @block.tensor
                    def _(pe):
                        def count(n):
                            for j in range(BC):
                                last = nc.tensor.matmul(psH[:, n, j * NT:(j + 1) * NT], oa[:, n, j, :], ob[:, n, j, :],
                                                        start=True, stop=True, skip_group_check=True)
                            last.then_inc(counted, 1)
                        for n in range(2):
                            pe.wait_ge(marked, n + 1)
                            count(n)
                        with pe.Fori(1, ROUNDS) as t:
                            for n in range(2):
                                pe.wait_ge(marked, t * 2 + (n + 1))
                                pe.wait_ge(kept, t * 2 + (n - 1))
                                count(n)

                    @block.scalar
                    def _(act):
                        with act.Fori(0, ROUNDS) as t:
                            for n in range(2):
                                wait_value(act, counted, t * 2 + (n + 1))
                                nc.scalar.activation(counts[:, bass.ds(t * (2 * BC) + (n * BC + 1), BC), :].rearrange("p c b -> p (c b)"),
                                                     psH[:, n, 0:BC * NT], ACT.Copy).then_inc(kept, 1)

                with ExitStack() as c2:
                    small = sb("small", [NT, 6, NT], F32, c2)
                    small_i = sb("small_i", [NT, 2, NT], I32, c2)
                    row_base = sb("row_base", [NT, 1], F32, c2)
                    own = sb("own", [NT, 3, NT], F32, c2)
                    most = sb("most", [NT, 2], F32, c2)
                    psB = c2.enter_context(nc.psum_tensor("psB", [NT, 512], F32))
                    psO = c2.enter_context(nc.psum_tensor("psOver", [T, 512], F32))
                    sem = lambda n: take_sem(c2, n)
                    chain, totals, based, over, told, s_iota = map(sem, ["slot_chain", "row_totals", "row_bases", "blocks_over", "told", "own_set"])
                    block = c2.enter_context(nc.Block())

                    @block.gpsimd
                    def _(pool):
                        nc.gpsimd.iota(own[:, 0, :], [[CAP, NT]], base=0, channel_multiplier=NT * CAP,
                                       allow_small_or_imprecise_dtypes=True).then_inc(s_iota, 1)

                    @block.tensor
                    def _(pe):
                        pe.wait_ge(over, 1)
                        nc.tensor.matmul(psO[:, 0:1], ones[0:NT, 0:T], most[:, 1:2], start=True, stop=True).then_inc(told, 1)
                        pe.wait_ge(totals, 1)
                        nc.tensor.matmul(psB[:, 0:1], below[0:NT, 0:NT], small[:, 2, NT - 1:NT], start=True, stop=True).then_inc(based, 1)

                    @block.vector
                    def _(dve):
                        ln = Chain(dve, chain)
                        for b in range(NT):
                            c = counts[:, 1:EC + 1, b]
                            last = nc.vector.tensor_tensor_scan(c, c, c, 0.0, ALU.add, ALU.max)
                        ln.step(last)
                        ln.step(nc.vector.tensor_reduce(most[:, 0:1], counts[:, EC, :], AX.X, ALU.max))
                        nc.vector.tensor_scalar(most[:, 1:2], most[:, 0:1], float(CAP), None, ALU.is_gt).then_inc(over, 1)
                        ln.step(nc.vector.tensor_scalar(small_i[:, 0, :], counts[:, EC, :], float(T - 1), None, ALU.add))
                        ln.step(nc.vector.tensor_scalar(small_i[:, 1, :], small_i[:, 0, :], 7, None, ALU.logical_shift_right))
                        ln.step(nc.vector.tensor_copy(small[:, 1, :], small_i[:, 1, :]))
                        nc.vector.tensor_tensor_scan(small[:, 2, :], small[:, 1, :], small[:, 1, :], 0.0, ALU.add, ALU.max).then_inc(totals, 1)
                        dve.wait_ge(told, 1)
                        ln.step(nc.vector.tensor_scalar(overfull[:, :], psO[:, 0:1], 1.0, None, ALU.min))
                        ln.step(nc.vector.tensor_copy(overfull_i[:, :], overfull[0:1, :]))
                        dve.wait_ge(based, 1)
                        ln.step(nc.vector.tensor_copy(row_base[:, :], psB[:, 0:1]))
                        ln.step(nc.vector.tensor_scalar(block_end[:, :], small[:, 2, :], row_base[:, :], None, ALU.add))
                        ln.step(nc.vector.tensor_tensor(small[:, 4, :], block_end[:, :], small[:, 1, :], ALU.subtract))
                        ln.step(nc.vector.tensor_scalar(small[:, 5, :], small[:, 4, :], float(T), None, ALU.mult))
                        dve.wait_ge(s_iota, 1)
                        ln.step(nc.vector.tensor_tensor(own[:, 1, :], small[:, 5, :], own[:, 0, :], ALU.subtract))
                        ln.step(nc.vector.scalar_tensor_tensor(out=own[:, 2, :], in0=own[:, 1, :], scalar=overfull[0:NT, :], in1=own[:, 0, :],
                                                               op0=ALU.mult, op1=ALU.add))
                        nc.vector.tensor_tensor(counts[:, 0:EC, :], counts[:, 0:EC, :],
                                                own[:, 2, :].unsqueeze(1).to_broadcast([NT, EC, NT]), ALU.add)

                BR = 16
                HC = 8
                with ExitStack() as c2:
                    oa = sb("oa2", [EP, BR, NT], BF16, c2)
                    ob = sb("ob2", [EP, BR, NT], BF16, c2)
                    oaT = sb("oaT", [NT, BR, 128], BF16, c2)
                    oaTf = sb("oaTf", [NT, BR, 128], F32, c2)
                    before = sb("before", [EP, BR, EP], BF16, c2)
                    pick = sb("pick", [EP, BR, NT], F32, c2)
                    psT = c2.enter_context(nc.psum_tensor("psT", [NT, BR, 128], BF16))
                    psS = c2.enter_context(nc.psum_tensor("psS", [EP, BR, 128], F32))
                    psR = c2.enter_context(nc.psum_tensor("psRk", [EP, 512], F32))
                    sem = lambda n: take_sem(c2, n)
                    marked, turned, copied, alike, masked, ranked, chain = map(
                        sem, ["marked", "turned", "copied", "alike", "masked", "ranked", "rank_chain"])
                    typ_st = sb("typ_st", [EP, 2, HC], I32, c2)
                    got = sb("got", [EP, 2, HC, 2 * L], F32, c2)
                    rel_gathered = [take_sem(c2, f"rel_gathered{i}") for i in range(2)]
                    types_staged, got_kept = take_sem(c2, "types_staged"), take_sem(c2, "got_kept")
                    block = c2.enter_context(nc.Block())

                    @block.gpsimd
                    def _(pool):
                        GR = EC // (2 * HC)

                        def gather(t, n):
                            nc.gpsimd.tensor_copy(typ_st[:, n, :], typ[:, bass.ds(t * (2 * HC) + n * HC, HC)]).then_inc(types_staged, 1)
                            wait_value(pool, types_staged, t * 2 + n + 1)
                            for j in range(HC):
                                pool.indirect_dma_start(
                                    out=got[:, n, j, :], out_offset=None, in_=rel_scores,
                                    in_offset=bass.IndirectOffsetOnAxis(ap=typ_st[:, n, j:j + 1].bitcast(U32), axis=0)).then_inc(rel_gathered[n], 16)

                        def keep(t, n):
                            wait_value(pool, rel_gathered[n], t * (16 * HC) + 16 * HC)
                            nc.gpsimd.tensor_copy(edge_rel[:, bass.ds(t * (2 * HC) + n * HC, HC), :], got[:, n, :, :]).then_inc(got_kept, 1)
                            wait_value(pool, got_kept, t * 2 + n + 1)
                        gather(0, 0)
                        gather(0, 1)
                        with pool.Fori(1, GR) as t:
                            for n in range(2):
                                keep(t - 1, n)
                                gather(t, n)
                        for n in range(2):
                            keep(GR - 1, n)

                    @block.vector
                    def _(dve):
                        ln = Chain(dve, chain)
                        with dve.Fori(0, EC // BR) as t:
                            ln.base, ln.n = t * 2, 0
                            for o, hi in ((oa, s_hi), (ob, d_hi)):
                                last = nc.vector.tensor_tensor(
                                    o[:, :, :], hi[:, bass.ds(t * BR, BR)].unsqueeze(2).to_broadcast([EP, BR, NT]),
                                    iota_t[:, :].unsqueeze(1).to_broadcast([EP, BR, NT]), ALU.is_equal)
                            last.then_inc(marked, 1)
                            dve.wait_ge(alike, t + 1)
                            for q in range(BR // 4):
                                last = nc.vector.tensor_tensor(before[:, 4 * q:4 * q + 4, :], psS[:, 4 * q:4 * q + 4, 0:EP],
                                                               below[0:EP, 0:EP].unsqueeze(1).to_broadcast([EP, 4, EP]), ALU.mult)
                            last.then_inc(masked, 1)
                            dve.wait_ge(ranked, t + 1)
                            ln.step(nc.vector.tensor_tensor(pick[:, :, :].rearrange("p c b -> p (c b)"), psR[:, 0:BR * NT],
                                                            ob[:, :, :].rearrange("p c b -> p (c b)"), ALU.mult))
                            ln.step(nc.vector.tensor_reduce(rank[:, bass.ds(t * BR, BR)], pick[:, :, :], AX.X, ALU.add))

                    @block.tensor
                    def _(pe):
                        with pe.Fori(0, EC // BR) as t:
                            wait_value(pe, marked, t + 1)
                            for j in range(BR):
                                last = nc.tensor.transpose(psT[:, j, 0:EP], oa[:, j, :], identb[0:EP, 0:EP])
                            last.then_inc(turned, 1)
                            pe.wait_ge(copied, t * 2 + 2)
                            for j in range(BR):
                                last = nc.tensor.matmul(psS[:, j, 0:EP], oaT[:, j, 0:EP], oaT[:, j, 0:EP], start=True, stop=True,
                                                        skip_group_check=True)
                            last.then_inc(alike, 1)
                            pe.wait_ge(masked, t + 1)
                            for j in range(BR):
                                o = psR[:, j * NT:(j + 1) * NT]
                                nc.tensor.matmul(o, oaTf[:, j, 0:EP], counts[:, bass.ds(t * BR + j, 1), :].rearrange("p a b -> p (a b)"),
                                                 start=True, stop=False, skip_group_check=True)
                                last = nc.tensor.matmul(o, before[:, j, :], ob[:, j, :], start=False, stop=True, skip_group_check=True)
                            last.then_inc(ranked, 1)

                    @block.scalar
                    def _(act):
                        with act.Fori(0, EC // BR) as t:
                            act.wait_ge(turned, t + 1)
                            nc.scalar.activation(oaT[:, :, 0:EP], psT[:, :, 0:EP], ACT.Copy).then_inc(copied, 1)
                            nc.scalar.activation(oaTf[:, :, 0:EP], psT[:, :, 0:EP], ACT.Copy).then_inc(copied, 1)

                with ExitStack() as c2:
                    ri = sb("ri", [EP, 5, EC], I32, c2)
                    rf = sb("rf", [EP, 5, EC], F32, c2)
                    chain = take_sem(c2, "row_chain")
                    block = c2.enter_context(nc.Block())

                    @block.vector
                    def _(dve):
                        ln = Chain(dve, chain)
                        ln.step(nc.vector.tensor_copy(ri[:, 0, :], rank[:, :]))
                        ln.step(nc.vector.tensor_scalar(ri[:, 1, :], ri[:, 0, :], -GC * T, None, ALU.bitwise_and))
                        ln.step(nc.vector.tensor_scalar(ri[:, 2, :], ri[:, 0, :], T - 1, 3, ALU.bitwise_and, ALU.logical_shift_left))
                        ln.step(nc.vector.tensor_scalar(ri[:, 3, :], ri[:, 0, :], 7, GC - 1, ALU.logical_shift_right, ALU.bitwise_and))
                        ln.step(nc.vector.tensor_tensor(ri[:, 4, :], ri[:, 1, :], ri[:, 2, :], ALU.bitwise_or))
                        ln.step(nc.vector.tensor_tensor(ri[:, 4, :], ri[:, 4, :], ri[:, 3, :], ALU.bitwise_or))
                        ln.step(nc.vector.tensor_copy(rf[:, 0, :], ri[:, 4, :]))
                        ln.step(nc.vector.tensor_scalar(ri[:, 1, :], ri[:, 0, :], T - 1, None, ALU.bitwise_and))
                        ln.step(nc.vector.tensor_scalar(ri[:, 2, :], ri[:, 0, :], 7, BCH - 1, ALU.logical_shift_right, ALU.bitwise_and))
                        ln.step(nc.vector.scalar_tensor_tensor(out=rf[:, 1, :], in0=ri[:, 1, :], scalar=float(NT * BCH), in1=ri[:, 2, :],
                                                               op0=ALU.mult, op1=ALU.add))
                        ln.step(nc.vector.scalar_tensor_tensor(out=rf[:, 2, :], in0=d_hi[:, :], scalar=float(BCH), in1=rf[:, 1, :],
                                                               op0=ALU.mult, op1=ALU.add))
                        ln.step(nc.vector.scalar_tensor_tensor(out=rf[:, 3, :], in0=s_hi[:, :], scalar=float(NT * BCH * T), in1=rf[:, 2, :],
                                                               op0=ALU.mult, op1=ALU.add))
                        ln.step(nc.vector.tensor_tensor(rf[:, 4, :], rf[:, 0, :], rf[:, 3, :], ALU.subtract))
                        ln.step(nc.vector.scalar_tensor_tensor(out=row_idx[:, :], in0=rf[:, 4, :], scalar=overfull[0:EP, :], in1=rf[:, 3, :],
                                                               op0=ALU.mult, op1=ALU.add))

            with ExitStack() as ctx:
                HC = 8
                stage = sb("stage", [EP, 2, HC, RW], F32, ctx)
                row_st = sb("row_st", [EP, 2, HC], I32, ctx)
                sem = lambda n: take_sem(ctx, n)
                attr_in_stage = [sem(f"attr_in_stage{i}") for i in range(2)]
                fields_set, s_one = sem("fields_set"), sem("ones_set")
                scattered = [sem(f"records_scattered{i}") for i in range(2)]
                block = ctx.enter_context(nc.Block())
                attr_cols = attr_in.rearrange("(p c) d -> p c d", p=EP)
                ROUNDS = EC // (2 * HC)

                @block.sync
                def _(sp):
                    def load(n, c0):
                        sp.dma_start(stage[:, n, :, 0:D], attr_cols[:, bass.ds(c0, HC), :]).then_inc(attr_in_stage[n], 16)
                    load(0, 0)
                    load(1, HC)
                    with sp.Fori(1, ROUNDS) as t:
                        for n in range(2):
                            wait_value(sp, scattered[n], t * (16 * HC))
                            load(n, t * (2 * HC) + n * HC)

                @block.vector
                def _(dve):
                    nc.vector.memset(stage[:, :, :, D:RW], 0.0).then_inc(s_one, 1)
                    dve.wait_ge(s_one, 1)
                    nc.vector.memset(stage[:, :, :, R_ONE:R_ONE + 1], 1.0).then_inc(s_one, 1)

                    def fields(n, c0):
                        cols = bass.ds(c0, HC)
                        nc.vector.tensor_copy(stage[:, n, :, R_SRC], slo[:, cols])
                        nc.vector.tensor_copy(stage[:, n, :, R_DST], dlo[:, cols])
                        nc.vector.tensor_copy(stage[:, n, :, R_REL:R_REL + 2 * L], edge_rel[:, cols, :])
                        nc.vector.tensor_copy(row_st[:, n, :], row_idx[:, cols]).then_inc(fields_set, 1)
                    dve.wait_ge(s_one, 2)
                    fields(0, 0)
                    fields(1, HC)
                    with dve.Fori(1, ROUNDS) as t:
                        for n in range(2):
                            wait_value(dve, scattered[n], t * (16 * HC))
                            fields(n, t * (2 * HC) + n * HC)

                @block.gpsimd
                def _(pool):
                    def scatter(n):
                        for j in range(HC):
                            pool.indirect_dma_start(
                                out=records, out_offset=bass.IndirectOffsetOnAxis(ap=row_st[:, n, j:j + 1].bitcast(U32), axis=0),
                                in_=stage[:, n, j, :], in_offset=None).then_inc(scattered[n], 16)

                    with pool.Fori(0, ROUNDS) as t:
                        for n in range(2):
                            wait_value(pool, fields_set, t * 2 + (n + 1))
                            wait_value(pool, attr_in_stage[n], (t + 1) * 16)
                            scatter(n)
                    for n in range(2):
                        pool.wait_ge(scattered[n], ROUNDS * 16 * HC)

        def dense_phase(name, sources, w_parts, finish, steps):
            K = sum(s.shape[2] for s in sources)
            with ExitStack() as ctx:
                stage = sb(name + "_stage", [T, K], F32, ctx)
                zT = sb(name + "_zT", [T, 2, T], F32, ctx)
                psT = ctx.enter_context(nc.psum_tensor(name + "_psT", [T, 2, T], F32))
                psO = ctx.enter_context(nc.psum_tensor(name + "_psO", [T, D], F32))
                sem = lambda n: take_sem(ctx, f"{name}_{n}")
                staged, turned, copied, multiplied, chain = map(sem, ["staged", "turned", "copied", "multiplied", "chain"])
                cuts = [(0, min(K, T))] + ([(T, K - T)] if K > T else [])
                block = ctx.enter_context(nc.Block())

                @block.vector
                def _(dve):
                    ln = Chain(dve, chain)
                    with dve.Fori(0, NT) as t:
                        o = 0
                        for s in sources:
                            w = s.shape[2]
                            last = nc.vector.tensor_scalar(stage[:, o:o + w], s[:, bass.ds(t, 1), :].rearrange("p a d -> p (a d)"),
                                                           1.0, None, ALU.mult)
                            o += w
                        last.then_inc(staged, 1)
                        dve.wait_ge(multiplied, t + 1)
                        ln.base, ln.n = t * steps, 0
                        finish(ln, bass.ds(t, 1), psO[:, :])
                        assert ln.n == steps

                @block.tensor
                def _(pe):
                    with pe.Fori(0, NT) as t:
                        wait_value(pe, staged, t + 1)
                        for i, (o, w) in enumerate(cuts):
                            last = nc.tensor.transpose(psT[0:w, i, :], stage[:, o:o + w], ident[:, :])
                        last.then_inc(turned, 1)
                        wait_value(pe, copied, t + 1)
                        for i, (o, w) in enumerate(cuts):
                            last = nc.tensor.matmul(psO[:, :], zT[0:w, i, :], w_parts[i], start=(i == 0), stop=(i == len(cuts) - 1))
                        last.then_inc(multiplied, 1)

                @block.scalar
                def _(act):
                    with act.Fori(0, NT) as t:
                        act.wait_ge(turned, t + 1)
                        for i, (o, w) in enumerate(cuts):
                            last = nc.scalar.activation(zT[0:w, i, :], psT[0:w, i, :], ACT.Copy)
                        last.then_inc(copied, 1)

        def vector_steps(name, steps, sqrt=None):
            with ExitStack() as ctx:
                chain = take_sem(ctx, name + "_chain")
                root_in = take_sem(ctx, name + "_root_in")
                root_out = take_sem(ctx, name + "_root_out")
                block = ctx.enter_context(nc.Block())

                @block.vector
                def _(dve):
                    steps(Chain(dve, chain), dve, root_in, root_out)

                if sqrt is not None:
                    @block.scalar
                    def _(act):
                        act.wait_ge(root_in, 1)
                        nc.scalar.activation(sqrt[1], sqrt[0], ACT.Sqrt).then_inc(root_out, 1)

        w1a, w1b = sb("w1a", [T, D], F32), sb("w1b", [D, D], F32)
        w2a, w2b = sb("w2a", [T, D], F32), sb("w2b", [D, D], F32)
        wo = sb("wo", [T, L, D], F32)
        wht = sb("wht", [D, L, 4 * D], F32)
        aht = sb("aht", [T, L, 4 * D], F32)
        rows = sb("rows", [T, 2 + 2 * L, D], F32)
        st = sb("st", [T, 6, NT], F32)
        with ExitStack() as ctx:
            s_load = take_sem(ctx, "weights_loaded")
            block = ctx.enter_context(nc.Block())

            @block.sync
            def _(sp):
                loads = [(w1a[:, :], W1[0:T, :]), (w1b[:, :], W1[T:3 * D, :]), (w2a[:, :], W2[0:T, :]), (w2b[:, :], W2[T:3 * D, :]),
                         (wo[:, :, :], W_o.rearrange("l p d -> p l d")),
                         (wht[:, :, 0:2 * D], W_h.rearrange("l p n -> p l n")), (wht[:, :, 2 * D:], W_t.rearrange("l p n -> p l n")),
                         (rows[:, 0, :], b1.partition_broadcast(T)), (rows[:, 1, :], b2.partition_broadcast(T))]
                for l in range(L):
                    loads += [(aht[:, l, 0:2 * D], att_h[l, :, :].rearrange("h d -> (h d)").partition_broadcast(T)),
                              (aht[:, l, 2 * D:], att_t[l, :, :].rearrange("h d -> (h d)").partition_broadcast(T)),
                              (rows[:, 2 + l, :], ln_g[l, :].partition_broadcast(T)),
                              (rows[:, 2 + L + l, :], ln_b[l, :].partition_broadcast(T))]
                for to, frm in loads:
                    sp.dma_start(to, frm).then_inc(s_load, 16)
                sp.wait_ge(s_load, 16 * len(loads))

        def networks(tag, near, attention, spread, w_shape):
            own_sb = ExitStack()

            def sb(name, shape, dt, stack=own_sb):
                return stack.enter_context(nc.sbuf_tensor(f"{tag}_{name}", shape, dt))

            with own_sb:
                with ExitStack() as ctx:
                    parts = sb("parts0", [T, NT, 3, D], BF16, ctx)
                    rest = sb("rest0", [T, NT, D], F32, ctx)
                    acc0 = sb("acc0", [T, NT, 2 * D + 1], F32, ctx)
                    acc1 = sb("acc1", [T, NT, D], F32, ctx)
                    inv_deg = sb("inv_deg", [T, NT], F32, ctx)
                    hid = sb("hid", [T, NT, D], F32, ctx)
                    mean = lambda a: inv_deg[:, :].unsqueeze(2).to_broadcast([T, NT, a.shape[2]])

                    vector_steps(tag + "split_x", lambda ln, dve, i, o: split_steps(nc, ln, parts, x[:, :, :], rest[:, :, :]))
                    near(tag + "near1", parts, "record", acc0)

                    def degrees(ln, dve, i, o):
                        ln.step(nc.vector.tensor_scalar(st[:, 0, :], acc0[:, :, 2 * D], 1.0, None, ALU.max))
                        ln.step(nc.vector.reciprocal(inv_deg[:, :], st[:, 0, :]))
                        a = acc0[:, :, 0:2 * D]
                        ln.step(nc.vector.tensor_tensor(a, a, mean(a), ALU.mult))
                    vector_steps(tag + "degrees", degrees)

                    def relu_out(to, bias):
                        def finish(ln, tile, ps):
                            y = to[:, tile, :].rearrange("p a d -> p (a d)")
                            ln.step(nc.vector.tensor_tensor(y, ps, bias, ALU.add))
                            ln.step(nc.vector.tensor_scalar(y, y, 0.0, None, ALU.max))
                        return finish
                    dense_phase(tag + "layer1", [x, acc0[:, :, 0:D], acc0[:, :, D:2 * D]], [w1a[:, :], w1b[:, :]], relu_out(hid, rows[:, 0, :]), 2)
                    vector_steps(tag + "split_hid", lambda ln, dve, i, o: split_steps(nc, ln, parts, hid[:, :, :], rest[:, :, :]))
                    near(tag + "near2", parts, None, acc1)
                    vector_steps(tag + "mean2", lambda ln, dve, i, o: ln.step(nc.vector.tensor_tensor(acc1[:, :, :], acc1[:, :, :], mean(acc1), ALU.mult)))
                    dense_phase(tag + "layer2", [hid, acc1, acc0[:, :, D:2 * D]], [w2a[:, :], w2b[:, :]], relu_out(rest, rows[:, 1, :]), 2)

                    def first_norm(ln, dve, i, o):
                        ln.step(nc.vector.tensor_tensor(rest[:, :, :], rest[:, :, :], x[:, :, :], ALU.add))
                        layernorm_steps(nc, ln, rest[:, :, :], x[:, :, :], hid[:, :, :], st, i, o, dve)
                    vector_steps(tag + "norm0", first_norm, (st[:, 3, :], st[:, 4, :]))

                def store_nodes(a):
                    with ExitStack() as ctx:
                        s_out = take_sem(ctx, tag + "_out_stored")
                        block = ctx.enter_context(nc.Block())

                        @block.sync
                        def _(sp):
                            sp.dma_start(out[0:(NT - 1) * T, :].rearrange("(t p) d -> p t d", p=T), a[:, 0:NT - 1, :]).then_inc(s_out, 16)
                            sp.dma_start(out[(NT - 1) * T:N, :], a[0:LAST, NT - 1, :]).then_inc(s_out, 16)
                            sp.wait_ge(s_out, 32)
                ent = sb("ent", [T, NT, D], F32)
                h = sb("h", [T, NT, D], F32)
                ah = sb("ah", [T, NT, D], F32)
                Z = sb("Z", [T, NT, 2 * D], F32)
                acc = sb("acc", [T, NT, 2 * D + 2], F32)
                parts = sb("parts", [T, NT, 3, 2 * D], BF16)
                w_edge = sb("w_edge", w_shape, F32)
                score4 = sb("score4", [T, NT, 4], F32)
                rest2 = sb("rest2", [T, NT, H], F32)
                pick_src = sb("pick_src", [T, NT, 3, H], BF16)
                pick_dst = sb("pick_dst", [T, NT, 3, H], BF16)
                norm = sb("norm", [T, NT, H], F32)

                vector_steps(tag + "ent", lambda ln, dve, i, o: ln.step(nc.vector.tensor_copy(ent[:, :, :], x[:, :, :])))
                for l in range(L):
                    nm = f"l{l}"

                    def layer_norm(ln, dve, i, o):
                        layernorm_steps(nc, ln, ent[:, :, :], h[:, :, :], ah[:, :, :], st, i, o, dve, rows[:, 2 + l, :], rows[:, 2 + L + l, :])
                        ln.step(nc.vector.tensor_scalar(ah[:, :, :], h[:, :, :], ALPHA, None, ALU.mult))
                    vector_steps(tag + nm + "_norm", layer_norm, (st[:, 3, :], st[:, 4, :]))
                    score_phase(tag + nm + "_score", h, NT, T, wht[:, l, :], aht[:, l, :], score4)

                    def split_scores(ln, dve, i, o):
                        split_steps(nc, ln, pick_src, score4[:, :, 0:2], rest2[:, :, :])
                        split_steps(nc, ln, pick_dst, score4[:, :, 2:4], rest2[:, :, :])
                    vector_steps(tag + nm + "_split_scores", split_scores)

                    attention(tag + nm, l, pick_src, pick_dst, w_edge, rest2)

                    vector_steps(tag + nm + "_split_h", lambda ln, dve, i, o: split_steps(nc, ln, parts[:, :, :, 0:D], h[:, :, :], Z[:, :, 0:D]))
                    for it in range(POW_ITER):
                        first = it == 0
                        spread(tag + f"{nm}_spread{it}", parts[:, :, :, 0:D] if first else parts, first, w_edge,
                               acc if first else acc[:, :, 0:2 * D])

                        def mix(ln, dve, i, o):
                            if first:
                                ln.step(nc.vector.tensor_scalar(norm[:, :, :], acc[:, :, 2 * D:2 * D + 2], 1e-30, None, ALU.max))
                                ln.step(nc.vector.reciprocal(norm[:, :, :], norm[:, :, :]))
                                ln.step(nc.vector.tensor_scalar(norm[:, :, :], norm[:, :, :], 1.0 - ALPHA, None, ALU.mult))
                            for k in range(H):
                                s = slice(k * D, (k + 1) * D)
                                ln.step(nc.vector.tensor_tensor(Z[:, :, s], acc[:, :, s], norm[:, :, k:k + 1].to_broadcast([T, NT, D]), ALU.mult))
                                ln.step(nc.vector.tensor_tensor(Z[:, :, s], Z[:, :, s], ah[:, :, :], ALU.add))
                            if it < POW_ITER - 1:
                                split_steps(nc, ln, parts, Z[:, :, :], acc[:, :, 0:2 * D])
                        vector_steps(tag + f"{nm}_mix{it}", mix)

                    def residual(ln, tile, ps):
                        y = ent[:, tile, :].rearrange("p a d -> p (a d)")
                        ln.step(nc.vector.tensor_tensor(y, y, ps, ALU.add))
                    dense_phase(tag + nm + "_conv", [Z], [wo[:, l, :]], residual, 1)

                def last_norm(ln, dve, i, o):
                    ln.step(nc.vector.tensor_tensor(ent[:, :, :], ent[:, :, :], x[:, :, :], ALU.add))
                    layernorm_steps(nc, ln, ent[:, :, :], h[:, :, :], ah[:, :, :], st, i, o, dve)
                vector_steps(tag + "norm_last", last_norm, (st[:, 3, :], st[:, 4, :]))
                store_nodes(h)

        def general_path():
            gstack = ExitStack()

            def sb(name, shape, dt, stack=gstack):
                return stack.enter_context(nc.sbuf_tensor("g_" + name, shape, dt))

            with gstack:
                src_lo = sb("src_lo", [T, NCH], F32)
                dst_lo = sb("dst_lo", [T, NCH], F32)
                s_rel = sb("s_rel", [T, NCH, 2 * L], F32)
                src_tile = sb("src_tile", [1, NCH], I32)
                dst_tile = sb("dst_tile", [1, NCH], I32)
                shifted = sb("shifted", [T, NCH, H], F32)
                least = sb("least", [T, 4], F32)
                top_of = sb("top_of", [T, NT, H], F32)

                with ExitStack() as c2:
                    iota_c = sb("iota_c", [NT, NCH], F32, c2)
                    passed = sb("passed", [NT, NCH], F32, c2)
                    rows_passed = sb("rows_passed", [NT, NCH], F32, c2)
                    kf = sb("kf", [1, 2, NCH], F32, c2)
                    psK = c2.enter_context(nc.psum_tensor("psK", [1, 3, 512], F32))
                    psR = c2.enter_context(nc.psum_tensor("psR", [1, 3, 512], F32))
                    sem = lambda n: take_sem(c2, n)
                    chain, compared, summed, s_iota = map(sem, ["chunk_chain", "ends_passed", "chunk_keys", "iota_set"])
                    block = c2.enter_context(nc.Block())
                    spans = [(i * 512, min(512, NCH - i * 512)) for i in range(-(-NCH // 512))]

                    @block.gpsimd
                    def _(pool):
                        nc.gpsimd.iota(iota_c[:, :], [[1, NCH]], base=0, channel_multiplier=0,
                                       allow_small_or_imprecise_dtypes=True).then_inc(s_iota, 1)

                    @block.tensor
                    def _(pe):
                        pe.wait_ge(compared, 1)
                        for i, (o, w) in enumerate(spans):
                            nc.tensor.matmul(psK[:, i, 0:w], ones[0:NT, 0:1], passed[:, o:o + w], start=True, stop=True)
                            last = nc.tensor.matmul(psR[:, i, 0:w], ones[0:NT, 0:1], rows_passed[:, o:o + w], start=True, stop=True)
                        last.then_inc(summed, 1)

                    @block.vector
                    def _(dve):
                        ln = Chain(dve, chain)
                        dve.wait_ge(s_iota, 1)
                        ln.step(nc.vector.tensor_scalar(passed[:, :], iota_c[:, :], block_end[:, 0:1], None, ALU.is_ge))
                        for b in range(1, NT):
                            ln.step(nc.vector.scalar_tensor_tensor(out=passed[:, :], in0=iota_c[:, :], scalar=block_end[:, b:b + 1],
                                                                   in1=passed[:, :], op0=ALU.is_ge, op1=ALU.add))
                        nc.vector.tensor_scalar(rows_passed[:, :], iota_c[:, :], block_end[:, NT - 1:NT], None, ALU.is_ge).then_inc(compared, 1)
                        dve.wait_ge(summed, 1)
                        for i, (o, w) in enumerate(spans):
                            nc.vector.tensor_copy(kf[:, 0, o:o + w], psK[:, i, 0:w])
                            last = nc.vector.tensor_copy(kf[:, 1, o:o + w], psR[:, i, 0:w])
                        ln.step(last)
                        nc.vector.scalar_tensor_tensor(out=dst_tile[:, :], in0=kf[:, 1, :], scalar=-float(NT), in1=kf[:, 0, :],
                                                       op0=ALU.mult, op1=ALU.add)
                        nc.vector.tensor_scalar(src_tile[:, :], kf[:, 1, :], float(NT - 1), None, ALU.min)

                with ExitStack() as ctx:
                    rec = sb("rec", [T, 2, GC, RW], F32, ctx)
                    mark = sb("mark", [T, 2, 2, GC, T], BF16, ctx)
                    turn = sb("turn", [T, 2, 2, GC * T], BF16, ctx)
                    psT = ctx.enter_context(nc.psum_tensor("psTurn", [T, 2, 2, GC * T], BF16))
                    sem = lambda n: take_sem(ctx, n)
                    loaded = [sem(f"rec_loaded{i}") for i in range(2)]
                    stored = [sem(f"turned_stored{i}") for i in range(2)]
                    kept, marked, turned, copied = map(sem, ["places_kept", "slots_marked", "marks_turned", "turned_copied"])
                    block = ctx.enter_context(nc.Block())

                    def rounds(eng, body):
                        body(0, True)
                        with eng.Fori(1, NG // 2) as t:
                            body(t, False)

                    @block.sync
                    def _(sp):
                        def body(t, first):
                            for n in range(2):
                                if not first:
                                    wait_value(sp, kept, t * 2 + (n - 1))
                                sp.dma_start(rec[:, n, :, :].rearrange("p c w -> p (c w)"),
                                             rec_groups[bass.ds(t * 2 + n, 1), :, :].rearrange("a p w -> (a p) w")).then_inc(loaded[n], 16)
                        rounds(sp, body)

                    @block.vector
                    def _(dve):
                        def body(t, first):
                            for n in range(2):
                                cols = bass.ds((t * 2 + n) * GC, GC)
                                wait_value(dve, loaded[n], t * 16 + 16)
                                nc.vector.tensor_copy(src_lo[:, cols], rec[:, n, :, R_SRC])
                                nc.vector.tensor_copy(dst_lo[:, cols], rec[:, n, :, R_DST])
                                if not first:
                                    wait_value(dve, turned, t * 2 + (n - 1))
                                for k, r in enumerate((R_SRC, R_DST)):
                                    nc.vector.tensor_tensor(mark[:, n, k, :, :], iota1[:, :].unsqueeze(1).to_broadcast([T, GC, T]),
                                                            rec[:, n, :, r:r + 1].to_broadcast([T, GC, T]), ALU.is_equal).then_inc(marked, 1)
                                nc.vector.tensor_copy(s_rel[:, cols, :], rec[:, n, :, R_REL:R_REL + 2 * L]).then_inc(kept, 1)
                        rounds(dve, body)

                    @block.tensor
                    def _(pe):
                        def body(t, first):
                            for n in range(2):
                                wait_value(pe, marked, t * 4 + (2 * n + 2))
                                if not first:
                                    wait_value(pe, copied, t * 4 + (2 * n - 2))
                                for k in range(2):
                                    for j in range(GC):
                                        last = nc.tensor.transpose(psT[:, n, k, j * T:(j + 1) * T], mark[:, n, k, j, :], identb[:, :])
                                last.then_inc(turned, 1)
                        rounds(pe, body)

                    @block.scalar
                    def _(act):
                        def body(t, first):
                            for n in range(2):
                                wait_value(act, turned, t * 2 + (n + 1))
                                if not first:
                                    wait_value(act, stored[n], t * 32)
                                for k in range(2):
                                    nc.scalar.activation(turn[:, n, k, :], psT[:, n, k, :], ACT.Copy).then_inc(copied, 1)
                                wait_value(act, copied, t * 4 + (2 * n + 2))
                                for k in range(2):
                                    act.dma_start(onehots[k, bass.ds(t * 2 + n, 1), :, :].rearrange("a p w -> (a p) w"),
                                                  turn[:, n, k, :]).then_inc(stored[n], 16)
                        rounds(act, body)
                        for n in range(2):
                            act.wait_ge(stored[n], NG * 16)

                ROUNDS = NCH // (2 * GC)

                def peeled(eng, body):
                    body(0, True, False)
                    with eng.Fori(1, ROUNDS - 1) as t:
                        body(t, False, False)
                    body(ROUNDS - 1, False, True)

                def tile_of(eng, tiles, c):
                    return eng.value_load(tiles[0:1, bass.ds(c, 1)], min_val=0, max_val=NT - 1)

                def spread_pass(name, turned, g_tiles, F, table, lo, s_tiles, weights, extra, acc):
                    GW = F if weights is None else 2 * D
                    XW = {None: 0, "record": D + 1, "weight": 2}[extra]
                    AW = 128 if GW + XW <= 128 else 256
                    with ExitStack() as ctx:
                        ot = sb(name + "_ot", [T, 2, GC, T], BF16, ctx)
                        gw = sb(name + "_gw", [T, 2, 4, GW], F32, ctx)
                        oh = sb(name + "_oh", [T, 2, 4, T], F32, ctx)
                        places = sb(name + "_places", [T, 2, 4], F32, ctx)
                        placed4 = take_sem(ctx, name + "_places_set")
                        rec = sb(name + "_rec", [T, 2, GC, RW], F32, ctx) if extra == "record" else None
                        gps = ctx.enter_context(nc.psum_tensor(name + "_gps", [T, 2, 4, 128], F32))
                        aps = ctx.enter_context(nc.psum_tensor(name + "_aps", [T, 2, 4, AW], F32))
                        sem = lambda n: take_sem(ctx, f"{name}_{n}")
                        ot_loaded = [sem(f"ot_loaded{i}") for i in range(2)]
                        rec_loaded = [sem(f"rec_loaded{i}") for i in range(2)]
                        gathered, weighted, marked, summed, added, cleared = map(
                            sem, ["gathered", "weighted", "marked", "summed", "added", "cleared"])
                        block = ctx.enter_context(nc.Block())

                        @block.sync
                        def _(sp):
                            def body(t, first, last):
                                for n in range(2):
                                    g = bass.ds(t * 2 + n, 1)
                                    if not first:
                                        sp.wait_ge(gathered, t * 4 + (2 * n - 2))
                                    sp.dma_start(ot[:, n, :, :].rearrange("p c e -> p (c e)"),
                                                 onehots[turned, g, :, :].rearrange("a p w -> (a p) w")).then_inc(ot_loaded[n], 16)
                                    if rec is not None:
                                        if not first:
                                            sp.wait_ge(summed, t * 4 + (2 * n - 2))
                                        sp.dma_start(rec[:, n, :, :].rearrange("p c w -> p (c w)"),
                                                     rec_groups[g, :, :].rearrange("a p w -> (a p) w")).then_inc(rec_loaded[n], 16)
                            peeled(sp, body)

                        @block.gpsimd
                        def _(pool):
                            def marking(t, first, last):
                                for k in range(4):
                                    if not (first and k < 2):
                                        wait_value(pool, summed, t * 4 + (k - 1))
                                    nc.gpsimd.tensor_copy(places[:, k % 2, :], lo[:, bass.ds(t * 16 + 4 * k, 4)]).then_inc(placed4, 1)
                                    wait_value(pool, placed4, t * 4 + (k + 1))
                                    for j in range(4):
                                        last_ = nc.gpsimd.tensor_scalar(oh[:, k % 2, j, :], iota1[:, :], places[:, k % 2, j:j + 1], None,
                                                                        ALU.is_equal)
                                    last_.then_inc(marked, 1)
                            peeled(pool, marking)

                        @block.tensor
                        def _(pe):
                            def gather(t, k, first):
                                n, j0 = k // 2, 4 * (k % 2)
                                if k % 2 == 0:
                                    pe.wait_ge(ot_loaded[n], t * 16 + 16)
                                if not (first and k < 2):
                                    pe.wait_ge(weighted, t * 4 + (k - 1))
                                for j in range(4):
                                    tile = tile_of(pe, g_tiles, t * 16 + (4 * k + j))
                                    for part in range(3):
                                        last = nc.tensor.matmul(gps[:, k % 2, j, 0:F], ot[:, n, j0 + j, :],
                                                                table[:, bass.ds(tile, 1), part, :].rearrange("p a d -> p (a d)"),
                                                                start=(part == 0), stop=(part == 2), skip_group_check=True)
                                last.then_inc(gathered, 1)

                            def add_up(t, k, first):
                                n, j0 = k // 2, 4 * (k % 2)
                                pe.wait_ge(weighted, t * 4 + (k + 1))
                                pe.wait_ge(marked, t * 4 + (k + 1))
                                if rec is not None and k % 2 == 0:
                                    pe.wait_ge(rec_loaded[n], t * 16 + 16)
                                if not (first and k < 2):
                                    pe.wait_ge(added, t * 16 + 4 * (k - 1))
                                for j in range(4):
                                    w = oh[:, k % 2, j, :]
                                    last = nc.tensor.matmul(aps[:, k % 2, j, 0:GW], w, gw[:, k % 2, j, :], start=True, stop=True,
                                                            skip_group_check=True)
                                    if extra == "record":
                                        last = nc.tensor.matmul(aps[:, k % 2, j, GW:GW + XW], w, rec[:, n, j0 + j, 0:XW],
                                                                start=True, stop=True, skip_group_check=True)
                                    if extra == "weight":
                                        last = nc.tensor.matmul(aps[:, k % 2, j, GW:GW + XW], w,
                                                                weights[:, bass.ds(t * 16 + (4 * k + j), 1), :].rearrange("p a h -> p (a h)"),
                                                                start=True, stop=True, skip_group_check=True)
                                last.then_inc(summed, 1)

                            def body(t, first, last):
                                for k in range(4):
                                    if k < 3:
                                        gather(t, k + 1, first)
                                    elif not last:
                                        gather(t + 1, 0, False)
                                    add_up(t, k, first)
                            gather(0, 0, True)
                            peeled(pe, body)

                        @block.vector
                        def _(dve):
                            nc.vector.memset(acc[:, :, :], 0.0).then_inc(cleared, 1)
                            dve.wait_ge(cleared, 1)

                            def weigh(t, k, first):
                                dve.wait_ge(gathered, t * 4 + (k + 1))
                                if not (first and k < 2):
                                    dve.wait_ge(summed, t * 4 + (k - 1))
                                g = gps[:, k % 2, :, 0:F]
                                if weights is None:
                                    nc.vector.tensor_scalar(gw[:, k % 2, :, :], g, 1.0, None, ALU.mult).then_inc(weighted, 1)
                                elif F == D:
                                    w = weights[:, bass.ds(t * 16 + 4 * k, 4), :]
                                    for h in range(H):
                                        last = nc.vector.tensor_tensor(gw[:, k % 2, :, h * D:(h + 1) * D], g,
                                                                       w[:, :, h:h + 1].to_broadcast([T, 4, D]), ALU.mult)
                                    last.then_inc(weighted, 1)
                                else:
                                    w = weights[:, bass.ds(t * 16 + 4 * k, 4), :].rearrange("p c h -> p (c h)")
                                    nc.vector.tensor_tensor(gw[:, k % 2, :, :].rearrange("p c (h d) -> p (c h) d", h=H),
                                                            gps[:, k % 2, :, :].rearrange("p c (h d) -> p (c h) d", h=H),
                                                            w.unsqueeze(2).to_broadcast([T, 4 * H, D]), ALU.mult).then_inc(weighted, 1)

                            def add(t, k, first):
                                dve.wait_ge(summed, t * 4 + (k + 1))
                                for j in range(4):
                                    tile = tile_of(dve, s_tiles, t * 16 + (4 * k + j))
                                    a = acc[:, bass.ds(tile, 1), :].rearrange("p a w -> p (a w)")
                                    if not (first and k == j == 0):
                                        dve.wait_ge(added, t * 16 + (4 * k + j))
                                    nc.vector.tensor_tensor(a, a, aps[:, k % 2, j, 0:GW + XW], ALU.add).then_inc(added, 1)

                            def body(t, first, last):
                                for k in range(4):
                                    if k < 3:
                                        weigh(t, k + 1, first)
                                    elif not last:
                                        weigh(t + 1, 0, False)
                                    add(t, k, first)
                            weigh(0, 0, True)
                            peeled(dve, body)

                def pick_pass(name, sides, finish):
                    NS = len(sides)
                    with ExitStack() as ctx:
                        ot = sb(name + "_ot", [T, 2, NS, GC, T], BF16, ctx)
                        val = sb(name + "_val", [T, 2, GC, H], F32, ctx)
                        ps = ctx.enter_context(nc.psum_tensor(name + "_ps", [T, 2, 512], F32))
                        sem = lambda n: take_sem(ctx, f"{name}_{n}")
                        loaded = [sem(f"loaded{i}") for i in range(2)]
                        picked, taken, chain, ready = map(sem, ["picked", "taken", "chain", "ready"])
                        block = ctx.enter_context(nc.Block())

                        def groups(eng, body):
                            body(0, True)
                            with eng.Fori(1, ROUNDS) as t:
                                body(t, False)

                        @block.sync
                        def _(sp):
                            def body(t, first):
                                for n in range(2):
                                    if not first:
                                        sp.wait_ge(picked, t * 2 + (n - 1))
                                    for i, (turned, _, _) in enumerate(sides):
                                        sp.dma_start(ot[:, n, i, :, :].rearrange("p c e -> p (c e)"),
                                                     onehots[turned, bass.ds(t * 2 + n, 1), :, :].rearrange("a p w -> (a p) w")).then_inc(loaded[n], 16)
                            groups(sp, body)

                        @block.tensor
                        def _(pe):
                            def body(t, first):
                                for n in range(2):
                                    pe.wait_ge(loaded[n], t * (16 * NS) + 16 * NS)
                                    if not first:
                                        pe.wait_ge(taken, t * 2 + (n - 1))
                                    for j in range(GC):
                                        for i, (_, tiles, table) in enumerate(sides):
                                            tile = tile_of(pe, tiles, t * (2 * GC) + (n * GC + j))
                                            last = nc.tensor.matmul(ps[:, n, (j * NS + i) * 6:(j * NS + i) * 6 + 6], ot[:, n, i, j, :],
                                                                    table[:, bass.ds(tile, 1), :, :].rearrange("p a k h -> p (a k h)"),
                                                                    start=True, stop=True, skip_group_check=True)
                                    last.then_inc(picked, 1)
                            groups(pe, body)

                        @block.vector
                        def _(dve):
                            def body(t, first):
                                for n in range(2):
                                    dve.wait_ge(picked, t * 2 + (n + 1))
                                    nc.vector.tensor_reduce(val[:, n, :, :], ps[:, n, 0:GC * NS * 6].rearrange("p (c k h) -> p c h k", c=GC, h=H),
                                                            AX.X, ALU.add).then_inc(taken, 1)
                                    dve.wait_ge(taken, t * 2 + (n + 1))
                                    finish(dve, val[:, n, :, :], bass.ds(t * (2 * GC) + n * GC, GC), chain, t * 2 + (n + 1))
                            groups(dve, body)

                def max_pass(name, shifted, top_of):
                    with ExitStack() as ctx:
                        oh = sb(name + "_oh", [T, 2, 4, T], F32, ctx)
                        places = sb(name + "_places", [T, 2, 4], F32, ctx)
                        placed4 = take_sem(ctx, name + "_places_set")
                        diag = sb(name + "_diag", [T, 2, 4, H, T], F32, ctx)
                        best = sb(name + "_best", [T, 2, 4, H], F32, ctx)
                        aps = ctx.enter_context(nc.psum_tensor(name + "_aps", [T, 2, 4, H * T], F32))
                        sem = lambda n: take_sem(ctx, f"{name}_{n}")
                        marked, spread, placed, reduced, cleared, noted = map(sem, ["marked", "spread", "placed", "reduced", "cleared", "noted"])
                        block = ctx.enter_context(nc.Block())

                        @block.gpsimd
                        def _(pool):
                            def marking(t, first, last):
                                for k in range(4):
                                    if not (first and k < 2):
                                        wait_value(pool, placed, t * 4 + (k - 1))
                                    nc.gpsimd.tensor_copy(places[:, k % 2, :], src_lo[:, bass.ds(t * 16 + 4 * k, 4)]).then_inc(placed4, 1)
                                    wait_value(pool, placed4, t * 4 + (k + 1))
                                    for j in range(4):
                                        last_ = nc.gpsimd.tensor_scalar(oh[:, k % 2, j, :], iota1[:, :], places[:, k % 2, j:j + 1], None,
                                                                        ALU.is_equal)
                                    last_.then_inc(marked, 1)
                            peeled(pool, marking)

                        @block.scalar
                        def _(act):
                            def spreading(t, first, last):
                                for k in range(4):
                                    if not (first and k < 2):
                                        wait_value(act, placed, t * 4 + (k - 1))
                                    for j in range(4):
                                        for h in range(H):
                                            last_ = nc.scalar.activation(
                                                diag[:, k % 2, j, h, :], ident[:, :], ACT.Copy,
                                                scale=shifted[:, bass.ds(t * 16 + (4 * k + j), 1), h:h + 1].rearrange("p a h -> p (a h)"))
                                    last_.then_inc(spread, 1)
                            peeled(act, spreading)

                        @block.tensor
                        def _(pe):
                            def place(t, first, last):
                                for k in range(4):
                                    pe.wait_ge(marked, t * 4 + (k + 1))
                                    pe.wait_ge(spread, t * 4 + (k + 1))
                                    if not (first and k < 2):
                                        pe.wait_ge(reduced, t * 4 + (k - 1))
                                    for j in range(4):
                                        last_ = nc.tensor.matmul(aps[:, k % 2, j, :], oh[:, k % 2, j, :],
                                                                 diag[:, k % 2, j, :, :].rearrange("p h e -> p (h e)"), start=True, stop=True,
                                                                 skip_group_check=True)
                                    last_.then_inc(placed, 1)
                            peeled(pe, place)

                        @block.vector
                        def _(dve):
                            nc.vector.memset(top_of[:, :, :], 0.0).then_inc(cleared, 1)
                            dve.wait_ge(cleared, 1)

                            def largest(t, first, last):
                                for k in range(4):
                                    dve.wait_ge(placed, t * 4 + (k + 1))
                                    nc.vector.tensor_reduce(best[:, k % 2, :, :].rearrange("p c h -> p (c h)"),
                                                            aps[:, k % 2, :, :].rearrange("p c (h e) -> p (c h) e", h=H), AX.X, ALU.max).then_inc(reduced, 1)
                                    dve.wait_ge(reduced, t * 4 + (k + 1))
                                    for j in range(4):
                                        tile = tile_of(dve, src_tile, t * 16 + (4 * k + j))
                                        m = top_of[:, bass.ds(tile, 1), :].rearrange("p a h -> p (a h)")
                                        if not (first and k == j == 0):
                                            dve.wait_ge(noted, t * 16 + (4 * k + j))
                                        nc.vector.tensor_tensor(m, m, best[:, k % 2, j, :], ALU.max).then_inc(noted, 1)
                            peeled(dve, largest)


                def near(name, parts, extra, acc):
                    spread_pass(name, 0, src_tile, D, parts, dst_lo, dst_tile, None, extra, acc)

                def spread(name, parts, first, w_edge, acc):
                    spread_pass(name, 1, dst_tile, D if first else 2 * D, parts, src_lo, src_tile, w_edge,
                                "weight" if first else None, acc)

                def attention(nm, l, pick_src, pick_dst, w_edge, rest2):
                    def edge_scores(dve, val, cols, chain, n):
                        nc.vector.tensor_tensor(val, val, s_rel[:, cols, 2 * l:2 * l + 2], ALU.add).then_inc(chain, 1)
                        dve.wait_ge(chain, n)
                        nc.vector.scalar_tensor_tensor(out=w_edge[:, cols, :], in0=val, scalar=0.01, in1=val, op0=ALU.mult, op1=ALU.max)
                    pick_pass(nm + "_edge", [(0, src_tile, pick_src), (1, dst_tile, pick_dst)], edge_scores)

                    with ExitStack() as ctx:
                        s_least, s_all = take_sem(ctx, nm + "_least"), take_sem(ctx, nm + "_all_least")
                        chain = take_sem(ctx, nm + "_least_chain")
                        block = ctx.enter_context(nc.Block())

                        @block.vector
                        def _(dve):
                            ln = Chain(dve, chain)
                            ln.step(nc.vector.tensor_reduce(least[:, 0:1], w_edge[:, :, :].rearrange("p c h -> p (c h)"), AX.X, ALU.min))
                            nc.vector.tensor_scalar(least[:, 1:2], least[:, 0:1], -1.0, None, ALU.mult).then_inc(s_least, 1)
                            dve.wait_ge(s_all, 1)
                            ln.step(nc.vector.tensor_scalar(least[:, 3:4], least[:, 2:3], 1.0, None, ALU.add))
                            nc.vector.tensor_scalar(shifted[:, :, :], w_edge[:, :, :], least[:, 3:4], None, ALU.add)

                        @block.gpsimd
                        def _(pool):
                            pool.wait_ge(s_least, 1)
                            nc.gpsimd.partition_all_reduce(least[:, 2:3], least[:, 1:2], T, bass.bass_isa.ReduceOp.max).then_inc(s_all, 1)
                    max_pass(nm + "_max", shifted, top_of)

                    def unshift(ln, dve, i, o):
                        ln.step(nc.vector.tensor_scalar(top_of[:, :, :], top_of[:, :, :], least[:, 3:4], None, ALU.subtract))
                        split_steps(nc, ln, pick_src, top_of[:, :, :], rest2[:, :, :])
                    vector_steps(nm + "_unshift", unshift)

                    def below_top(dve, val, cols, chain, n):
                        nc.vector.tensor_tensor(w_edge[:, cols, :], w_edge[:, cols, :], val, ALU.subtract)
                    pick_pass(nm + "_under", [(0, src_tile, pick_src)], below_top)
                    with ExitStack() as ctx:
                        block = ctx.enter_context(nc.Block())

                        @block.scalar
                        def _(act):
                            nc.scalar.activation(w_edge[:, :, :], w_edge[:, :, :], ACT.Exp)


                networks("g_", near, attention, spread, [T, NCH, H])


        def fast_path():
            SC = NT * BCH
            UNITS = [4] * (SC // 4) + ([SC % 4] if SC % 4 else [])
            NU = len(UNITS)
            RING = 5
            slot = lambda i: i % 4 if i < NU - 1 else 4
            held = lambda i: (5 if i < 4 else 4) if i < NU - 1 else NU
            rec_tiles = records[0:NT * SC * T, :].rearrange("(s p c) w -> s p (c w)", p=T, c=SC)
            OST, ODT, OS, OD = range(4)

            def after(eng, sem, t, per, off, apart=False):
                if isinstance(t, int):
                    if t * per + off > 0:
                        eng.wait_ge(sem, t * per + off)
                elif apart:
                    wait_value(eng, sem, t * per + off)
                else:
                    eng.wait_ge(sem, t * per + off)

            def tile_pairs(eng, body):
                body(0, (0, 1))
                with eng.Fori(1, NT // 2) as t:
                    body(t, (0, 1))
                body(NT // 2, (0,))

            def skewed(eng, per, stages):
                most, least_ = max(a for a, _ in stages), min(a for a, _ in stages)

                def step(t, k, end):
                    for lead, f in stages:
                        kk = k + lead
                        if (isinstance(t, int) and t == 0 and kk < 0) or (end is not None and kk >= end):
                            continue
                        over, kk = divmod(kk, 2 * per)
                        f(t + over if over else t, kk // per, kk % per)
                for k in range(-most, 0):
                    step(0, k, None)
                for k in range(2 * per):
                    step(0, k, None)
                with eng.Fori(1, NT // 2) as t:
                    for k in range(2 * per):
                        step(t, k, None)
                for k in range(per - least_):
                    step(NT // 2, k, per)

            s_rel = sb("fs_rel", [T, NT, SC, 2 * L], F32)
            MU = [8] * (SC // 8) + [SC % 8]
            NM = len(MU)
            with ExitStack() as ctx:
                iotab = sb("iotab", [T, T], BF16, ctx)
                rec = sb("f_rec", [T, 2, SC, RW], F32, ctx)
                ident8 = sb("ident8", [T, T], F8, ctx)
                out8 = sb("f_out8", [T, 2, 4, SC * T], F8, ctx)
                psT = ctx.enter_context(nc.psum_tensor("f_psT", [T, 2, 2, 8 * T], F32))
                sem = lambda n: take_sem(ctx, "f_" + n)
                loaded = [sem(f"rec_loaded{i}") for i in range(2)]
                stored = [sem(f"onehots_stored{i}") for i in range(2)]
                marked, turned, copied, kept, s_iota = map(sem, ["marked", "turned", "copied", "kept", "iota"])
                block = ctx.enter_context(nc.Block())

                @block.sync
                def _(sp):
                    def body(t, tiles):
                        for n in tiles:
                            after(sp, kept, t, 2, n - 1, True)
                            sp.dma_start(rec[:, n, :, :].rearrange("p c w -> p (c w)"),
                                         rec_tiles[bass.ds(t * 2 + n, 1), :, :].rearrange("a p w -> (a p) w")).then_inc(loaded[n], 16)
                    tile_pairs(sp, body)

                @block.vector
                def _(dve):
                    nc.vector.tensor_copy(ident8[:, :], identb[:, :], saturate=False).then_inc(s_iota, 1)
                    nc.vector.tensor_copy(iotab[:, :], iota1[:, :]).then_inc(s_iota, 1)
                    dve.wait_ge(s_iota, 2)

                    def body(t, tiles):
                        for n in tiles:
                            after(dve, loaded[n], t, 16, 16, True)
                            after(dve, stored[n], t, 64, 0, True)
                            for i, m in enumerate(MU):
                                for c in range(8 * i, 8 * i + m):
                                    for k, r in enumerate((R_SRC, R_DST)):
                                        last = nc.vector.tensor_scalar(out8[:, n, 2 + k, c * T:(c + 1) * T], iotab[:, :],
                                                                       rec[:, n, c, r:r + 1], None, ALU.is_equal, saturate=False)
                                last.then_inc(marked, 1)
                            nc.vector.tensor_copy(s_rel[:, bass.ds(t * 2 + n, 1), :, :].rearrange("p a c k -> p (a c) k"),
                                                  rec[:, n, :, R_REL:R_REL + 2 * L]).then_inc(kept, 1)
                    tile_pairs(dve, body)

                @block.tensor
                def _(pe):
                    def body(t, tiles):
                        for n in tiles:
                            for i, m in enumerate(MU):
                                u = NM * n + i
                                after(pe, marked, t, 2 * NM, u + 1, True)
                                after(pe, copied, t, 2 * NM, u - 1, True)
                                for k in range(2):
                                    for c in range(m):
                                        o = (8 * i + c) * T
                                        last = nc.tensor.matmul(psT[:, u % 2, k, c * T:(c + 1) * T], out8[:, n, 2 + k, o:o + T], ident8[:, :],
                                                                start=True, stop=True, skip_group_check=True)
                                last.then_inc(turned, 1)
                    tile_pairs(pe, body)

                @block.scalar
                def _(act):
                    def body(t, tiles):
                        for n in tiles:
                            after(act, stored[n], t, 64, 0, True)
                            for i, m in enumerate(MU):
                                u = NM * n + i
                                after(act, turned, t, 2 * NM, u + 1, True)
                                for k in range(2):
                                    last = nc.scalar.activation(out8[:, n, k, 8 * i * T:(8 * i + m) * T], psT[:, u % 2, k, 0:m * T], ACT.Copy, saturate=False)
                                last.then_inc(copied, 1)
                            after(act, copied, t, 2 * NM, NM * (n + 1), True)
                            for k in range(4):
                                act.dma_start(onehots8[k, bass.ds(t * 2 + n, 1), :, :].rearrange("a p w -> (a p) w"),
                                              out8[:, n, k, :].bitcast(U8)).then_inc(stored[n], 16)
                    tile_pairs(act, body)
                    act.wait_ge(stored[0], 64 * (NT // 2 + 1))
                    act.wait_ge(stored[1], 64 * (NT // 2))

            def load_onehots(sp, ot, kinds, t, n, loaded):
                for j, k in enumerate(kinds):
                    sp.dma_start(ot[:, n, j, :].bitcast(U8), onehots8[k, bass.ds(t * 2 + n, 1), :, :].rearrange("a p w -> (a p) w")).then_inc(loaded[n], 16)

            def spread_units(name, kinds, F, table, weights, extra, acc, by_target):
                GW = {None: F, "record": 2 * D, "weight": 2 * D + 2, "heads": 2 * D}[extra]
                AW = GW + (1 if extra == "record" else 0)
                with ExitStack() as ctx:
                    ot = sb(name + "_ot", [T, 2, 2, SC * T], F8, ctx)
                    gw = sb(name + "_gw", [T, RING, 4, GW], F32, ctx)
                    rest = sb(name + "_rest", [T, RING, 4, GW], F32, ctx)
                    parts = sb(name + "_parts", [T, RING, 3, 4, GW], BF16, ctx)
                    if by_target:
                        stab = sb(name + "_stab", [T, 2, 3, D], BF16, ctx)
                    if extra == "record":
                        rec = sb(name + "_rec", [T, 2, SC, RW], F32, ctx)
                        one = sb(name + "_one", [T, 1], BF16, ctx)
                    gps = ctx.enter_context(nc.psum_tensor(name + "_gps", [T, RING, 4, 128], F32))
                    aps = ctx.enter_context(nc.psum_tensor(name + "_aps", [T, 2, 2, 256], F32))
                    sem = lambda n: take_sem(ctx, f"{name}_{n}")
                    loaded = [sem(f"onehots_in{i}") for i in range(2)]
                    rec_in = [sem(f"rec_in{i}") for i in range(2)]
                    staged, gathered, weighted, high, rested, middle, low, summed, added, cleared = map(
                        sem, ["staged", "gathered", "weighted", "high", "rested", "middle", "low", "summed", "added", "cleared"])
                    block = ctx.enter_context(nc.Block())

                    def done(eng, sem, t, n, i, apart=False):
                        after(eng, sem, t, 2 * NU, NU * n + i + 1, apart)

                    def freed(eng, sem, t, n, i, apart=False):
                        after(eng, sem, t, 2 * NU, NU * n + i + 1 - held(i), apart)

                    @block.sync
                    def _(sp):
                        def body(t, tiles):
                            for n in tiles:
                                after(sp, summed, t, 2 * NU, NU * (n - 1), True)
                                load_onehots(sp, ot, kinds, t, n, loaded)
                                if extra == "record":
                                    sp.dma_start(rec[:, n, :, :].rearrange("p c w -> p (c w)"),
                                                 rec_tiles[bass.ds(t * 2 + n, 1), :, :].rearrange("a p w -> (a p) w")).then_inc(rec_in[n], 16)
                        tile_pairs(sp, body)

                    @block.tensor
                    def _(pe):
                        def gather(t, n, i):
                            if i == 0:
                                after(pe, loaded[n], t, 32, 32, True)
                                if by_target:
                                    after(pe, staged, t, 2, n + 1, True)
                            freed(pe, weighted, t, n, i, True)
                            for j in range(UNITS[i]):
                                c = 4 * i + j
                                for part in range(3):
                                    rhs = stab[:, n, part, :] if by_target else table[:, c // BCH, part, :]
                                    last = nc.tensor.matmul(gps[:, slot(i), j, 0:F], ot[:, n, 0, c * T:(c + 1) * T], rhs,
                                                            start=(part == 0), stop=(part == 2), skip_group_check=True)
                            last.then_inc(gathered, 1)

                        def total(t, n, i):
                            done(pe, low, t, n, i, True)
                            if by_target:
                                after(pe, added, t, 2 * NU, NU * n + i - 1, True)
                            elif i == 0:
                                after(pe, added, t, 2, n - 1, True)
                            for j in range(UNITS[i]):
                                c = 4 * i + j
                                w = ot[:, n, 1, c * T:(c + 1) * T]
                                if by_target:
                                    o = aps[:, (NU * n + i) % 2, j // BCH, :]
                                    first, last_ = j % BCH == 0, j % BCH == BCH - 1
                                else:
                                    o = aps[:, n, 0, :]
                                    first, last_ = c == 0, c == SC - 1
                                if extra == "record":
                                    nc.tensor.matmul(o[:, GW:GW + 1], w, one[:, :], start=first, stop=last_, skip_group_check=True)
                                for part in range(3):
                                    last = nc.tensor.matmul(o[:, 0:GW], w, parts[:, slot(i), part, j, :],
                                                            start=first and part == 0 and extra != "record",
                                                            stop=last_ and part == 2, skip_group_check=True)
                            last.then_inc(summed, 1)
                        skewed(pe, NU, [(3, gather), (0, total)])

                    @block.vector
                    def _(dve):
                        if by_target:
                            nc.vector.memset(acc[:, :, :], 0.0).then_inc(cleared, 1)
                            dve.wait_ge(cleared, 1)
                        if extra == "record":
                            nc.vector.memset(one[:, :], 1.0)

                        def weigh(t, n, i):
                            m = UNITS[i]
                            done(dve, gathered, t, n, i)
                            freed(dve, rested, t, n, i)
                            g, o = gps[:, slot(i), 0:m, 0:F], gw[:, slot(i), 0:m, :]
                            if extra == "record":
                                if i == 0:
                                    after(dve, rec_in[n], t, 16, 16)
                                nc.vector.tensor_copy(o[:, :, D:2 * D], rec[:, n, 4 * i:4 * i + m, 0:D])
                            if weights is None:
                                nc.vector.tensor_copy(o[:, :, 0:D], g).then_inc(weighted, 1)
                                return
                            w = weights[:, bass.ds(t * 2 + n, 1), 4 * i:4 * i + m, :].rearrange("p a c h -> p (a c) h")
                            if extra == "weight":
                                nc.vector.tensor_scalar(o[:, :, 2 * D:2 * D + 2], w, 1.0, None, ALU.mult)
                            heads = o[:, :, 0:2 * D].rearrange("p c (h d) -> p c h d", h=H)
                            g = g.unsqueeze(2).to_broadcast([T, m, H, D]) if F == D else g.rearrange("p c (h d) -> p c h d", h=H)
                            nc.vector.tensor_tensor(heads, g, w.unsqueeze(3).to_broadcast([T, m, H, D]), ALU.mult).then_inc(weighted, 1)

                        def stage_table(t, n, i):
                            if i == 0:
                                after(dve, gathered, t, 2 * NU, NU * (n - 1))
                                nc.vector.tensor_scalar(stab[:, n, :, :].rearrange("p k d -> p (k d)"),
                                                        table[:, bass.ds(t * 2 + n, 1), :, :].rearrange("p a k d -> p (a k d)"),
                                                        1.0, None, ALU.mult).then_inc(staged, 1)

                        def lowest(t, n, i):
                            m = UNITS[i]
                            done(dve, middle, t, n, i)
                            nc.vector.tensor_tensor(parts[:, slot(i), 2, 0:m, :], rest[:, slot(i), 0:m, :], parts[:, slot(i), 1, 0:m, :],
                                                    ALU.subtract).then_inc(low, 1)

                        def add(t, n, i):
                            done(dve, summed, t, n, i)
                            if by_target:
                                m = UNITS[i] // BCH
                                after(dve, added, t, 2 * NU, NU * n + i)
                                a = acc[:, 2 * i:2 * i + m, 0:AW]
                                nc.vector.tensor_tensor(a, a, aps[:, (NU * n + i) % 2, 0:m, 0:AW], ALU.add).then_inc(added, 1)
                            elif i == NU - 1:
                                nc.vector.tensor_scalar(acc[:, bass.ds(t * 2 + n, 1), 0:AW].rearrange("p a w -> p (a w)"),
                                                        aps[:, n, 0, 0:AW], 1.0, None, ALU.mult).then_inc(added, 1)

                        def add_last(t, n, i):
                            if by_target or i == NU - 1:
                                add(t, n, i)
                        stages = [(2, weigh), (0, lowest), (-1, add_last)]
                        if by_target:
                            stages = [(8, stage_table)] + stages
                        skewed(dve, NU, stages)

                    @block.scalar
                    def _(act):
                        def highest(t, n, i):
                            m = UNITS[i]
                            done(act, weighted, t, n, i)
                            freed(act, summed, t, n, i)
                            nc.scalar.activation(parts[:, slot(i), 0, 0:m, :], gw[:, slot(i), 0:m, :], ACT.Copy).then_inc(high, 1)

                        def mid(t, n, i):
                            m = UNITS[i]
                            done(act, rested, t, n, i)
                            nc.scalar.activation(parts[:, slot(i), 1, 0:m, :], rest[:, slot(i), 0:m, :], ACT.Copy).then_inc(middle, 1)
                        skewed(act, NU, [(1, highest), (0, mid)])

                    @block.gpsimd
                    def _(pool):
                        def remains(t, n, i):
                            m = UNITS[i]
                            done(pool, high, t, n, i, True)
                            freed(pool, low, t, n, i, True)
                            nc.gpsimd.tensor_tensor(rest[:, slot(i), 0:m, :], gw[:, slot(i), 0:m, :], parts[:, slot(i), 0, 0:m, :],
                                                    ALU.subtract).then_inc(rested, 1)
                        skewed(pool, NU, [(0, remains)])

            def attention(name, l, pick_src, pick_dst, w_edge, rest2):
                AG = 7
                DG = (SC - 4 * AG) // 2
                AS = 2 * DG
                with ExitStack() as ctx:
                    ot = sb(name + "_ot", [T, 2, 3, SC * T], F8, ctx)
                    stab = sb(name + "_stab", [T, 2, 6], BF16, ctx)
                    mtab = sb(name + "_mtab", [T, 2, 3, H], BF16, ctx)
                    val = sb(name + "_val", [T, SC, H], F32, ctx)
                    score = sb(name + "_score", [T, 2, SC, H], F32, ctx)
                    shifted = sb(name + "_shifted", [T, 2, SC, H], F32, ctx)
                    run = sb(name + "_run", [T, 2, 4, H, T], BF16, ctx)
                    run_a = sb(name + "_run_a", [T, 2, 4, H, T], BF16, ctx)
                    prod = sb(name + "_prod", [T, AG, 4, H, T], BF16, ctx)
                    merge = sb(name + "_merge", [T, 7, H, T], BF16, ctx)
                    top1 = sb(name + "_top", [T, 3, H], F32, ctx)
                    under_ = sb(name + "_under", [T, SC, H], F32, ctx)
                    diff = sb(name + "_diff", [T, 2, SC, H], F32, ctx)
                    size = sb(name + "_size", [T, 3, 4 * D], F32, ctx)
                    shift = sb(name + "_shift", [T, 4], F32, ctx)
                    pick_ps = ctx.enter_context(nc.psum_tensor(name + "_pick", [T, 2, 512], F32))
                    under_ps = ctx.enter_context(nc.psum_tensor(name + "_upick", [T, 512], F32))
                    turn_ps = ctx.enter_context(nc.psum_tensor(name + "_turn", [T, H, T], BF16))
                    sem = lambda n: take_sem(ctx, f"{name}_{n}")
                    loaded = [sem(f"onehots_in{i}") for i in range(2)]
                    (staged, picked, taken, scored, scanned, multiplied, folded, halved, merged, turned, topped, undered, below_, expd,
                     s_chain, t_chain, u_chain, setup) = map(
                        sem, ["staged", "picked", "taken", "scored", "scanned", "multiplied", "folded", "halved", "merged", "turned", "topped",
                              "undered", "below", "expd", "s_chain", "t_chain", "u_chain", "setup"])
                    block = ctx.enter_context(nc.Block())
                    HALF = SC // 2

                    @block.sync
                    def _(sp):
                        def body(t, tiles):
                            for n in tiles:
                                for j, (k, used) in enumerate(((ODT, picked), (OS, merged), (OST, undered))):
                                    after(sp, used, t, 2, n - 1, True)
                                    sp.dma_start(ot[:, n, j, :].bitcast(U8),
                                                 onehots8[k, bass.ds(t * 2 + n, 1), :, :].rearrange("a p w -> (a p) w")).then_inc(loaded[n], 16)
                        tile_pairs(sp, body)

                    @block.tensor
                    def _(pe):
                        def pick(t, n, i):
                            after(pe, loaded[n], t, 48, 48, True)
                            after(pe, staged, t, 2, n + 1, True)
                            after(pe, taken, t, 2, n, True)
                            for c in range(SC):
                                o = pick_ps[:, c // HALF, (c % HALF) * 12:(c % HALF) * 12 + 12]
                                nc.tensor.matmul(o[:, 0:6], ot[:, n, 2, c * T:(c + 1) * T], stab[:, n, :], start=True, stop=True,
                                                 skip_group_check=True)
                                last = nc.tensor.matmul(o[:, 6:12], ot[:, n, 0, c * T:(c + 1) * T],
                                                        pick_dst[:, c // BCH, :, :].rearrange("p k h -> p (k h)"), start=True, stop=True,
                                                        skip_group_check=True)
                            last.then_inc(picked, 1)

                        def turn(t, n, i):
                            after(pe, merged, t, 2, n + 1, True)
                            for h in range(H):
                                last = nc.tensor.transpose(turn_ps[:, h, :], merge[:, 6, h, :], identb[:, :])
                            last.then_inc(turned, 1)

                        def pick_top(t, n, i):
                            after(pe, topped, t, 2, n + 1, True)
                            after(pe, below_, t, 2, n, True)
                            for c in range(SC):
                                last = nc.tensor.matmul(under_ps[:, c * 6:c * 6 + 6], ot[:, n, 2, c * T:(c + 1) * T],
                                                        mtab[:, n, :, :].rearrange("p k h -> p (k h)"), start=True, stop=True,
                                                        skip_group_check=True)
                            last.then_inc(undered, 1)
                        skewed(pe, 1, [(-1, turn), (-1, pick_top), (1, pick)])

                    @block.vector
                    def _(dve):
                        ln = Chain(dve, setup)
                        for k, a in enumerate((aht[:, l, :], ar[:, :])):
                            ln.step(nc.vector.tensor_scalar(size[:, k, :], a, -1.0, None, ALU.mult))
                            ln.step(nc.vector.tensor_tensor(size[:, k, :], size[:, k, :], a, ALU.max))
                            ln.step(nc.vector.tensor_reduce(shift[:, k:k + 1], size[:, k, :], AX.X, ALU.add))
                        ln.step(nc.vector.tensor_tensor(shift[:, 2:3], shift[:, 0:1], shift[:, 1:2], ALU.add))
                        ln.step(nc.vector.tensor_scalar(shift[:, 3:4], shift[:, 2:3], 0.01, 1.0, ALU.mult, ALU.add))

                        def get_scores(t, n, i):
                            after(dve, picked, t, 2, n + 1)
                            for b in range(2):
                                last = nc.vector.tensor_reduce(val[:, b * HALF:(b + 1) * HALF, :],
                                                               pick_ps[:, b, 0:HALF * 12].rearrange("p (c k h) -> p c h k", c=HALF, h=H),
                                                               AX.X, ALU.add)
                            last.then_inc(taken, 1)
                            after(dve, taken, t, 2, n + 1)
                            nc.vector.tensor_tensor(val[:, :, :], val[:, :, :],
                                                    s_rel[:, bass.ds(t * 2 + n, 1), :, 2 * l:2 * l + 2].rearrange("p a c h -> p (a c) h"),
                                                    ALU.add).then_inc(s_chain, 1)
                            after(dve, s_chain, t, 4, 2 * n + 1)
                            nc.vector.scalar_tensor_tensor(out=score[:, n, :, :], in0=val[:, :, :], scalar=0.01, in1=val[:, :, :],
                                                           op0=ALU.mult, op1=ALU.max).then_inc(s_chain, 1)
                            after(dve, s_chain, t, 4, 2 * n + 2)
                            nc.vector.tensor_scalar(shifted[:, n, :, :], score[:, n, :, :], shift[:, 3:4], None, ALU.add).then_inc(scored, 1)

                        def scan(t, n, groups):
                            if groups[0] == 0:
                                after(dve, scored, t, 2, n + 1, True)
                            for g in groups:
                                if g >= 2:
                                    after(dve, scanned, t, 2 * DG, DG * n + g - 1, True)
                                for j in range(2):
                                    for h in range(H):
                                        c = 2 * g + j
                                        a, o = run[:, n, (g % 2) * 2 + j, h, :], ot[:, n, 1, c * T:(c + 1) * T]
                                        s = shifted[:, n, c, h:h + 1]
                                        if g < 2:
                                            last = nc.vector.tensor_scalar(a, o, s, None, ALU.mult)
                                        else:
                                            last = nc.vector.scalar_tensor_tensor(out=a, in0=o, scalar=s, in1=a, op0=ALU.mult, op1=ALU.max)
                                last.then_inc(scanned, 1)

                        def fold(t, n, g):
                            after(dve, multiplied, t, 2 * AG, AG * n + g + 1, True)
                            flat = lambda a: a.rearrange("p c h e -> p (c h e)")
                            if g > 1:
                                after(dve, folded, t, 2 * (AG - 1), (AG - 1) * n + g - 1, True)
                            nc.vector.tensor_tensor(flat(run_a[:, n, :, :, :]), flat(prod[:, 0, :, :, :] if g == 1 else run_a[:, n, :, :, :]),
                                                    flat(prod[:, g, :, :, :]), ALU.max).then_inc(folded, 1)

                        def largest(t, n, i):
                            after(dve, scanned, t, 2 * DG, DG * (n + 1))
                            after(dve, folded, t, 2 * (AG - 1), (AG - 1) * (n + 1))
                            flat = lambda a: a.rearrange("p c h e -> p (c h e)")
                            nc.vector.tensor_tensor(flat(merge[:, 0:4, :, :]), flat(run[:, n, :, :, :]), flat(run_a[:, n, :, :, :]),
                                                    ALU.max).then_inc(halved, 1)
                            after(dve, halved, t, 4, 2 * n + 1)
                            nc.vector.tensor_tensor(flat(merge[:, 4:6, :, :]), flat(merge[:, 0:2, :, :]), flat(merge[:, 2:4, :, :]),
                                                    ALU.max).then_inc(halved, 1)
                            after(dve, halved, t, 4, 2 * n + 2)
                            nc.vector.tensor_tensor(flat(merge[:, 6:7, :, :]), flat(merge[:, 4:5, :, :]), flat(merge[:, 5:6, :, :]),
                                                    ALU.max).then_inc(merged, 1)

                        def top(t, n, i):
                            after(dve, turned, t, 2, n + 1)
                            k = 0

                            def then(ins):
                                nonlocal k
                                k += 1
                                ins.then_inc(t_chain, 1)
                                after(dve, t_chain, t, 10, 5 * n + k)
                            then(nc.vector.tensor_reduce(top1[:, 0, :], turn_ps[:, :, :], AX.X, ALU.max))
                            then(nc.vector.tensor_scalar(top1[:, 1, :], top1[:, 0, :], shift[:, 3:4], None, ALU.subtract))
                            then(nc.vector.tensor_copy(mtab[:, n, 0, :], top1[:, 1, :]))
                            then(nc.vector.tensor_tensor(top1[:, 2, :], top1[:, 1, :], mtab[:, n, 0, :], ALU.subtract))
                            then(nc.vector.tensor_copy(mtab[:, n, 1, :], top1[:, 2, :]))
                            nc.vector.tensor_tensor(mtab[:, n, 2, :], top1[:, 2, :], mtab[:, n, 1, :], ALU.subtract).then_inc(topped, 1)

                        def under(t, n, i):
                            after(dve, undered, t, 2, n + 1)
                            after(dve, expd, t, 2, n - 1)
                            nc.vector.tensor_reduce(under_[:, :, :], under_ps[:, 0:SC * 6].rearrange("p (c k h) -> p c h k", c=SC, h=H),
                                                    AX.X, ALU.add).then_inc(u_chain, 1)
                            after(dve, u_chain, t, 2, n + 1)
                            nc.vector.tensor_tensor(diff[:, n, :, :], score[:, n, :, :], under_[:, :, :], ALU.subtract).then_inc(below_, 1)
                        def scan_1(t, n, i):
                            scan(t, n, range(0, 6))
                            fold(t, n, 1)

                        def scan_2(t, n, i):
                            scan(t, n, range(6, 8))
                            fold(t, n, 2)
                            scan(t, n, range(8, 9))
                            fold(t, n, 3)

                        def scan_3(t, n, i):
                            scan(t, n, range(9, DG))
                            for g in range(4, AG):
                                fold(t, n, g)
                        skewed(dve, 1, [(0, scan_1), (-1, top), (0, scan_2), (-1, under), (1, get_scores), (0, scan_3), (0, largest)])

                    @block.scalar
                    def _(act):
                        def stage(t, n, i):
                            after(act, picked, t, 2, n - 1, True)
                            nc.scalar.activation(stab[:, n, :], pick_src[:, bass.ds(t * 2 + n, 1), :, :].rearrange("p a k h -> p (a k h)"),
                                                 ACT.Copy).then_inc(staged, 1)

                        def multiply(t, n, i):
                            after(act, scored, t, 2, n + 1, True)
                            for g in range(AG):
                                after(act, folded, t, 2 * (AG - 1), (AG - 1) * (n - 1) + max(g, 1), True)
                                for j in range(4):
                                    for h in range(H):
                                        c = AS + 4 * g + j
                                        last = nc.scalar.activation(prod[:, g, j, h, :], ot[:, n, 1, c * T:(c + 1) * T], ACT.Copy,
                                                                    scale=shifted[:, n, c, h:h + 1])
                                last.then_inc(multiplied, 1)

                        def weights(t, n, i):
                            after(act, below_, t, 2, n + 1, True)
                            nc.scalar.activation(w_edge[:, bass.ds(t * 2 + n, 1), :, :].rearrange("p a c h -> p (a c h)"),
                                                 diff[:, n, :, :].rearrange("p c h -> p (c h)"), ACT.Exp).then_inc(expd, 1)
                        skewed(act, 1, [(1, stage), (0, multiply), (-1, weights)])

            def near(name, parts, extra, acc):
                spread_units(name, (OST, OD), D, parts, None, extra, acc, True)

            def spread(name, parts, first, w_edge, acc):
                spread_units(name, (ODT, OS), D if first else 2 * D, parts, w_edge, "weight" if first else "heads", acc, False)

            networks("f_", near, attention, spread, [T, NT, SC, H])

        over = nc.values_load(overfull_i[0:1, 0:1], min_val=0, max_val=1)
        with nc.If(over > 0):
            general_path()
        with nc.Else():
            fast_path()


_INS = ["x", "src", "dst", "edge_attr_64", "edge_type_500", "L0_gnn_W1", "L0_gnn_b1", "L0_gnn_W2", "L0_gnn_b2",
        "L1_gnn_relation_embed", "L1_gnn_ln_gamma", "L1_gnn_ln_beta", "L1_gnn_W_h", "L1_gnn_W_t", "L1_gnn_W_r",
        "L1_gnn_att_h", "L1_gnn_att_t", "L1_gnn_att_r", "L1_gnn_W_o"]


def kernel(**inputs):
    import numpy as np
    import concourse.bacc as bacc
    from concourse.bass_utils import run_bass_kernel_spmd as run

    nc = bacc.Bacc("TRN2", target_bir_lowering=False, num_devices=1)
    arrays, args = {}, []
    for name in _INS:
        a = np.ascontiguousarray(inputs[name])
        arrays[f"in_{name}"] = a
        args.append(nc.dram_tensor(f"in_{name}", a.shape, mybir.dt.from_np(a.dtype), kind="ExternalInput").ap())
    out = nc.dram_tensor("out_nodes", (N, D), F32, kind="ExternalOutput").ap()
    gnn_program(nc, *args, out)
    return run(nc, [arrays], core_ids=[0]).results[0]["out_nodes"]
```

```python
import concourse.bass as bass
from concourse import mybir
from contextlib import ExitStack

F32 = mybir.dt.float32
BF16 = mybir.dt.bfloat16
F8 = mybir.dt.float8e4
U8 = mybir.dt.uint8
I32 = mybir.dt.int32
U32 = mybir.dt.uint32
ALU = mybir.AluOpType
ACT = mybir.ActivationFunctionType
AX = mybir.AxisListType

N = 3125
E = 100000
D = 64
H = 2
R = 500
L = 2
T = 128
NT = -(-N // T)
LAST = N - (NT - 1) * T
EP = 125
EC = E // EP
NBLK = NT * NT
BCH = 2
CAP = BCH * T
GC = 8
NCH = -(-((E + NBLK * (T - 1)) // T) // (2 * GC)) * 2 * GC
NG = NCH // GC
NQ = NCH // 4
RW = 72
R_ONE, R_SRC, R_DST, R_REL = 64, 65, 66, 68
ALPHA = 0.15
POW_ITER = 3
LN_EPS = 1e-5
RP = 125
RT = R // RP


def wait_value(eng, sem, value):
    eng.wait_ge(sem, value)
    eng.nop(nofuse=True)


def after(eng, sem, t, per, off, apart=False):
    if isinstance(t, int):
        if t * per + off > 0:
            eng.wait_ge(sem, t * per + off)
    elif apart:
        wait_value(eng, sem, t * per + off)
    else:
        eng.wait_ge(sem, t * per + off)


def tile_pairs(eng, body):
    body(0, (0, 1))
    with eng.Fori(1, NT // 2) as t:
        body(t, (0, 1))
    body(NT // 2, (0,))


def skewed(eng, per, stages, tiles=NT):
    most, least = max(a for a, _ in stages), min(a for a, _ in stages)
    last = (tiles - 1) // 2
    units = (tiles - 2 * last) * per

    def step(t, k, end):
        for lead, f in stages:
            kk = k + lead
            if (isinstance(t, int) and t == 0 and kk < 0) or (end is not None and kk >= end):
                continue
            over, kk = divmod(kk, 2 * per)
            f(t + over if over else t, kk // per, kk % per)
    for k in range(-most, 2 * per):
        step(0, k, None)
    if last > 1:
        with eng.Fori(1, last) as t:
            for k in range(2 * per):
                step(t, k, None)
    for k in range(units - least):
        step(last, k, units)


class Chain:

    def __init__(self, eng, sem):
        self.eng, self.sem, self.base, self.n = eng, sem, 0, 0

    def step(self, ins):
        self.n += 1
        ins.then_inc(self.sem, 1)
        self.eng.wait_ge(self.sem, self.base + self.n)


def layernorm_steps(nc, ln, x, y, tmp, st, sqrt_in, sqrt_out, dve, gamma=None, beta=None):
    nt = x.shape[1]
    bc = lambda a: a.unsqueeze(2).to_broadcast([T, nt, D])
    ln.step(nc.vector.tensor_reduce(st[:, 0, :], x, AX.X, ALU.add))
    ln.step(nc.vector.tensor_scalar(st[:, 1, :], st[:, 0, :], 1.0 / D, None, ALU.mult))
    ln.step(nc.vector.tensor_tensor(y, x, bc(st[:, 1, :]), ALU.subtract))
    ln.step(nc.vector.tensor_tensor(tmp, y, y, ALU.mult))
    ln.step(nc.vector.tensor_reduce(st[:, 2, :], tmp, AX.X, ALU.add))
    nc.vector.tensor_scalar(st[:, 3, :], st[:, 2, :], 1.0 / D, LN_EPS, ALU.mult, ALU.add).then_inc(sqrt_in, 1)
    dve.wait_ge(sqrt_out, 1)
    ln.step(nc.vector.reciprocal(st[:, 5, :], st[:, 4, :]))
    ln.step(nc.vector.tensor_tensor(y, y, bc(st[:, 5, :]), ALU.mult))
    if gamma is not None:
        row = lambda a: a.unsqueeze(1).to_broadcast([T, nt, D])
        ln.step(nc.vector.tensor_tensor(y, y, row(gamma), ALU.mult))
        ln.step(nc.vector.tensor_tensor(y, y, row(beta), ALU.add))


def split_steps(nc, ln, parts, src, rest):
    ln.step(nc.vector.tensor_copy(parts[:, :, 0, :], src))
    ln.step(nc.vector.tensor_tensor(rest, src, parts[:, :, 0, :], ALU.subtract))
    ln.step(nc.vector.tensor_copy(parts[:, :, 1, :], rest))
    ln.step(nc.vector.tensor_tensor(parts[:, :, 2, :], rest, parts[:, :, 1, :], ALU.subtract))


def gnn_program(nc, x_in, src_in, dst_in, attr_in, type_in, W1, b1, W2, b2, rel, ln_g, ln_b,
                W_h, W_t, W_r, att_h, att_t, att_r, W_o, out):
    top = ExitStack()

    taken_sems = {}

    def take_sem(stack, name):
        if id(stack) not in taken_sems:
            taken_sems[id(stack)] = []

            def give_back():
                nc.clear_and_free_semaphores(taken_sems.pop(id(stack)))
                nc.all_engine_barrier()
            stack.callback(give_back)
        taken_sems[id(stack)].append(nc.alloc_semaphore(name))
        return taken_sems[id(stack)][-1]

    def sb(name, shape, dt, stack=top):
        return stack.enter_context(nc.sbuf_tensor(name, shape, dt))

    records = nc.dram_tensor("records", (NCH * T, RW), F32).ap()
    onehots = nc.dram_tensor("onehots", (2, NG, T, GC * T), BF16).ap()
    onehots8 = nc.dram_tensor("onehots8", (4, NT, T, NT * BCH * T), U8).ap()
    rel_scores = nc.dram_tensor("rel_scores", (R, 2 * L), F32).ap()
    rec_groups = records.rearrange("(g p c) w -> g p (c w)", p=T, c=GC)

    with top:
        iota1 = sb("iota1", [T, T], F32)
        ident = sb("ident", [T, T], F32)
        identb = sb("identb", [T, T], BF16)
        below = sb("below", [T, T], F32)
        ones = sb("ones", [T, T], F32)
        x = sb("x", [T, NT, D], F32)
        block_end = sb("block_end", [NT, NT], F32)
        overfull = sb("overfull", [T, 1], F32)
        overfull_i = sb("overfull_i", [1, 1], I32)
        ar = sb("ar", [T, 4 * D], F32)

        def score_phase(name, table, nt, rows, w_ap, att_ap, result):
            with ExitStack() as ctx:
                stage = sb(name + "_stage", [T, 2, D], F32, ctx)
                tT = sb(name + "_tT", [D, 2, T], F32, ctx)
                act = sb(name + "_act", [T, 2, 4 * D], F32, ctx)
                prod = sb(name + "_prod", [T, 2, 4, D], F32, ctx)
                psT = ctx.enter_context(nc.psum_tensor(name + "_psT", [D, 2, 512], F32))
                psW = ctx.enter_context(nc.psum_tensor(name + "_psW", [T, 2, 512], F32))
                sem = lambda n: take_sem(ctx, f"{name}_{n}")
                staged, turned, copied, multiplied, squashed, weighted, summed = map(
                    sem, ["staged", "turned", "copied", "multiplied", "squashed", "weighted", "summed"])
                block = ctx.enter_context(nc.Block())

                @block.vector
                def _(dve):
                    def put(t, n, i):
                        after(dve, turned, t, 2, n - 1)
                        nc.vector.tensor_scalar(stage[0:rows, n, :], table[0:rows, bass.ds(t * 2 + n, 1), :].rearrange("p a d -> p (a d)"),
                                                1.0, None, ALU.mult).then_inc(staged, 1)

                    def finish(t, n, i):
                        after(dve, squashed, t, 2, n + 1)
                        nc.vector.tensor_tensor(prod[0:rows, n, :, :].rearrange("p k d -> p (k d)"), act[0:rows, n, :],
                                                att_ap[0:rows, :], ALU.mult).then_inc(weighted, 1)
                        after(dve, weighted, t, 2, n + 1)
                        nc.vector.tensor_reduce(result[0:rows, bass.ds(t * 2 + n, 1), :].rearrange("p a k -> p (a k)"),
                                                prod[0:rows, n, :, :], AX.X, ALU.add).then_inc(summed, 1)
                    skewed(dve, 1, [(1, put), (0, finish)], nt)

                @block.tensor
                def _(pe):
                    def turn(t, n, i):
                        after(pe, staged, t, 2, n + 1, True)
                        after(pe, copied, t, 2, n - 1, True)
                        nc.tensor.transpose(psT[:, n, 0:rows], stage[0:rows, n, :], ident[0:rows, 0:rows]).then_inc(turned, 1)

                    def multiply(t, n, i):
                        after(pe, copied, t, 2, n + 1, True)
                        after(pe, squashed, t, 2, n - 1, True)
                        nc.tensor.matmul(psW[0:rows, n, 0:4 * D], tT[:, n, 0:rows], w_ap, start=True, stop=True).then_inc(multiplied, 1)
                    skewed(pe, 1, [(1, turn), (0, multiply)], nt)

                @block.scalar
                def _(act_e):
                    def copy(t, n, i):
                        after(act_e, turned, t, 2, n + 1)
                        after(act_e, multiplied, t, 2, n - 1)
                        nc.scalar.activation(tT[:, n, 0:rows], psT[:, n, 0:rows], ACT.Copy).then_inc(copied, 1)

                    def squash(t, n, i):
                        after(act_e, multiplied, t, 2, n + 1)
                        after(act_e, weighted, t, 2, n - 1)
                        nc.scalar.activation(act[0:rows, n, :], psW[0:rows, n, 0:4 * D], ACT.Tanh).then_inc(squashed, 1)
                    skewed(act_e, 1, [(1, copy), (0, squash)], nt)

        with ExitStack() as ctx:
            sem = lambda n: take_sem(ctx, n)
            s_load, s_set, s_xz = map(sem, ["x_loaded", "const_set", "x_zeroed"])
            block = ctx.enter_context(nc.Block())

            @block.vector
            def _(dve):
                nc.vector.memset(x[:, NT - 1, :], 0.0).then_inc(s_xz, 1)

            @block.sync
            def _(sp):
                sp.wait_ge(s_xz, 1)
                sp.dma_start(x[:, 0:NT - 1, :], x_in[0:(NT - 1) * T, :].rearrange("(t p) d -> p t d", p=T)).then_inc(s_load, 16)
                sp.dma_start(x[0:LAST, NT - 1, :], x_in[(NT - 1) * T:N, :]).then_inc(s_load, 16)
                sp.wait_ge(s_load, 32)

            @block.gpsimd
            def _(pool):
                nc.gpsimd.iota(iota1[:, :], [[1, T]], base=1, channel_multiplier=0, allow_small_or_imprecise_dtypes=True)
                nc.gpsimd.memset(ident[:, :], 0.0).then_inc(s_set, 1)
                nc.gpsimd.memset(identb[:, :], 0.0).then_inc(s_set, 1)
                nc.gpsimd.memset(ones[:, :], 1.0).then_inc(s_set, 1)
                pool.wait_ge(s_set, 3)
                for m in (ident, identb):
                    nc.gpsimd.affine_select(out=m[:, :], in_=m[:, :], compare_op=ALU.not_equal, fill=1.0,
                                            base=0, pattern=[[-1, T]], channel_multiplier=1)
                nc.gpsimd.affine_select(out=below[:, :], in_=ones[:, :], compare_op=ALU.is_gt, fill=0.0,
                                        base=0, pattern=[[1, T]], channel_multiplier=-1)

        with ExitStack() as ctx:
            rel_sb = sb("rel_sb", [T, RT, D], F32, ctx)
            wr = sb("wr", [D, 4 * D], F32, ctx)
            rs = sb("rs", [T, RT, 4], F32, ctx)
            with ExitStack() as c2:
                s_load = take_sem(c2, "rel_loaded")
                block = c2.enter_context(nc.Block())

                @block.sync
                def _(sp):
                    sp.dma_start(rel_sb[0:RP, :, :], rel.rearrange("(t p) d -> p t d", p=RP)).then_inc(s_load, 16)
                    sp.dma_start(wr[:, :].rearrange("p (l n) -> p l n", l=L), W_r.rearrange("l p n -> p l n")).then_inc(s_load, 16)
                    sp.dma_start(ar[:, :], att_r.rearrange("l h d -> (l h d)").partition_broadcast(T)).then_inc(s_load, 16)
                    sp.wait_ge(s_load, 48)
            score_phase("rel", rel_sb, RT, RP, wr[:, :], ar, rs)
            with ExitStack() as c2:
                s_store = take_sem(c2, "rel_stored")
                block = c2.enter_context(nc.Block())

                @block.sync
                def _(sp):
                    sp.dma_start(rel_scores.rearrange("(t p) k -> p t k", p=RP), rs[0:RP, :, :]).then_inc(s_store, 16)
                    sp.wait_ge(s_store, 16)

        with ExitStack() as slot_ctx:
            row_idx = sb("row_idx", [EP, EC], I32, slot_ctx)
            slo = sb("slo", [EP, EC], F32, slot_ctx)
            dlo = sb("dlo", [EP, EC], F32, slot_ctx)
            typ = sb("typ", [EP, EC], I32, slot_ctx)
            edge_rel = sb("edge_rel", [EP, EC, 2 * L], F32, slot_ctx)
            with ExitStack() as ctx:
                BR = 16
                s_hi = sb("s_hi", [EP, EC + BR], F32, ctx)
                d_hi = sb("d_hi", [EP, EC + BR], F32, ctx)
                iota_t = sb("iota_t", [EP, NT], F32, ctx)
                counts = sb("counts", [NT, EC + 1, NT], F32, ctx)
                rank = sb("rank", [EP, EC], F32, ctx)

                with ExitStack() as c2:
                    src_i = sb("src_i", [EP, EC], I32, c2)
                    dst_i = sb("dst_i", [EP, EC], I32, c2)
                    hi_i = sb("hi_i", [EP, 4, EC], I32, c2)
                    s_load = take_sem(c2, "edges_loaded")
                    chain = take_sem(c2, "cut_chain")
                    block = c2.enter_context(nc.Block())

                    @block.sync
                    def _(sp):
                        for to, frm in ((src_i, src_in), (dst_i, dst_in), (typ, type_in)):
                            sp.dma_start(to[:, :], frm.rearrange("(p c) -> p c", p=EP)).then_inc(s_load, 16)
                        sp.wait_ge(s_load, 48)

                    @block.gpsimd
                    def _(pool):
                        nc.gpsimd.iota(iota_t[:, :], [[1, NT]], base=0, channel_multiplier=0, allow_small_or_imprecise_dtypes=True)

                    @block.vector
                    def _(dve):
                        dve.wait_ge(s_load, 48)
                        nc.vector.memset(counts[:, 0, :], 0.0)
                        for i, (a, hi, lo) in enumerate(((src_i, s_hi, slo), (dst_i, d_hi, dlo))):
                            nc.vector.tensor_scalar(hi_i[:, 2 * i, :], a[:, :], 7, None, ALU.logical_shift_right).then_inc(chain, 1)
                            nc.vector.tensor_scalar(hi_i[:, 2 * i + 1, :], a[:, :], T - 1, None, ALU.bitwise_and).then_inc(chain, 1)
                            dve.wait_ge(chain, 2 * i + 2)
                            nc.vector.tensor_copy(hi[:, 0:EC], hi_i[:, 2 * i, :])
                            nc.vector.memset(hi[:, EC:], 0.0)
                            nc.vector.tensor_scalar(lo[:, :], hi_i[:, 2 * i + 1, :], 1.0, None, ALU.add)

                HC = 8
                GATHER_FIRST = 3
                typ_st = sb("typ_st", [EP, 2, HC], I32, ctx)
                got = sb("got", [EP, 2, HC, 2 * L], F32, ctx)

                def gather_sems(stack, beside):
                    return [[take_sem(stack, f"{beside}_rel_gathered{i}") for i in range(2)], take_sem(stack, beside + "_types_staged"),
                            take_sem(stack, beside + "_got_kept")]

                def gather_rel(pool, sems, first, count):
                    rel_gathered, types_staged, got_kept = sems

                    def gather(r, n):
                        c0 = r * (2 * HC) + (first * 2 * HC + n * HC)
                        nc.gpsimd.tensor_copy(typ_st[:, n, :], typ[:, bass.ds(c0, HC)]).then_inc(types_staged, 1)
                        wait_value(pool, types_staged, r * 2 + n + 1)
                        for j in range(HC):
                            pool.indirect_dma_start(
                                out=got[:, n, j, :], out_offset=None, in_=rel_scores,
                                in_offset=bass.IndirectOffsetOnAxis(ap=typ_st[:, n, j:j + 1].bitcast(U32), axis=0)).then_inc(rel_gathered[n], 16)

                    def keep(r, n):
                        wait_value(pool, rel_gathered[n], r * (16 * HC) + 16 * HC)
                        c0 = r * (2 * HC) + (first * 2 * HC + n * HC)
                        nc.gpsimd.tensor_copy(edge_rel[:, bass.ds(c0, HC), :], got[:, n, :, :]).then_inc(got_kept, 1)
                        wait_value(pool, got_kept, r * 2 + n + 1)
                    gather(0, 0)
                    gather(0, 1)
                    with pool.Fori(1, count) as r:
                        for n in range(2):
                            keep(r - 1, n)
                            gather(r, n)
                    for n in range(2):
                        keep(count - 1, n)

                BC = 20
                with ExitStack() as c2:
                    oa = sb("oa", [EP, 2, BC, NT], BF16, c2)
                    ob = sb("ob", [EP, 2, BC, NT], BF16, c2)
                    psH = c2.enter_context(nc.psum_tensor("psH", [NT, 2, 512], F32))
                    sem = lambda n: take_sem(c2, n)
                    marked, counted, kept = map(sem, ["cols_marked", "cols_counted", "counts_kept"])
                    rel_sems = gather_sems(c2, "count")
                    block = c2.enter_context(nc.Block())

                    @block.gpsimd
                    def _(pool):
                        gather_rel(pool, rel_sems, 0, GATHER_FIRST)

                    def mark(n, c0):
                        for o, hi in ((oa, s_hi), (ob, d_hi)):
                            last = nc.vector.tensor_tensor(
                                o[:, n, :, :], hi[:, bass.ds(c0, BC)].unsqueeze(2).to_broadcast([EP, BC, NT]),
                                iota_t[:, :].unsqueeze(1).to_broadcast([EP, BC, NT]), ALU.is_equal)
                        last.then_inc(marked, 1)

                    ROUNDS = EC // BC // 2

                    @block.vector
                    def _(dve):
                        mark(0, 0)
                        mark(1, BC)
                        with dve.Fori(1, ROUNDS) as t:
                            for n in range(2):
                                dve.wait_ge(counted, t * 2 + (n - 1))
                                mark(n, t * (2 * BC) + n * BC)

                    @block.tensor
                    def _(pe):
                        def count(n):
                            for j in range(BC):
                                last = nc.tensor.matmul(psH[:, n, j * NT:(j + 1) * NT], oa[:, n, j, :], ob[:, n, j, :],
                                                        start=True, stop=True, skip_group_check=True)
                            last.then_inc(counted, 1)
                        for n in range(2):
                            pe.wait_ge(marked, n + 1)
                            count(n)
                        with pe.Fori(1, ROUNDS) as t:
                            for n in range(2):
                                pe.wait_ge(marked, t * 2 + (n + 1))
                                pe.wait_ge(kept, t * 2 + (n - 1))
                                count(n)

                    @block.scalar
                    def _(act):
                        with act.Fori(0, ROUNDS) as t:
                            for n in range(2):
                                wait_value(act, counted, t * 2 + (n + 1))
                                nc.scalar.activation(counts[:, bass.ds(t * (2 * BC) + (n * BC + 1), BC), :].rearrange("p c b -> p (c b)"),
                                                     psH[:, n, 0:BC * NT], ACT.Copy).then_inc(kept, 1)

                with ExitStack() as c2:
                    small = sb("small", [NT, 6, NT], F32, c2)
                    small_i = sb("small_i", [NT, 2, NT], I32, c2)
                    row_base = sb("row_base", [NT, 1], F32, c2)
                    own = sb("own", [NT, 3, NT], F32, c2)
                    most = sb("most", [NT, 2], F32, c2)
                    psB = c2.enter_context(nc.psum_tensor("psB", [NT, 512], F32))
                    psO = c2.enter_context(nc.psum_tensor("psOver", [T, 512], F32))
                    sem = lambda n: take_sem(c2, n)
                    chain, totals, based, over, told, s_iota = map(sem, ["slot_chain", "row_totals", "row_bases", "blocks_over", "told", "own_set"])
                    rel_sems = gather_sems(c2, "base")
                    block = c2.enter_context(nc.Block())

                    @block.gpsimd
                    def _(pool):
                        nc.gpsimd.iota(own[:, 0, :], [[CAP, NT]], base=0, channel_multiplier=NT * CAP,
                                       allow_small_or_imprecise_dtypes=True).then_inc(s_iota, 1)
                        gather_rel(pool, rel_sems, GATHER_FIRST, GATHER_FIRST)

                    @block.tensor
                    def _(pe):
                        pe.wait_ge(over, 1)
                        nc.tensor.matmul(psO[:, 0:1], ones[0:NT, 0:T], most[:, 1:2], start=True, stop=True).then_inc(told, 1)
                        pe.wait_ge(totals, 1)
                        nc.tensor.matmul(psB[:, 0:1], below[0:NT, 0:NT], small[:, 2, NT - 1:NT], start=True, stop=True).then_inc(based, 1)

                    @block.vector
                    def _(dve):
                        ln = Chain(dve, chain)
                        for b in range(NT):
                            c = counts[:, 1:EC + 1, b]
                            last = nc.vector.tensor_tensor_scan(c, c, c, 0.0, ALU.add, ALU.max)
                        ln.step(last)
                        ln.step(nc.vector.tensor_reduce(most[:, 0:1], counts[:, EC, :], AX.X, ALU.max))
                        nc.vector.tensor_scalar(most[:, 1:2], most[:, 0:1], float(CAP), None, ALU.is_gt).then_inc(over, 1)
                        ln.step(nc.vector.tensor_scalar(small_i[:, 0, :], counts[:, EC, :], float(T - 1), None, ALU.add))
                        ln.step(nc.vector.tensor_scalar(small_i[:, 1, :], small_i[:, 0, :], 7, None, ALU.logical_shift_right))
                        ln.step(nc.vector.tensor_copy(small[:, 1, :], small_i[:, 1, :]))
                        nc.vector.tensor_tensor_scan(small[:, 2, :], small[:, 1, :], small[:, 1, :], 0.0, ALU.add, ALU.max).then_inc(totals, 1)
                        dve.wait_ge(told, 1)
                        ln.step(nc.vector.tensor_scalar(overfull[:, :], psO[:, 0:1], 1.0, None, ALU.min))
                        ln.step(nc.vector.tensor_copy(overfull_i[:, :], overfull[0:1, :]))
                        dve.wait_ge(based, 1)
                        ln.step(nc.vector.tensor_copy(row_base[:, :], psB[:, 0:1]))
                        ln.step(nc.vector.tensor_scalar(block_end[:, :], small[:, 2, :], row_base[:, :], None, ALU.add))
                        ln.step(nc.vector.tensor_tensor(small[:, 4, :], block_end[:, :], small[:, 1, :], ALU.subtract))
                        ln.step(nc.vector.tensor_scalar(small[:, 5, :], small[:, 4, :], float(T), None, ALU.mult))
                        dve.wait_ge(s_iota, 1)
                        ln.step(nc.vector.tensor_tensor(own[:, 1, :], small[:, 5, :], own[:, 0, :], ALU.subtract))
                        ln.step(nc.vector.scalar_tensor_tensor(out=own[:, 2, :], in0=own[:, 1, :], scalar=overfull[0:NT, :], in1=own[:, 0, :],
                                                               op0=ALU.mult, op1=ALU.add))
                        nc.vector.tensor_tensor(counts[:, 0:EC, :], counts[:, 0:EC, :],
                                                own[:, 2, :].unsqueeze(1).to_broadcast([NT, EC, NT]), ALU.add)

                with ExitStack() as c2:
                    oa = sb("oa2", [EP, BR, NT], BF16, c2)
                    ob = sb("ob2", [EP, 2, BR, NT], BF16, c2)
                    oaT = sb("oaT", [NT, BR, 128], BF16, c2)
                    oaTf = sb("oaTf", [NT, 2, BR, 128], F32, c2)
                    before = sb("before", [EP, BR, EP], BF16, c2)
                    pick = sb("pick", [EP, BR, NT], F32, c2)
                    zeros = sb("zeros", [T, GC * RW], F32, c2)
                    psT = c2.enter_context(nc.psum_tensor("psT", [NT, BR, 128], BF16))
                    psS = c2.enter_context(nc.psum_tensor("psS", [EP, BR, 128], F32))
                    psR = c2.enter_context(nc.psum_tensor("psRk", [EP, 512], F32))
                    sem = lambda n: take_sem(c2, n)
                    marked, turned, copied, copied_f, alike, masked, ranked, picked, s_zero, s_clear = map(
                        sem, ["marked", "turned", "copied", "copied_f", "alike", "masked", "ranked", "picked", "zero_ready", "cleared"])
                    rel_sems = gather_sems(c2, "rank")
                    block = c2.enter_context(nc.Block())

                    @block.gpsimd
                    def _(pool):
                        gather_rel(pool, rel_sems, 2 * GATHER_FIRST, EC // (2 * HC) - 2 * GATHER_FIRST)

                    def rounds(eng, body):
                        assert EC // BR % 2 == 0
                        for n in range(2):
                            body(0, n)
                        with eng.Fori(1, EC // BR // 2) as t:
                            for n in range(2):
                                body(t, n)

                    @block.sync
                    def _(sp):
                        sp.wait_ge(s_zero, 1)
                        with sp.Fori(0, NG) as g:
                            sp.dma_start(rec_groups[bass.ds(g, 1), :, :].rearrange("a p w -> (a p) w"), zeros[:, :]).then_inc(s_clear, 16)
                        sp.wait_ge(s_clear, NG * 16)

                    @block.vector
                    def _(dve):
                        nc.vector.memset(zeros[:, :], 0.0).then_inc(s_zero, 1)

                        def mark(t, n, c0):
                            for o, hi in ((oa[:, :, :], s_hi), (ob[:, n, :, :], d_hi)):
                                last = nc.vector.tensor_tensor(
                                    o, hi[:, bass.ds(c0, BR)].unsqueeze(2).to_broadcast([EP, BR, NT]),
                                    iota_t[:, :].unsqueeze(1).to_broadcast([EP, BR, NT]), ALU.is_equal)
                            last.then_inc(marked, 1)

                        def body(t, n):
                            after(dve, turned, t, 2, n + 1)
                            mark(t, 1 - n, t * (2 * BR) + (n + 1) * BR)
                            after(dve, alike, t, 2, n + 1)
                            for q in range(BR // 4):
                                last = nc.vector.tensor_tensor(before[:, 4 * q:4 * q + 4, :], psS[:, 4 * q:4 * q + 4, 0:EP],
                                                               below[0:EP, 0:EP].unsqueeze(1).to_broadcast([EP, 4, EP]), ALU.mult)
                            last.then_inc(masked, 1)
                            after(dve, ranked, t, 2, n + 1)
                            nc.vector.tensor_tensor(pick[:, :, :].rearrange("p c b -> p (c b)"), psR[:, 0:BR * NT],
                                                    ob[:, n, :, :].rearrange("p c b -> p (c b)"), ALU.mult).then_inc(picked, 1)
                            after(dve, picked, t, 2, n + 1)
                            nc.vector.tensor_reduce(rank[:, bass.ds(t * (2 * BR) + n * BR, BR)], pick[:, :, :], AX.X, ALU.add)
                        mark(0, 0, 0)
                        rounds(dve, body)

                    @block.tensor
                    def _(pe):
                        def turn():
                            for j in range(BR):
                                last = nc.tensor.transpose(psT[:, j, 0:EP], oa[:, j, :], identb[0:EP, 0:EP])
                            last.then_inc(turned, 1)

                        def body(t, n):
                            after(pe, copied, t, 2, n + 1, True)
                            after(pe, masked, t, 2, n, True)
                            for j in range(BR):
                                last = nc.tensor.matmul(psS[:, j, 0:EP], oaT[:, j, 0:EP], oaT[:, j, 0:EP], start=True, stop=True,
                                                        skip_group_check=True)
                            last.then_inc(alike, 1)
                            after(pe, marked, t, 2, n + 2, True)
                            after(pe, copied_f, t, 2, n + 1, True)
                            turn()
                            after(pe, masked, t, 2, n + 1, True)
                            after(pe, picked, t, 2, n, True)
                            for j in range(BR):
                                o = psR[:, j * NT:(j + 1) * NT]
                                nc.tensor.matmul(o, oaTf[:, n, j, 0:EP],
                                                 counts[:, bass.ds(t * (2 * BR) + n * BR + j, 1), :].rearrange("p a b -> p (a b)"),
                                                 start=True, stop=False, skip_group_check=True)
                                last = nc.tensor.matmul(o, before[:, j, :], ob[:, n, j, :], start=False, stop=True, skip_group_check=True)
                            last.then_inc(ranked, 1)
                        pe.wait_ge(marked, 1)
                        turn()
                        rounds(pe, body)

                    @block.scalar
                    def _(act):
                        def body(t, n):
                            after(act, turned, t, 2, n + 1)
                            nc.scalar.activation(oaT[:, :, 0:EP], psT[:, :, 0:EP], ACT.Copy).then_inc(copied, 1)
                            after(act, ranked, t, 2, n - 1)
                            nc.scalar.activation(oaTf[:, n, :, 0:EP], psT[:, :, 0:EP], ACT.Copy).then_inc(copied_f, 1)
                        rounds(act, body)

                with ExitStack() as c2:
                    ri = sb("ri", [EP, 5, EC], I32, c2)
                    rf = sb("rf", [EP, 5, EC], F32, c2)
                    chain = take_sem(c2, "row_chain")
                    block = c2.enter_context(nc.Block())

                    @block.vector
                    def _(dve):
                        ln = Chain(dve, chain)
                        ln.step(nc.vector.tensor_copy(ri[:, 0, :], rank[:, :]))
                        ln.step(nc.vector.tensor_scalar(ri[:, 1, :], ri[:, 0, :], -GC * T, None, ALU.bitwise_and))
                        ln.step(nc.vector.tensor_scalar(ri[:, 2, :], ri[:, 0, :], T - 1, 3, ALU.bitwise_and, ALU.logical_shift_left))
                        ln.step(nc.vector.tensor_scalar(ri[:, 3, :], ri[:, 0, :], 7, GC - 1, ALU.logical_shift_right, ALU.bitwise_and))
                        ln.step(nc.vector.tensor_tensor(ri[:, 4, :], ri[:, 1, :], ri[:, 2, :], ALU.bitwise_or))
                        ln.step(nc.vector.tensor_tensor(ri[:, 4, :], ri[:, 4, :], ri[:, 3, :], ALU.bitwise_or))
                        ln.step(nc.vector.tensor_copy(rf[:, 0, :], ri[:, 4, :]))
                        ln.step(nc.vector.tensor_scalar(ri[:, 1, :], ri[:, 0, :], T - 1, None, ALU.bitwise_and))
                        ln.step(nc.vector.tensor_scalar(ri[:, 2, :], ri[:, 0, :], 7, BCH - 1, ALU.logical_shift_right, ALU.bitwise_and))
                        ln.step(nc.vector.scalar_tensor_tensor(out=rf[:, 1, :], in0=ri[:, 1, :], scalar=float(NT * BCH), in1=ri[:, 2, :],
                                                               op0=ALU.mult, op1=ALU.add))
                        ln.step(nc.vector.scalar_tensor_tensor(out=rf[:, 2, :], in0=d_hi[:, 0:EC], scalar=float(BCH), in1=rf[:, 1, :],
                                                               op0=ALU.mult, op1=ALU.add))
                        ln.step(nc.vector.scalar_tensor_tensor(out=rf[:, 3, :], in0=s_hi[:, 0:EC], scalar=float(NT * BCH * T), in1=rf[:, 2, :],
                                                               op0=ALU.mult, op1=ALU.add))
                        ln.step(nc.vector.tensor_tensor(rf[:, 4, :], rf[:, 0, :], rf[:, 3, :], ALU.subtract))
                        ln.step(nc.vector.scalar_tensor_tensor(out=row_idx[:, :], in0=rf[:, 4, :], scalar=overfull[0:EP, :], in1=rf[:, 3, :],
                                                               op0=ALU.mult, op1=ALU.add))

            with ExitStack() as ctx:
                HC = 8
                stage = sb("stage", [EP, 2, HC, RW], F32, ctx)
                row_st = sb("row_st", [EP, 2, HC], I32, ctx)
                sem = lambda n: take_sem(ctx, n)
                attr_in_stage = [sem(f"attr_in_stage{i}") for i in range(2)]
                fields_set, s_one = sem("fields_set"), sem("ones_set")
                scattered = [sem(f"records_scattered{i}") for i in range(2)]
                block = ctx.enter_context(nc.Block())
                attr_cols = attr_in.rearrange("(p c) d -> p c d", p=EP)
                ROUNDS = EC // (2 * HC)

                @block.sync
                def _(sp):
                    def load(n, c0):
                        sp.dma_start(stage[:, n, :, 0:D], attr_cols[:, bass.ds(c0, HC), :]).then_inc(attr_in_stage[n], 16)
                    load(0, 0)
                    load(1, HC)
                    with sp.Fori(1, ROUNDS) as t:
                        for n in range(2):
                            wait_value(sp, scattered[n], t * (16 * HC))
                            load(n, t * (2 * HC) + n * HC)

                @block.vector
                def _(dve):
                    nc.vector.memset(stage[:, :, :, D:RW], 0.0).then_inc(s_one, 1)
                    dve.wait_ge(s_one, 1)
                    nc.vector.memset(stage[:, :, :, R_ONE:R_ONE + 1], 1.0).then_inc(s_one, 1)

                    def fields(n, c0):
                        cols = bass.ds(c0, HC)
                        nc.vector.tensor_copy(stage[:, n, :, R_SRC], slo[:, cols])
                        nc.vector.tensor_copy(stage[:, n, :, R_DST], dlo[:, cols])
                        nc.vector.tensor_copy(stage[:, n, :, R_REL:R_REL + 2 * L], edge_rel[:, cols, :])
                        nc.vector.tensor_copy(row_st[:, n, :], row_idx[:, cols]).then_inc(fields_set, 1)
                    dve.wait_ge(s_one, 2)
                    fields(0, 0)
                    fields(1, HC)
                    with dve.Fori(1, ROUNDS) as t:
                        for n in range(2):
                            wait_value(dve, scattered[n], t * (16 * HC))
                            fields(n, t * (2 * HC) + n * HC)

                @block.gpsimd
                def _(pool):
                    def scatter(n):
                        for j in range(HC):
                            pool.indirect_dma_start(
                                out=records, out_offset=bass.IndirectOffsetOnAxis(ap=row_st[:, n, j:j + 1].bitcast(U32), axis=0),
                                in_=stage[:, n, j, :], in_offset=None).then_inc(scattered[n], 16)

                    with pool.Fori(0, ROUNDS) as t:
                        for n in range(2):
                            wait_value(pool, fields_set, t * 2 + (n + 1))
                            wait_value(pool, attr_in_stage[n], (t + 1) * 16)
                            scatter(n)
                    for n in range(2):
                        pool.wait_ge(scattered[n], ROUNDS * 16 * HC)

        def dense_phase(name, sources, w_parts, finish, steps):
            K = sum(s.shape[2] for s in sources)
            with ExitStack() as ctx:
                stage = sb(name + "_stage", [T, 2, K], F32, ctx)
                zT = sb(name + "_zT", [T, 2, 2, T], F32, ctx)
                psT = ctx.enter_context(nc.psum_tensor(name + "_psT", [T, 2, 4, T], F32))
                psO = ctx.enter_context(nc.psum_tensor(name + "_psO", [T, 2, 512], F32))
                sem = lambda n: take_sem(ctx, f"{name}_{n}")
                staged, turned, copied, multiplied, chain = map(sem, ["staged", "turned", "copied", "multiplied", "chain"])
                cuts = [(0, min(K, T))] + ([(T, K - T)] if K > T else [])
                block = ctx.enter_context(nc.Block())

                @block.vector
                def _(dve):
                    ln = Chain(dve, chain)

                    def put(t, n, i):
                        after(dve, turned, t, 2, n - 1)
                        o = 0
                        for s in sources:
                            w = s.shape[2]
                            last = nc.vector.tensor_scalar(stage[:, n, o:o + w], s[:, bass.ds(t * 2 + n, 1), :].rearrange("p a d -> p (a d)"),
                                                           1.0, None, ALU.mult)
                            o += w
                        last.then_inc(staged, 1)

                    def end(t, n, i):
                        after(dve, multiplied, t, 2, n + 1)
                        ln.base, ln.n = t * (2 * steps) + n * steps, 0
                        finish(ln, bass.ds(t * 2 + n, 1), psO[:, n, 0:D])
                        assert ln.n == steps
                    skewed(dve, 1, [(1, put), (0, end)])

                @block.tensor
                def _(pe):
                    def turn(t, n, i):
                        after(pe, staged, t, 2, n + 1, True)
                        after(pe, copied, t, 2, n - 1, True)
                        for i, (o, w) in enumerate(cuts):
                            last = nc.tensor.transpose(psT[0:w, n, i, :], stage[:, n, o:o + w], ident[:, :])
                        last.then_inc(turned, 1)

                    def multiply(t, n, i):
                        after(pe, copied, t, 2, n + 1, True)
                        after(pe, chain, t, 2 * steps, (n - 1) * steps, True)
                        for i, (o, w) in enumerate(cuts):
                            last = nc.tensor.matmul(psO[:, n, 0:D], zT[0:w, n, i, :], w_parts[i], start=(i == 0), stop=(i == len(cuts) - 1))
                        last.then_inc(multiplied, 1)
                    skewed(pe, 1, [(1, turn), (0, multiply)])

                @block.scalar
                def _(act):
                    def copy(t, n, i):
                        after(act, turned, t, 2, n + 1)
                        after(act, multiplied, t, 2, n - 1)
                        for i, (o, w) in enumerate(cuts):
                            last = nc.scalar.activation(zT[0:w, n, i, :], psT[0:w, n, i, :], ACT.Copy)
                        last.then_inc(copied, 1)
                    skewed(act, 1, [(0, copy)])

        def vector_steps(name, steps, sqrt=None):
            with ExitStack() as ctx:
                chain = take_sem(ctx, name + "_chain")
                root_in = take_sem(ctx, name + "_root_in")
                root_out = take_sem(ctx, name + "_root_out")
                block = ctx.enter_context(nc.Block())

                @block.vector
                def _(dve):
                    steps(Chain(dve, chain), dve, root_in, root_out)

                if sqrt is not None:
                    @block.scalar
                    def _(act):
                        act.wait_ge(root_in, 1)
                        nc.scalar.activation(sqrt[1], sqrt[0], ACT.Sqrt).then_inc(root_out, 1)

        w1a, w1b = sb("w1a", [T, D], F32), sb("w1b", [D, D], F32)
        w2a, w2b = sb("w2a", [T, D], F32), sb("w2b", [D, D], F32)
        wo = sb("wo", [T, L, D], F32)
        wht = sb("wht", [D, L, 4 * D], F32)
        aht = sb("aht", [T, L, 4 * D], F32)
        rows = sb("rows", [T, 2 + 2 * L, D], F32)
        st = sb("st", [T, 6, NT], F32)
        with ExitStack() as ctx:
            s_load = take_sem(ctx, "weights_loaded")
            block = ctx.enter_context(nc.Block())

            @block.sync
            def _(sp):
                loads = [(w1a[:, :], W1[0:T, :]), (w1b[:, :], W1[T:3 * D, :]), (w2a[:, :], W2[0:T, :]), (w2b[:, :], W2[T:3 * D, :]),
                         (wo[:, :, :], W_o.rearrange("l p d -> p l d")),
                         (wht[:, :, 0:2 * D], W_h.rearrange("l p n -> p l n")), (wht[:, :, 2 * D:], W_t.rearrange("l p n -> p l n")),
                         (rows[:, 0, :], b1.partition_broadcast(T)), (rows[:, 1, :], b2.partition_broadcast(T))]
                for l in range(L):
                    loads += [(aht[:, l, 0:2 * D], att_h[l, :, :].rearrange("h d -> (h d)").partition_broadcast(T)),
                              (aht[:, l, 2 * D:], att_t[l, :, :].rearrange("h d -> (h d)").partition_broadcast(T)),
                              (rows[:, 2 + l, :], ln_g[l, :].partition_broadcast(T)),
                              (rows[:, 2 + L + l, :], ln_b[l, :].partition_broadcast(T))]
                for to, frm in loads:
                    sp.dma_start(to, frm).then_inc(s_load, 16)
                sp.wait_ge(s_load, 16 * len(loads))

        def networks(tag, near, attention, spread, w_shape):
            own_sb = ExitStack()

            def sb(name, shape, dt, stack=own_sb):
                return stack.enter_context(nc.sbuf_tensor(f"{tag}_{name}", shape, dt))

            with own_sb:
                with ExitStack() as ctx:
                    parts = sb("parts0", [T, NT, 3, D], BF16, ctx)
                    rest = sb("rest0", [T, NT, D], F32, ctx)
                    acc0 = sb("acc0", [T, NT, 2 * D + 1], F32, ctx)
                    acc1 = sb("acc1", [T, NT, D], F32, ctx)
                    inv_deg = sb("inv_deg", [T, NT], F32, ctx)
                    hid = sb("hid", [T, NT, D], F32, ctx)
                    mean = lambda a: inv_deg[:, :].unsqueeze(2).to_broadcast([T, NT, a.shape[2]])

                    vector_steps(tag + "split_x", lambda ln, dve, i, o: split_steps(nc, ln, parts, x[:, :, :], rest[:, :, :]))
                    near(tag + "near1", parts, "record", acc0)

                    def degrees(ln, dve, i, o):
                        ln.step(nc.vector.tensor_scalar(st[:, 0, :], acc0[:, :, 2 * D], 1.0, None, ALU.max))
                        ln.step(nc.vector.reciprocal(inv_deg[:, :], st[:, 0, :]))
                        a = acc0[:, :, 0:2 * D]
                        ln.step(nc.vector.tensor_tensor(a, a, mean(a), ALU.mult))
                    vector_steps(tag + "degrees", degrees)

                    def relu_out(to, bias):
                        def finish(ln, tile, ps):
                            y = to[:, tile, :].rearrange("p a d -> p (a d)")
                            ln.step(nc.vector.tensor_tensor(y, ps, bias, ALU.add))
                            ln.step(nc.vector.tensor_scalar(y, y, 0.0, None, ALU.max))
                        return finish
                    dense_phase(tag + "layer1", [x, acc0[:, :, 0:D], acc0[:, :, D:2 * D]], [w1a[:, :], w1b[:, :]], relu_out(hid, rows[:, 0, :]), 2)
                    vector_steps(tag + "split_hid", lambda ln, dve, i, o: split_steps(nc, ln, parts, hid[:, :, :], rest[:, :, :]))
                    near(tag + "near2", parts, None, acc1)
                    vector_steps(tag + "mean2", lambda ln, dve, i, o: ln.step(nc.vector.tensor_tensor(acc1[:, :, :], acc1[:, :, :], mean(acc1), ALU.mult)))
                    dense_phase(tag + "layer2", [hid, acc1, acc0[:, :, D:2 * D]], [w2a[:, :], w2b[:, :]], relu_out(rest, rows[:, 1, :]), 2)

                    def first_norm(ln, dve, i, o):
                        ln.step(nc.vector.tensor_tensor(rest[:, :, :], rest[:, :, :], x[:, :, :], ALU.add))
                        layernorm_steps(nc, ln, rest[:, :, :], x[:, :, :], hid[:, :, :], st, i, o, dve)
                    vector_steps(tag + "norm0", first_norm, (st[:, 3, :], st[:, 4, :]))

                def store_nodes(a):
                    with ExitStack() as ctx:
                        s_out = take_sem(ctx, tag + "_out_stored")
                        block = ctx.enter_context(nc.Block())

                        @block.sync
                        def _(sp):
                            sp.dma_start(out[0:(NT - 1) * T, :].rearrange("(t p) d -> p t d", p=T), a[:, 0:NT - 1, :]).then_inc(s_out, 16)
                            sp.dma_start(out[(NT - 1) * T:N, :], a[0:LAST, NT - 1, :]).then_inc(s_out, 16)
                            sp.wait_ge(s_out, 32)
                ent = sb("ent", [T, NT, D], F32)
                h = sb("h", [T, NT, D], F32)
                ah = sb("ah", [T, NT, D], F32)
                Z = sb("Z", [T, NT, 2 * D], F32)
                acc = sb("acc", [T, NT, 2 * D + 2], F32)
                parts = sb("parts", [T, NT, 3, 2 * D], BF16)
                w_edge = sb("w_edge", w_shape, F32)
                score4 = sb("score4", [T, NT, 4], F32)
                rest2 = sb("rest2", [T, NT, H], F32)
                pick_src = sb("pick_src", [T, NT, 3, H], BF16)
                pick_dst = sb("pick_dst", [T, NT, 3, H], BF16)
                norm = sb("norm", [T, NT, H], F32)

                vector_steps(tag + "ent", lambda ln, dve, i, o: ln.step(nc.vector.tensor_copy(ent[:, :, :], x[:, :, :])))
                for l in range(L):
                    nm = f"l{l}"

                    def layer_norm(ln, dve, i, o):
                        layernorm_steps(nc, ln, ent[:, :, :], h[:, :, :], ah[:, :, :], st, i, o, dve, rows[:, 2 + l, :], rows[:, 2 + L + l, :])
                        ln.step(nc.vector.tensor_scalar(ah[:, :, :], h[:, :, :], ALPHA, None, ALU.mult))
                    vector_steps(tag + nm + "_norm", layer_norm, (st[:, 3, :], st[:, 4, :]))
                    score_phase(tag + nm + "_score", h, NT, T, wht[:, l, :], aht[:, l, :], score4)

                    def split_scores(ln, dve, i, o):
                        split_steps(nc, ln, pick_src, score4[:, :, 0:2], rest2[:, :, :])
                        split_steps(nc, ln, pick_dst, score4[:, :, 2:4], rest2[:, :, :])
                    vector_steps(tag + nm + "_split_scores", split_scores)

                    attention(tag + nm, l, pick_src, pick_dst, w_edge, rest2)

                    vector_steps(tag + nm + "_split_h", lambda ln, dve, i, o: split_steps(nc, ln, parts[:, :, :, 0:D], h[:, :, :], Z[:, :, 0:D]))
                    for it in range(POW_ITER):
                        first = it == 0
                        spread(tag + f"{nm}_spread{it}", parts[:, :, :, 0:D] if first else parts, first, w_edge,
                               acc if first else acc[:, :, 0:2 * D])

                        def mix(ln, dve, i, o):
                            if first:
                                ln.step(nc.vector.tensor_scalar(norm[:, :, :], acc[:, :, 2 * D:2 * D + 2], 1e-30, None, ALU.max))
                                ln.step(nc.vector.reciprocal(norm[:, :, :], norm[:, :, :]))
                                ln.step(nc.vector.tensor_scalar(norm[:, :, :], norm[:, :, :], 1.0 - ALPHA, None, ALU.mult))
                            for k in range(H):
                                s = slice(k * D, (k + 1) * D)
                                ln.step(nc.vector.tensor_tensor(Z[:, :, s], acc[:, :, s], norm[:, :, k:k + 1].to_broadcast([T, NT, D]), ALU.mult))
                                ln.step(nc.vector.tensor_tensor(Z[:, :, s], Z[:, :, s], ah[:, :, :], ALU.add))
                            if it < POW_ITER - 1:
                                split_steps(nc, ln, parts, Z[:, :, :], acc[:, :, 0:2 * D])
                        vector_steps(tag + f"{nm}_mix{it}", mix)

                    def residual(ln, tile, ps):
                        y = ent[:, tile, :].rearrange("p a d -> p (a d)")
                        ln.step(nc.vector.tensor_tensor(y, y, ps, ALU.add))
                    dense_phase(tag + nm + "_conv", [Z], [wo[:, l, :]], residual, 1)

                def last_norm(ln, dve, i, o):
                    ln.step(nc.vector.tensor_tensor(ent[:, :, :], ent[:, :, :], x[:, :, :], ALU.add))
                    layernorm_steps(nc, ln, ent[:, :, :], h[:, :, :], ah[:, :, :], st, i, o, dve)
                vector_steps(tag + "norm_last", last_norm, (st[:, 3, :], st[:, 4, :]))
                store_nodes(h)

        def general_path():
            gstack = ExitStack()

            def sb(name, shape, dt, stack=gstack):
                return stack.enter_context(nc.sbuf_tensor("g_" + name, shape, dt))

            with gstack:
                src_lo = sb("src_lo", [T, NCH], F32)
                dst_lo = sb("dst_lo", [T, NCH], F32)
                s_rel = sb("s_rel", [T, NCH, 2 * L], F32)
                src_tile = sb("src_tile", [1, NCH], I32)
                dst_tile = sb("dst_tile", [1, NCH], I32)
                shifted = sb("shifted", [T, NCH, H], F32)
                least = sb("least", [T, 4], F32)
                top_of = sb("top_of", [T, NT, H], F32)

                with ExitStack() as c2:
                    iota_c = sb("iota_c", [NT, NCH], F32, c2)
                    passed = sb("passed", [NT, NCH], F32, c2)
                    rows_passed = sb("rows_passed", [NT, NCH], F32, c2)
                    kf = sb("kf", [1, 2, NCH], F32, c2)
                    psK = c2.enter_context(nc.psum_tensor("psK", [1, 3, 512], F32))
                    psR = c2.enter_context(nc.psum_tensor("psR", [1, 3, 512], F32))
                    sem = lambda n: take_sem(c2, n)
                    chain, compared, summed, s_iota = map(sem, ["chunk_chain", "ends_passed", "chunk_keys", "iota_set"])
                    block = c2.enter_context(nc.Block())
                    spans = [(i * 512, min(512, NCH - i * 512)) for i in range(-(-NCH // 512))]

                    @block.gpsimd
                    def _(pool):
                        nc.gpsimd.iota(iota_c[:, :], [[1, NCH]], base=0, channel_multiplier=0,
                                       allow_small_or_imprecise_dtypes=True).then_inc(s_iota, 1)

                    @block.tensor
                    def _(pe):
                        pe.wait_ge(compared, 1)
                        for i, (o, w) in enumerate(spans):
                            nc.tensor.matmul(psK[:, i, 0:w], ones[0:NT, 0:1], passed[:, o:o + w], start=True, stop=True)
                            last = nc.tensor.matmul(psR[:, i, 0:w], ones[0:NT, 0:1], rows_passed[:, o:o + w], start=True, stop=True)
                        last.then_inc(summed, 1)

                    @block.vector
                    def _(dve):
                        ln = Chain(dve, chain)
                        dve.wait_ge(s_iota, 1)
                        ln.step(nc.vector.tensor_scalar(passed[:, :], iota_c[:, :], block_end[:, 0:1], None, ALU.is_ge))
                        for b in range(1, NT):
                            ln.step(nc.vector.scalar_tensor_tensor(out=passed[:, :], in0=iota_c[:, :], scalar=block_end[:, b:b + 1],
                                                                   in1=passed[:, :], op0=ALU.is_ge, op1=ALU.add))
                        nc.vector.tensor_scalar(rows_passed[:, :], iota_c[:, :], block_end[:, NT - 1:NT], None, ALU.is_ge).then_inc(compared, 1)
                        dve.wait_ge(summed, 1)
                        for i, (o, w) in enumerate(spans):
                            nc.vector.tensor_copy(kf[:, 0, o:o + w], psK[:, i, 0:w])
                            last = nc.vector.tensor_copy(kf[:, 1, o:o + w], psR[:, i, 0:w])
                        ln.step(last)
                        nc.vector.scalar_tensor_tensor(out=dst_tile[:, :], in0=kf[:, 1, :], scalar=-float(NT), in1=kf[:, 0, :],
                                                       op0=ALU.mult, op1=ALU.add)
                        nc.vector.tensor_scalar(src_tile[:, :], kf[:, 1, :], float(NT - 1), None, ALU.min)

                with ExitStack() as ctx:
                    rec = sb("rec", [T, 2, GC, RW], F32, ctx)
                    mark = sb("mark", [T, 2, 2, GC, T], BF16, ctx)
                    turn = sb("turn", [T, 2, 2, GC * T], BF16, ctx)
                    psT = ctx.enter_context(nc.psum_tensor("psTurn", [T, 2, 2, GC * T], BF16))
                    sem = lambda n: take_sem(ctx, n)
                    loaded = [sem(f"rec_loaded{i}") for i in range(2)]
                    stored = [sem(f"turned_stored{i}") for i in range(2)]
                    kept, marked, turned, copied = map(sem, ["places_kept", "slots_marked", "marks_turned", "turned_copied"])
                    block = ctx.enter_context(nc.Block())

                    def rounds(eng, body):
                        body(0, True)
                        with eng.Fori(1, NG // 2) as t:
                            body(t, False)

                    @block.sync
                    def _(sp):
                        def body(t, first):
                            for n in range(2):
                                if not first:
                                    wait_value(sp, kept, t * 2 + (n - 1))
                                sp.dma_start(rec[:, n, :, :].rearrange("p c w -> p (c w)"),
                                             rec_groups[bass.ds(t * 2 + n, 1), :, :].rearrange("a p w -> (a p) w")).then_inc(loaded[n], 16)
                        rounds(sp, body)

                    @block.vector
                    def _(dve):
                        def body(t, first):
                            for n in range(2):
                                cols = bass.ds((t * 2 + n) * GC, GC)
                                wait_value(dve, loaded[n], t * 16 + 16)
                                nc.vector.tensor_copy(src_lo[:, cols], rec[:, n, :, R_SRC])
                                nc.vector.tensor_copy(dst_lo[:, cols], rec[:, n, :, R_DST])
                                if not first:
                                    wait_value(dve, turned, t * 2 + (n - 1))
                                for k, r in enumerate((R_SRC, R_DST)):
                                    nc.vector.tensor_tensor(mark[:, n, k, :, :], iota1[:, :].unsqueeze(1).to_broadcast([T, GC, T]),
                                                            rec[:, n, :, r:r + 1].to_broadcast([T, GC, T]), ALU.is_equal).then_inc(marked, 1)
                                nc.vector.tensor_copy(s_rel[:, cols, :], rec[:, n, :, R_REL:R_REL + 2 * L]).then_inc(kept, 1)
                        rounds(dve, body)

                    @block.tensor
                    def _(pe):
                        def body(t, first):
                            for n in range(2):
                                wait_value(pe, marked, t * 4 + (2 * n + 2))
                                if not first:
                                    wait_value(pe, copied, t * 4 + (2 * n - 2))
                                for k in range(2):
                                    for j in range(GC):
                                        last = nc.tensor.transpose(psT[:, n, k, j * T:(j + 1) * T], mark[:, n, k, j, :], identb[:, :])
                                last.then_inc(turned, 1)
                        rounds(pe, body)

                    @block.scalar
                    def _(act):
                        def body(t, first):
                            for n in range(2):
                                wait_value(act, turned, t * 2 + (n + 1))
                                if not first:
                                    wait_value(act, stored[n], t * 32)
                                for k in range(2):
                                    nc.scalar.activation(turn[:, n, k, :], psT[:, n, k, :], ACT.Copy).then_inc(copied, 1)
                                wait_value(act, copied, t * 4 + (2 * n + 2))
                                for k in range(2):
                                    act.dma_start(onehots[k, bass.ds(t * 2 + n, 1), :, :].rearrange("a p w -> (a p) w"),
                                                  turn[:, n, k, :]).then_inc(stored[n], 16)
                        rounds(act, body)
                        for n in range(2):
                            act.wait_ge(stored[n], NG * 16)

                ROUNDS = NCH // (2 * GC)

                def peeled(eng, body):
                    body(0, True, False)
                    with eng.Fori(1, ROUNDS - 1) as t:
                        body(t, False, False)
                    body(ROUNDS - 1, False, True)

                def tile_of(eng, tiles, c):
                    return eng.value_load(tiles[0:1, bass.ds(c, 1)], min_val=0, max_val=NT - 1)

                def spread_pass(name, turned, g_tiles, F, table, lo, s_tiles, weights, extra, acc):
                    GW = F if weights is None else 2 * D
                    XW = {None: 0, "record": D + 1, "weight": 2}[extra]
                    AW = 128 if GW + XW <= 128 else 256
                    with ExitStack() as ctx:
                        ot = sb(name + "_ot", [T, 2, GC, T], BF16, ctx)
                        gw = sb(name + "_gw", [T, 2, 4, GW], F32, ctx)
                        oh = sb(name + "_oh", [T, 2, 4, T], F32, ctx)
                        places = sb(name + "_places", [T, 2, 4], F32, ctx)
                        placed4 = take_sem(ctx, name + "_places_set")
                        rec = sb(name + "_rec", [T, 2, GC, RW], F32, ctx) if extra == "record" else None
                        gps = ctx.enter_context(nc.psum_tensor(name + "_gps", [T, 2, 4, 128], F32))
                        aps = ctx.enter_context(nc.psum_tensor(name + "_aps", [T, 2, 4, AW], F32))
                        sem = lambda n: take_sem(ctx, f"{name}_{n}")
                        ot_loaded = [sem(f"ot_loaded{i}") for i in range(2)]
                        rec_loaded = [sem(f"rec_loaded{i}") for i in range(2)]
                        gathered, weighted, marked, summed, added, cleared = map(
                            sem, ["gathered", "weighted", "marked", "summed", "added", "cleared"])
                        block = ctx.enter_context(nc.Block())

                        @block.sync
                        def _(sp):
                            def body(t, first, last):
                                for n in range(2):
                                    g = bass.ds(t * 2 + n, 1)
                                    if not first:
                                        sp.wait_ge(gathered, t * 4 + (2 * n - 2))
                                    sp.dma_start(ot[:, n, :, :].rearrange("p c e -> p (c e)"),
                                                 onehots[turned, g, :, :].rearrange("a p w -> (a p) w")).then_inc(ot_loaded[n], 16)
                                    if rec is not None:
                                        if not first:
                                            sp.wait_ge(summed, t * 4 + (2 * n - 2))
                                        sp.dma_start(rec[:, n, :, :].rearrange("p c w -> p (c w)"),
                                                     rec_groups[g, :, :].rearrange("a p w -> (a p) w")).then_inc(rec_loaded[n], 16)
                            peeled(sp, body)

                        @block.gpsimd
                        def _(pool):
                            def marking(t, first, last):
                                for k in range(4):
                                    if not (first and k < 2):
                                        wait_value(pool, summed, t * 4 + (k - 1))
                                    nc.gpsimd.tensor_copy(places[:, k % 2, :], lo[:, bass.ds(t * 16 + 4 * k, 4)]).then_inc(placed4, 1)
                                    wait_value(pool, placed4, t * 4 + (k + 1))
                                    for j in range(4):
                                        last_ = nc.gpsimd.tensor_scalar(oh[:, k % 2, j, :], iota1[:, :], places[:, k % 2, j:j + 1], None,
                                                                        ALU.is_equal)
                                    last_.then_inc(marked, 1)
                            peeled(pool, marking)

                        @block.tensor
                        def _(pe):
                            def gather(t, k, first):
                                n, j0 = k // 2, 4 * (k % 2)
                                if k % 2 == 0:
                                    pe.wait_ge(ot_loaded[n], t * 16 + 16)
                                if not (first and k < 2):
                                    pe.wait_ge(weighted, t * 4 + (k - 1))
                                for j in range(4):
                                    tile = tile_of(pe, g_tiles, t * 16 + (4 * k + j))
                                    for part in range(3):
                                        last = nc.tensor.matmul(gps[:, k % 2, j, 0:F], ot[:, n, j0 + j, :],
                                                                table[:, bass.ds(tile, 1), part, :].rearrange("p a d -> p (a d)"),
                                                                start=(part == 0), stop=(part == 2), skip_group_check=True)
                                last.then_inc(gathered, 1)

                            def add_up(t, k, first):
                                n, j0 = k // 2, 4 * (k % 2)
                                pe.wait_ge(weighted, t * 4 + (k + 1))
                                pe.wait_ge(marked, t * 4 + (k + 1))
                                if rec is not None and k % 2 == 0:
                                    pe.wait_ge(rec_loaded[n], t * 16 + 16)
                                if not (first and k < 2):
                                    pe.wait_ge(added, t * 16 + 4 * (k - 1))
                                for j in range(4):
                                    w = oh[:, k % 2, j, :]
                                    last = nc.tensor.matmul(aps[:, k % 2, j, 0:GW], w, gw[:, k % 2, j, :], start=True, stop=True,
                                                            skip_group_check=True)
                                    if extra == "record":
                                        last = nc.tensor.matmul(aps[:, k % 2, j, GW:GW + XW], w, rec[:, n, j0 + j, 0:XW],
                                                                start=True, stop=True, skip_group_check=True)
                                    if extra == "weight":
                                        last = nc.tensor.matmul(aps[:, k % 2, j, GW:GW + XW], w,
                                                                weights[:, bass.ds(t * 16 + (4 * k + j), 1), :].rearrange("p a h -> p (a h)"),
                                                                start=True, stop=True, skip_group_check=True)
                                last.then_inc(summed, 1)

                            def body(t, first, last):
                                for k in range(4):
                                    if k < 3:
                                        gather(t, k + 1, first)
                                    elif not last:
                                        gather(t + 1, 0, False)
                                    add_up(t, k, first)
                            gather(0, 0, True)
                            peeled(pe, body)

                        @block.vector
                        def _(dve):
                            nc.vector.memset(acc[:, :, :], 0.0).then_inc(cleared, 1)
                            dve.wait_ge(cleared, 1)

                            def weigh(t, k, first):
                                dve.wait_ge(gathered, t * 4 + (k + 1))
                                if not (first and k < 2):
                                    dve.wait_ge(summed, t * 4 + (k - 1))
                                g = gps[:, k % 2, :, 0:F]
                                if weights is None:
                                    nc.vector.tensor_scalar(gw[:, k % 2, :, :], g, 1.0, None, ALU.mult).then_inc(weighted, 1)
                                elif F == D:
                                    w = weights[:, bass.ds(t * 16 + 4 * k, 4), :]
                                    for h in range(H):
                                        last = nc.vector.tensor_tensor(gw[:, k % 2, :, h * D:(h + 1) * D], g,
                                                                       w[:, :, h:h + 1].to_broadcast([T, 4, D]), ALU.mult)
                                    last.then_inc(weighted, 1)
                                else:
                                    w = weights[:, bass.ds(t * 16 + 4 * k, 4), :].rearrange("p c h -> p (c h)")
                                    nc.vector.tensor_tensor(gw[:, k % 2, :, :].rearrange("p c (h d) -> p (c h) d", h=H),
                                                            gps[:, k % 2, :, :].rearrange("p c (h d) -> p (c h) d", h=H),
                                                            w.unsqueeze(2).to_broadcast([T, 4 * H, D]), ALU.mult).then_inc(weighted, 1)

                            def add(t, k, first):
                                dve.wait_ge(summed, t * 4 + (k + 1))
                                for j in range(4):
                                    tile = tile_of(dve, s_tiles, t * 16 + (4 * k + j))
                                    a = acc[:, bass.ds(tile, 1), :].rearrange("p a w -> p (a w)")
                                    if not (first and k == j == 0):
                                        dve.wait_ge(added, t * 16 + (4 * k + j))
                                    nc.vector.tensor_tensor(a, a, aps[:, k % 2, j, 0:GW + XW], ALU.add).then_inc(added, 1)

                            def body(t, first, last):
                                for k in range(4):
                                    if k < 3:
                                        weigh(t, k + 1, first)
                                    elif not last:
                                        weigh(t + 1, 0, False)
                                    add(t, k, first)
                            weigh(0, 0, True)
                            peeled(dve, body)

                def pick_pass(name, sides, finish):
                    NS = len(sides)
                    with ExitStack() as ctx:
                        ot = sb(name + "_ot", [T, 2, NS, GC, T], BF16, ctx)
                        val = sb(name + "_val", [T, 2, GC, H], F32, ctx)
                        ps = ctx.enter_context(nc.psum_tensor(name + "_ps", [T, 2, 512], F32))
                        sem = lambda n: take_sem(ctx, f"{name}_{n}")
                        loaded = [sem(f"loaded{i}") for i in range(2)]
                        picked, taken, chain, ready = map(sem, ["picked", "taken", "chain", "ready"])
                        block = ctx.enter_context(nc.Block())

                        def groups(eng, body):
                            body(0, True)
                            with eng.Fori(1, ROUNDS) as t:
                                body(t, False)

                        @block.sync
                        def _(sp):
                            def body(t, first):
                                for n in range(2):
                                    if not first:
                                        sp.wait_ge(picked, t * 2 + (n - 1))
                                    for i, (turned, _, _) in enumerate(sides):
                                        sp.dma_start(ot[:, n, i, :, :].rearrange("p c e -> p (c e)"),
                                                     onehots[turned, bass.ds(t * 2 + n, 1), :, :].rearrange("a p w -> (a p) w")).then_inc(loaded[n], 16)
                            groups(sp, body)

                        @block.tensor
                        def _(pe):
                            def body(t, first):
                                for n in range(2):
                                    pe.wait_ge(loaded[n], t * (16 * NS) + 16 * NS)
                                    if not first:
                                        pe.wait_ge(taken, t * 2 + (n - 1))
                                    for j in range(GC):
                                        for i, (_, tiles, table) in enumerate(sides):
                                            tile = tile_of(pe, tiles, t * (2 * GC) + (n * GC + j))
                                            last = nc.tensor.matmul(ps[:, n, (j * NS + i) * 6:(j * NS + i) * 6 + 6], ot[:, n, i, j, :],
                                                                    table[:, bass.ds(tile, 1), :, :].rearrange("p a k h -> p (a k h)"),
                                                                    start=True, stop=True, skip_group_check=True)
                                    last.then_inc(picked, 1)
                            groups(pe, body)

                        @block.vector
                        def _(dve):
                            def body(t, first):
                                for n in range(2):
                                    dve.wait_ge(picked, t * 2 + (n + 1))
                                    nc.vector.tensor_reduce(val[:, n, :, :], ps[:, n, 0:GC * NS * 6].rearrange("p (c k h) -> p c h k", c=GC, h=H),
                                                            AX.X, ALU.add).then_inc(taken, 1)
                                    dve.wait_ge(taken, t * 2 + (n + 1))
                                    finish(dve, val[:, n, :, :], bass.ds(t * (2 * GC) + n * GC, GC), chain, t * 2 + (n + 1))
                            groups(dve, body)

                def max_pass(name, shifted, top_of):
                    with ExitStack() as ctx:
                        oh = sb(name + "_oh", [T, 2, 4, T], F32, ctx)
                        places = sb(name + "_places", [T, 2, 4], F32, ctx)
                        placed4 = take_sem(ctx, name + "_places_set")
                        diag = sb(name + "_diag", [T, 2, 4, H, T], F32, ctx)
                        best = sb(name + "_best", [T, 2, 4, H], F32, ctx)
                        aps = ctx.enter_context(nc.psum_tensor(name + "_aps", [T, 2, 4, H * T], F32))
                        sem = lambda n: take_sem(ctx, f"{name}_{n}")
                        marked, spread, placed, reduced, cleared, noted = map(sem, ["marked", "spread", "placed", "reduced", "cleared", "noted"])
                        block = ctx.enter_context(nc.Block())

                        @block.gpsimd
                        def _(pool):
                            def marking(t, first, last):
                                for k in range(4):
                                    if not (first and k < 2):
                                        wait_value(pool, placed, t * 4 + (k - 1))
                                    nc.gpsimd.tensor_copy(places[:, k % 2, :], src_lo[:, bass.ds(t * 16 + 4 * k, 4)]).then_inc(placed4, 1)
                                    wait_value(pool, placed4, t * 4 + (k + 1))
                                    for j in range(4):
                                        last_ = nc.gpsimd.tensor_scalar(oh[:, k % 2, j, :], iota1[:, :], places[:, k % 2, j:j + 1], None,
                                                                        ALU.is_equal)
                                    last_.then_inc(marked, 1)
                            peeled(pool, marking)

                        @block.scalar
                        def _(act):
                            def spreading(t, first, last):
                                for k in range(4):
                                    if not (first and k < 2):
                                        wait_value(act, placed, t * 4 + (k - 1))
                                    for j in range(4):
                                        for h in range(H):
                                            last_ = nc.scalar.activation(
                                                diag[:, k % 2, j, h, :], ident[:, :], ACT.Copy,
                                                scale=shifted[:, bass.ds(t * 16 + (4 * k + j), 1), h:h + 1].rearrange("p a h -> p (a h)"))
                                    last_.then_inc(spread, 1)
                            peeled(act, spreading)

                        @block.tensor
                        def _(pe):
                            def place(t, first, last):
                                for k in range(4):
                                    pe.wait_ge(marked, t * 4 + (k + 1))
                                    pe.wait_ge(spread, t * 4 + (k + 1))
                                    if not (first and k < 2):
                                        pe.wait_ge(reduced, t * 4 + (k - 1))
                                    for j in range(4):
                                        last_ = nc.tensor.matmul(aps[:, k % 2, j, :], oh[:, k % 2, j, :],
                                                                 diag[:, k % 2, j, :, :].rearrange("p h e -> p (h e)"), start=True, stop=True,
                                                                 skip_group_check=True)
                                    last_.then_inc(placed, 1)
                            peeled(pe, place)

                        @block.vector
                        def _(dve):
                            nc.vector.memset(top_of[:, :, :], 0.0).then_inc(cleared, 1)
                            dve.wait_ge(cleared, 1)

                            def largest(t, first, last):
                                for k in range(4):
                                    dve.wait_ge(placed, t * 4 + (k + 1))
                                    nc.vector.tensor_reduce(best[:, k % 2, :, :].rearrange("p c h -> p (c h)"),
                                                            aps[:, k % 2, :, :].rearrange("p c (h e) -> p (c h) e", h=H), AX.X, ALU.max).then_inc(reduced, 1)
                                    dve.wait_ge(reduced, t * 4 + (k + 1))
                                    for j in range(4):
                                        tile = tile_of(dve, src_tile, t * 16 + (4 * k + j))
                                        m = top_of[:, bass.ds(tile, 1), :].rearrange("p a h -> p (a h)")
                                        if not (first and k == j == 0):
                                            dve.wait_ge(noted, t * 16 + (4 * k + j))
                                        nc.vector.tensor_tensor(m, m, best[:, k % 2, j, :], ALU.max).then_inc(noted, 1)
                            peeled(dve, largest)


                def near(name, parts, extra, acc):
                    spread_pass(name, 0, src_tile, D, parts, dst_lo, dst_tile, None, extra, acc)

                def spread(name, parts, first, w_edge, acc):
                    spread_pass(name, 1, dst_tile, D if first else 2 * D, parts, src_lo, src_tile, w_edge,
                                "weight" if first else None, acc)

                def attention(nm, l, pick_src, pick_dst, w_edge, rest2):
                    def edge_scores(dve, val, cols, chain, n):
                        nc.vector.tensor_tensor(val, val, s_rel[:, cols, 2 * l:2 * l + 2], ALU.add).then_inc(chain, 1)
                        dve.wait_ge(chain, n)
                        nc.vector.scalar_tensor_tensor(out=w_edge[:, cols, :], in0=val, scalar=0.01, in1=val, op0=ALU.mult, op1=ALU.max)
                    pick_pass(nm + "_edge", [(0, src_tile, pick_src), (1, dst_tile, pick_dst)], edge_scores)

                    with ExitStack() as ctx:
                        s_least, s_all = take_sem(ctx, nm + "_least"), take_sem(ctx, nm + "_all_least")
                        chain = take_sem(ctx, nm + "_least_chain")
                        block = ctx.enter_context(nc.Block())

                        @block.vector
                        def _(dve):
                            ln = Chain(dve, chain)
                            ln.step(nc.vector.tensor_reduce(least[:, 0:1], w_edge[:, :, :].rearrange("p c h -> p (c h)"), AX.X, ALU.min))
                            nc.vector.tensor_scalar(least[:, 1:2], least[:, 0:1], -1.0, None, ALU.mult).then_inc(s_least, 1)
                            dve.wait_ge(s_all, 1)
                            ln.step(nc.vector.tensor_scalar(least[:, 3:4], least[:, 2:3], 1.0, None, ALU.add))
                            nc.vector.tensor_scalar(shifted[:, :, :], w_edge[:, :, :], least[:, 3:4], None, ALU.add)

                        @block.gpsimd
                        def _(pool):
                            pool.wait_ge(s_least, 1)
                            nc.gpsimd.partition_all_reduce(least[:, 2:3], least[:, 1:2], T, bass.bass_isa.ReduceOp.max).then_inc(s_all, 1)
                    max_pass(nm + "_max", shifted, top_of)

                    def unshift(ln, dve, i, o):
                        ln.step(nc.vector.tensor_scalar(top_of[:, :, :], top_of[:, :, :], least[:, 3:4], None, ALU.subtract))
                        split_steps(nc, ln, pick_src, top_of[:, :, :], rest2[:, :, :])
                    vector_steps(nm + "_unshift", unshift)

                    def below_top(dve, val, cols, chain, n):
                        nc.vector.tensor_tensor(w_edge[:, cols, :], w_edge[:, cols, :], val, ALU.subtract)
                    pick_pass(nm + "_under", [(0, src_tile, pick_src)], below_top)
                    with ExitStack() as ctx:
                        block = ctx.enter_context(nc.Block())

                        @block.scalar
                        def _(act):
                            nc.scalar.activation(w_edge[:, :, :], w_edge[:, :, :], ACT.Exp)


                networks("g_", near, attention, spread, [T, NCH, H])


        def fast_path():
            SC = NT * BCH
            UNITS = [4] * (SC // 4) + ([SC % 4] if SC % 4 else [])
            NU = len(UNITS)
            RING = 5
            slot = lambda i: i % 4 if i < NU - 1 else 4
            held = lambda i: (5 if i < 4 else 4) if i < NU - 1 else NU
            rec_tiles = records[0:NT * SC * T, :].rearrange("(s p c) w -> s p (c w)", p=T, c=SC)
            OST, ODT, OS, OD = range(4)

            s_rel = sb("fs_rel", [T, NT, SC, 2 * L], F32)
            MU = [8] * (SC // 8) + [SC % 8]
            NM = len(MU)
            with ExitStack() as ctx:
                iotab = sb("iotab", [T, T], BF16, ctx)
                rec = sb("f_rec", [T, 2, SC, RW], F32, ctx)
                ident8 = sb("ident8", [T, T], F8, ctx)
                out8 = sb("f_out8", [T, 2, 4, SC * T], F8, ctx)
                psT = ctx.enter_context(nc.psum_tensor("f_psT", [T, 2, 2, 8 * T], F32))
                sem = lambda n: take_sem(ctx, "f_" + n)
                loaded = [sem(f"rec_loaded{i}") for i in range(2)]
                stored = [sem(f"onehots_stored{i}") for i in range(2)]
                marked, turned, copied, kept, s_iota = map(sem, ["marked", "turned", "copied", "kept", "iota"])
                block = ctx.enter_context(nc.Block())

                @block.sync
                def _(sp):
                    def body(t, tiles):
                        for n in tiles:
                            after(sp, kept, t, 2, n - 1, True)
                            sp.dma_start(rec[:, n, :, :].rearrange("p c w -> p (c w)"),
                                         rec_tiles[bass.ds(t * 2 + n, 1), :, :].rearrange("a p w -> (a p) w")).then_inc(loaded[n], 16)
                    tile_pairs(sp, body)

                @block.vector
                def _(dve):
                    nc.vector.tensor_copy(ident8[:, :], identb[:, :], saturate=False).then_inc(s_iota, 1)
                    nc.vector.tensor_copy(iotab[:, :], iota1[:, :]).then_inc(s_iota, 1)
                    dve.wait_ge(s_iota, 2)

                    def body(t, tiles):
                        for n in tiles:
                            after(dve, loaded[n], t, 16, 16, True)
                            after(dve, stored[n], t, 64, 0, True)
                            for i, m in enumerate(MU):
                                for k, r in enumerate((R_SRC, R_DST)):
                                    last = nc.vector.tensor_tensor(
                                        out8[:, n, 2 + k, 8 * i * T:(8 * i + m) * T].rearrange("p (c e) -> p c e", e=T),
                                        iotab[:, :].unsqueeze(1).to_broadcast([T, m, T]),
                                        rec[:, n, 8 * i:8 * i + m, r].unsqueeze(2).to_broadcast([T, m, T]), ALU.is_equal, saturate=False)
                                last.then_inc(marked, 1)
                            nc.vector.tensor_copy(s_rel[:, bass.ds(t * 2 + n, 1), :, :].rearrange("p a c k -> p (a c) k"),
                                                  rec[:, n, :, R_REL:R_REL + 2 * L]).then_inc(kept, 1)
                    tile_pairs(dve, body)

                @block.tensor
                def _(pe):
                    def body(t, tiles):
                        for n in tiles:
                            for i, m in enumerate(MU):
                                u = NM * n + i
                                after(pe, marked, t, 2 * NM, u + 1, True)
                                after(pe, copied, t, 2 * NM, u - 1, True)
                                for k in range(2):
                                    for c in range(m):
                                        o = (8 * i + c) * T
                                        last = nc.tensor.matmul(psT[:, u % 2, k, c * T:(c + 1) * T], out8[:, n, 2 + k, o:o + T], ident8[:, :],
                                                                start=True, stop=True, skip_group_check=True)
                                last.then_inc(turned, 1)
                    tile_pairs(pe, body)

                @block.scalar
                def _(act):
                    def body(t, tiles):
                        for n in tiles:
                            after(act, stored[n], t, 64, 0, True)
                            for i, m in enumerate(MU):
                                u = NM * n + i
                                after(act, turned, t, 2 * NM, u + 1, True)
                                for k in range(2):
                                    last = nc.scalar.activation(out8[:, n, k, 8 * i * T:(8 * i + m) * T], psT[:, u % 2, k, 0:m * T], ACT.Copy, saturate=False)
                                last.then_inc(copied, 1)
                            after(act, copied, t, 2 * NM, NM * (n + 1), True)
                            for k in range(4):
                                act.dma_start(onehots8[k, bass.ds(t * 2 + n, 1), :, :].rearrange("a p w -> (a p) w"),
                                              out8[:, n, k, :].bitcast(U8)).then_inc(stored[n], 16)
                    tile_pairs(act, body)
                    act.wait_ge(stored[0], 64 * (NT // 2 + 1))
                    act.wait_ge(stored[1], 64 * (NT // 2))

            def load_onehots(sp, ot, kinds, t, n, loaded):
                for j, k in enumerate(kinds):
                    sp.dma_start(ot[:, n, j, :].bitcast(U8), onehots8[k, bass.ds(t * 2 + n, 1), :, :].rearrange("a p w -> (a p) w")).then_inc(loaded[n], 16)

            def spread_units(name, kinds, F, table, weights, extra, acc, by_target):
                GW = {None: F, "record": 2 * D, "weight": 2 * D + 2, "heads": 2 * D}[extra]
                AW = GW + (1 if extra == "record" else 0)
                with ExitStack() as ctx:
                    ot = sb(name + "_ot", [T, 2, 2, SC * T], F8, ctx)
                    gw = sb(name + "_gw", [T, RING, 4, GW], F32, ctx)
                    rest = sb(name + "_rest", [T, RING, 4, GW], F32, ctx)
                    parts = sb(name + "_parts", [T, RING, 3, 4, GW], BF16, ctx)
                    if by_target:
                        stab = sb(name + "_stab", [T, 2, 3, D], BF16, ctx)
                    if extra == "record":
                        rec = sb(name + "_rec", [T, 2, SC, RW], F32, ctx)
                        one = sb(name + "_one", [T, 1], BF16, ctx)
                    gps = ctx.enter_context(nc.psum_tensor(name + "_gps", [T, RING, 4, 128], F32))
                    aps = ctx.enter_context(nc.psum_tensor(name + "_aps", [T, 2, 2, 256], F32))
                    sem = lambda n: take_sem(ctx, f"{name}_{n}")
                    loaded = [sem(f"onehots_in{i}") for i in range(2)]
                    rec_in = [sem(f"rec_in{i}") for i in range(2)]
                    staged, gathered, weighted, high, rested, middle, low, summed, added, cleared = map(
                        sem, ["staged", "gathered", "weighted", "high", "rested", "middle", "low", "summed", "added", "cleared"])
                    block = ctx.enter_context(nc.Block())

                    def done(eng, sem, t, n, i, apart=False):
                        after(eng, sem, t, 2 * NU, NU * n + i + 1, apart)

                    def freed(eng, sem, t, n, i, apart=False):
                        after(eng, sem, t, 2 * NU, NU * n + i + 1 - held(i), apart)

                    @block.sync
                    def _(sp):
                        def body(t, tiles):
                            for n in tiles:
                                after(sp, summed, t, 2 * NU, NU * (n - 1), True)
                                load_onehots(sp, ot, kinds, t, n, loaded)
                                if extra == "record":
                                    sp.dma_start(rec[:, n, :, :].rearrange("p c w -> p (c w)"),
                                                 rec_tiles[bass.ds(t * 2 + n, 1), :, :].rearrange("a p w -> (a p) w")).then_inc(rec_in[n], 16)
                        tile_pairs(sp, body)

                    @block.tensor
                    def _(pe):
                        def gather(t, n, i):
                            if i == 0:
                                after(pe, loaded[n], t, 32, 32, True)
                                if by_target:
                                    after(pe, staged, t, 2, n + 1, True)
                            freed(pe, weighted, t, n, i, True)
                            for j in range(UNITS[i]):
                                c = 4 * i + j
                                for part in range(3):
                                    rhs = stab[:, n, part, :] if by_target else table[:, c // BCH, part, :]
                                    last = nc.tensor.matmul(gps[:, slot(i), j, 0:F], ot[:, n, 0, c * T:(c + 1) * T], rhs,
                                                            start=(part == 0), stop=(part == 2), skip_group_check=True)
                            last.then_inc(gathered, 1)

                        def total(t, n, i):
                            done(pe, low, t, n, i, True)
                            if by_target:
                                after(pe, added, t, 2 * NU, NU * n + i - 1, True)
                            elif i == 0:
                                after(pe, added, t, 2, n - 1, True)
                            for j in range(UNITS[i]):
                                c = 4 * i + j
                                w = ot[:, n, 1, c * T:(c + 1) * T]
                                if by_target:
                                    o = aps[:, (NU * n + i) % 2, j // BCH, :]
                                    first, last_ = j % BCH == 0, j % BCH == BCH - 1
                                else:
                                    o = aps[:, n, 0, :]
                                    first, last_ = c == 0, c == SC - 1
                                if extra == "record":
                                    nc.tensor.matmul(o[:, GW:GW + 1], w, one[:, :], start=first, stop=last_, skip_group_check=True)
                                for part in range(3):
                                    last = nc.tensor.matmul(o[:, 0:GW], w, parts[:, slot(i), part, j, :],
                                                            start=first and part == 0 and extra != "record",
                                                            stop=last_ and part == 2, skip_group_check=True)
                            last.then_inc(summed, 1)
                        skewed(pe, NU, [(4, gather), (0, total)])

                    @block.vector
                    def _(dve):
                        if by_target:
                            nc.vector.memset(acc[:, :, :], 0.0).then_inc(cleared, 1)
                            dve.wait_ge(cleared, 1)
                        if extra == "record":
                            nc.vector.memset(one[:, :], 1.0)

                        def weigh(t, n, i):
                            m = UNITS[i]
                            done(dve, gathered, t, n, i)
                            g, o = gps[:, slot(i), 0:m, 0:F], gw[:, slot(i), 0:m, :]
                            if extra == "record":
                                if i == 0:
                                    after(dve, rec_in[n], t, 16, 16)
                                nc.vector.tensor_copy(o[:, :, D:2 * D], rec[:, n, 4 * i:4 * i + m, 0:D])
                            if weights is None:
                                nc.vector.tensor_copy(o[:, :, 0:D], g).then_inc(weighted, 1)
                                return
                            w = weights[:, bass.ds(t * 2 + n, 1), 4 * i:4 * i + m, :].rearrange("p a c h -> p (a c) h")
                            if extra == "weight":
                                nc.vector.tensor_scalar(o[:, :, 2 * D:2 * D + 2], w, 1.0, None, ALU.mult)
                            heads = o[:, :, 0:2 * D].rearrange("p c (h d) -> p c h d", h=H)
                            g = g.unsqueeze(2).to_broadcast([T, m, H, D]) if F == D else g.rearrange("p c (h d) -> p c h d", h=H)
                            nc.vector.tensor_tensor(heads, g, w.unsqueeze(3).to_broadcast([T, m, H, D]), ALU.mult).then_inc(weighted, 1)

                        def stage_table(t, n, i):
                            if i == 0:
                                after(dve, gathered, t, 2 * NU, NU * (n - 1))
                                nc.vector.tensor_scalar(stab[:, n, :, :].rearrange("p k d -> p (k d)"),
                                                        table[:, bass.ds(t * 2 + n, 1), :, :].rearrange("p a k d -> p (a k d)"),
                                                        1.0, None, ALU.mult).then_inc(staged, 1)

                        def lowest(t, n, i):
                            m = UNITS[i]
                            done(dve, middle, t, n, i)
                            nc.vector.tensor_tensor(parts[:, slot(i), 2, 0:m, :], rest[:, slot(i), 0:m, :], parts[:, slot(i), 1, 0:m, :],
                                                    ALU.subtract).then_inc(low, 1)

                        def add(t, n, i):
                            done(dve, summed, t, n, i)
                            if by_target:
                                m = UNITS[i] // BCH
                                after(dve, added, t, 2 * NU, NU * n + i)
                                a = acc[:, 2 * i:2 * i + m, 0:AW]
                                nc.vector.tensor_tensor(a, a, aps[:, (NU * n + i) % 2, 0:m, 0:AW], ALU.add).then_inc(added, 1)
                            elif i == NU - 1:
                                nc.vector.tensor_scalar(acc[:, bass.ds(t * 2 + n, 1), 0:AW].rearrange("p a w -> p (a w)"),
                                                        aps[:, n, 0, 0:AW], 1.0, None, ALU.mult).then_inc(added, 1)

                        def add_last(t, n, i):
                            if by_target or i == NU - 1:
                                add(t, n, i)
                        stages = [(3, weigh), (0, lowest), (-1, add_last)]
                        if by_target:
                            stages = [(8, stage_table)] + stages
                        skewed(dve, NU, stages)

                    @block.scalar
                    def _(act):
                        def highest(t, n, i):
                            m = UNITS[i]
                            done(act, weighted, t, n, i)
                            freed(act, summed, t, n, i)
                            nc.scalar.activation(parts[:, slot(i), 0, 0:m, :], gw[:, slot(i), 0:m, :], ACT.Copy).then_inc(high, 1)

                        def mid(t, n, i):
                            m = UNITS[i]
                            done(act, rested, t, n, i)
                            nc.scalar.activation(parts[:, slot(i), 1, 0:m, :], rest[:, slot(i), 0:m, :], ACT.Copy).then_inc(middle, 1)
                        skewed(act, NU, [(0, mid), (2, highest)])

                    @block.gpsimd
                    def _(pool):
                        def remains(t, n, i):
                            m = UNITS[i]
                            done(pool, high, t, n, i)
                            nc.gpsimd.tensor_tensor(rest[:, slot(i), 0:m, :], gw[:, slot(i), 0:m, :], parts[:, slot(i), 0, 0:m, :],
                                                    ALU.subtract).then_inc(rested, 1)
                        skewed(pool, NU, [(0, remains)])

            def attention(name, l, pick_src, pick_dst, w_edge, rest2):
                NG4 = -(-SC // 4)
                CMP = ["D", "D"] + ["A", "P", "A", "D"] * ((NG4 - 2) // 4 + 1)
                CMP = CMP[:NG4 - 1] + ["D"]
                AK, PK = ([k for k in range(NG4) if CMP[k] == e] for e in "AP")
                size_of = lambda k: min(4, SC - 4 * k)
                with ExitStack() as ctx:
                    ot = sb(name + "_ot", [T, 2, 3, SC * T], F8, ctx)
                    stab = sb(name + "_stab", [T, 2, 6], BF16, ctx)
                    mtab = sb(name + "_mtab", [T, 2, 3, H], BF16, ctx)
                    val = sb(name + "_val", [T, SC, H], F32, ctx)
                    score = sb(name + "_score", [T, 2, SC, H], F32, ctx)
                    shifted = sb(name + "_shifted", [T, 2, SC, H], F32, ctx)
                    run = sb(name + "_run", [T, 2, 4, H, T], BF16, ctx)
                    prod_d = sb(name + "_prod_d", [T, 2, 4, H, T], BF16, ctx)
                    prod_a = sb(name + "_prod_a", [T, len(AK), 4, H, T], BF16, ctx)
                    prod_p = sb(name + "_prod_p", [T, len(PK), 4, H, T], BF16, ctx)
                    merge = sb(name + "_merge", [T, 7, H, T], BF16, ctx)
                    top1 = sb(name + "_top", [T, 3, H], F32, ctx)
                    under_ = sb(name + "_under", [T, SC, H], F32, ctx)
                    diff = sb(name + "_diff", [T, 2, SC, H], F32, ctx)
                    size = sb(name + "_size", [T, 3, 4 * D], F32, ctx)
                    shift = sb(name + "_shift", [T, 4], F32, ctx)
                    pick_ps = ctx.enter_context(nc.psum_tensor(name + "_pick", [T, 2, 512], F32))
                    under_ps = ctx.enter_context(nc.psum_tensor(name + "_upick", [T, 512], F32))
                    turn_ps = ctx.enter_context(nc.psum_tensor(name + "_turn", [T, H, T], BF16))
                    sem = lambda n: take_sem(ctx, f"{name}_{n}")
                    loaded = [sem(f"onehots_in{i}") for i in range(2)]
                    targets_in = [sem(f"targets_in{i}") for i in range(2)]
                    (staged, picked, taken, scored, made_d, made_a, made_p, folded, halved, merged, turned, topped, undered, below_, expd,
                     s_chain, t_chain, u_chain, setup) = map(
                        sem, ["staged", "picked", "taken", "scored", "made_d", "made_a", "made_p", "folded", "halved", "merged", "turned", "topped",
                              "undered", "below", "expd", "s_chain", "t_chain", "u_chain", "setup"])
                    block = ctx.enter_context(nc.Block())
                    HALF = SC // 2

                    def factors(n, k):
                        m, shape = size_of(k), [T, size_of(k), H, T]
                        return (ot[:, n, 1, 4 * k * T:(4 * k + m) * T].rearrange("p (c e) -> p c e", e=T).unsqueeze(2).to_broadcast(shape),
                                shifted[:, n, 4 * k:4 * k + m, :].unsqueeze(3).to_broadcast(shape))

                    @block.sync
                    def _(sp):
                        def body(t, tiles):
                            for n in tiles:
                                for j, (k, used) in enumerate(((ODT, picked), (OS, merged), (OST, undered))):
                                    after(sp, used, t, 2, n - 1, True)
                                    sp.dma_start(ot[:, n, j, :].bitcast(U8),
                                                 onehots8[k, bass.ds(t * 2 + n, 1), :, :].rearrange("a p w -> (a p) w")
                                                 ).then_inc(targets_in[n] if k == ODT else loaded[n], 16)
                        tile_pairs(sp, body)

                    @block.tensor
                    def _(pe):
                        def pick_target(t, n, i):
                            after(pe, targets_in[n], t, 16, 16, True)
                            after(pe, taken, t, 2, n, True)
                            for c in range(SC):
                                o = pick_ps[:, c // HALF, (c % HALF) * 12:(c % HALF) * 12 + 12]
                                nc.tensor.matmul(o[:, 6:12], ot[:, n, 0, c * T:(c + 1) * T],
                                                 pick_dst[:, c // BCH, :, :].rearrange("p k h -> p (k h)"), start=True, stop=True,
                                                 skip_group_check=True)

                        def pick_source(t, n, i):
                            after(pe, loaded[n], t, 32, 32, True)
                            after(pe, staged, t, 2, n + 1, True)
                            for c in range(SC):
                                o = pick_ps[:, c // HALF, (c % HALF) * 12:(c % HALF) * 12 + 12]
                                last = nc.tensor.matmul(o[:, 0:6], ot[:, n, 2, c * T:(c + 1) * T], stab[:, n, :], start=True, stop=True,
                                                        skip_group_check=True)
                            last.then_inc(picked, 1)

                        def turn(t, n, i):
                            after(pe, merged, t, 2, n + 1, True)
                            for h in range(H):
                                last = nc.tensor.transpose(turn_ps[:, h, :], merge[:, 6, h, :], identb[:, :])
                            last.then_inc(turned, 1)

                        def pick_top(t, n, i):
                            after(pe, topped, t, 2, n + 1, True)
                            after(pe, below_, t, 2, n, True)
                            for c in range(SC):
                                last = nc.tensor.matmul(under_ps[:, c * 6:c * 6 + 6], ot[:, n, 2, c * T:(c + 1) * T],
                                                        mtab[:, n, :, :].rearrange("p k h -> p (k h)"), start=True, stop=True,
                                                        skip_group_check=True)
                            last.then_inc(undered, 1)
                        skewed(pe, 1, [(1, pick_target), (-1, turn), (-1, pick_top), (1, pick_source)])

                    @block.vector
                    def _(dve):
                        ln = Chain(dve, setup)
                        for k, a in enumerate((aht[:, l, :], ar[:, :])):
                            ln.step(nc.vector.tensor_scalar(size[:, k, :], a, -1.0, None, ALU.mult))
                            ln.step(nc.vector.tensor_tensor(size[:, k, :], size[:, k, :], a, ALU.max))
                            ln.step(nc.vector.tensor_reduce(shift[:, k:k + 1], size[:, k, :], AX.X, ALU.add))
                        ln.step(nc.vector.tensor_tensor(shift[:, 2:3], shift[:, 0:1], shift[:, 1:2], ALU.add))
                        ln.step(nc.vector.tensor_scalar(shift[:, 3:4], shift[:, 2:3], 0.01, 1.0, ALU.mult, ALU.add))

                        def get_scores(t, n, i):
                            after(dve, picked, t, 2, n + 1)
                            for b in range(2):
                                last = nc.vector.tensor_reduce(val[:, b * HALF:(b + 1) * HALF, :],
                                                               pick_ps[:, b, 0:HALF * 12].rearrange("p (c k h) -> p c h k", c=HALF, h=H),
                                                               AX.X, ALU.add)
                            last.then_inc(taken, 1)
                            after(dve, taken, t, 2, n + 1)
                            nc.vector.tensor_tensor(val[:, :, :], val[:, :, :],
                                                    s_rel[:, bass.ds(t * 2 + n, 1), :, 2 * l:2 * l + 2].rearrange("p a c h -> p (a c) h"),
                                                    ALU.add).then_inc(s_chain, 1)
                            after(dve, s_chain, t, 4, 2 * n + 1)
                            nc.vector.scalar_tensor_tensor(out=score[:, n, :, :], in0=val[:, :, :], scalar=0.01, in1=val[:, :, :],
                                                           op0=ALU.mult, op1=ALU.max).then_inc(s_chain, 1)
                            after(dve, s_chain, t, 4, 2 * n + 2)
                            nc.vector.tensor_scalar(shifted[:, n, :, :], score[:, n, :, :], shift[:, 3:4], None, ALU.add).then_inc(scored, 1)

                        def compare(t, n, k):
                            m = size_of(k)
                            to = run[:, k % 2, 0:m, :, :]
                            flat = lambda a: a.rearrange("p c h e -> p (c h e)")
                            if k < 2:
                                nc.vector.tensor_tensor(to, *factors(n, k), ALU.mult).then_inc(folded, 1)
                                return
                            if CMP[k] == "D":
                                p = prod_d[:, D_MADE.index(k) % 2, 0:m, :, :]
                                after(dve, made_d, t, 2 * len(D_MADE), len(D_MADE) * n + D_MADE.index(k) + 1, True)
                            elif CMP[k] == "A":
                                p = prod_a[:, AK.index(k), :, :, :]
                                after(dve, made_a, t, 2 * len(AK), len(AK) * n + AK.index(k) + 1, True)
                            else:
                                p = prod_p[:, PK.index(k), :, :, :]
                                after(dve, made_p, t, 2 * len(PK), len(PK) * n + PK.index(k) + 1, True)
                            after(dve, folded, t, 2 * NG4, NG4 * n + k - 1, True)
                            nc.vector.tensor_tensor(flat(to), flat(to), flat(p), ALU.max).then_inc(folded, 1)

                        def make(t, n, k):
                            nc.vector.tensor_tensor(prod_d[:, D_MADE.index(k) % 2, 0:size_of(k), :, :], *factors(n, k), ALU.mult).then_inc(made_d, 1)

                        def largest(t, n, i):
                            after(dve, folded, t, 2 * NG4, NG4 * (n + 1))
                            flat = lambda a: a.rearrange("p c h e -> p (c h e)")
                            nc.vector.tensor_tensor(flat(merge[:, 0:4, :, :]), flat(run[:, 0, :, :, :]), flat(run[:, 1, :, :, :]),
                                                    ALU.max).then_inc(halved, 1)
                            after(dve, halved, t, 4, 2 * n + 1)
                            nc.vector.tensor_tensor(flat(merge[:, 4:6, :, :]), flat(merge[:, 0:2, :, :]), flat(merge[:, 2:4, :, :]),
                                                    ALU.max).then_inc(halved, 1)
                            after(dve, halved, t, 4, 2 * n + 2)
                            nc.vector.tensor_tensor(flat(merge[:, 6:7, :, :]), flat(merge[:, 4:5, :, :]), flat(merge[:, 5:6, :, :]),
                                                    ALU.max).then_inc(merged, 1)

                        def top(t, n, i):
                            after(dve, turned, t, 2, n + 1)
                            k = 0

                            def then(ins):
                                nonlocal k
                                k += 1
                                ins.then_inc(t_chain, 1)
                                after(dve, t_chain, t, 10, 5 * n + k)
                            then(nc.vector.tensor_reduce(top1[:, 0, :], turn_ps[:, :, :], AX.X, ALU.max))
                            then(nc.vector.tensor_scalar(top1[:, 1, :], top1[:, 0, :], shift[:, 3:4], None, ALU.subtract))
                            then(nc.vector.tensor_copy(mtab[:, n, 0, :], top1[:, 1, :]))
                            then(nc.vector.tensor_tensor(top1[:, 2, :], top1[:, 1, :], mtab[:, n, 0, :], ALU.subtract))
                            then(nc.vector.tensor_copy(mtab[:, n, 1, :], top1[:, 2, :]))
                            nc.vector.tensor_tensor(mtab[:, n, 2, :], top1[:, 2, :], mtab[:, n, 1, :], ALU.subtract).then_inc(topped, 1)

                        def under(t, n, i):
                            after(dve, undered, t, 2, n + 1)
                            after(dve, expd, t, 2, n - 1)
                            nc.vector.tensor_reduce(under_[:, :, :], under_ps[:, 0:SC * 6].rearrange("p (c k h) -> p c h k", c=SC, h=H),
                                                    AX.X, ALU.add).then_inc(u_chain, 1)
                            after(dve, u_chain, t, 2, n + 1)
                            nc.vector.tensor_tensor(diff[:, n, :, :], score[:, n, :, :], under_[:, :, :], ALU.subtract).then_inc(below_, 1)
                        D_MADE = [k for k in range(2, NG4) if CMP[k] == "D"]

                        def scan(ks):
                            def f(t, n, i):
                                if ks[0] == 0:
                                    after(dve, scored, t, 2, n + 1, True)
                                for k in ks:
                                    if k + 1 in D_MADE:
                                        make(t, n, k + 1)
                                    compare(t, n, k)
                            return f
                        skewed(dve, 1, [(0, scan(range(0, 2))), (-1, top), (0, scan(range(2, 6))), (-1, under),
                                        (0, scan(range(6, NG4 - 2))), (1, get_scores), (0, scan(range(NG4 - 2, NG4))), (0, largest)])

                    @block.scalar
                    def _(act):
                        def stage(t, n, i):
                            after(act, picked, t, 2, n - 1, True)
                            nc.scalar.activation(stab[:, n, :], pick_src[:, bass.ds(t * 2 + n, 1), :, :].rearrange("p a k h -> p (a k h)"),
                                                 ACT.Copy).then_inc(staged, 1)

                        def multiply(t, n, i):
                            after(act, scored, t, 2, n + 1, True)
                            for a, k in enumerate(AK):
                                after(act, folded, t, 2 * NG4, NG4 * (n - 1) + k + 1, True)
                                for j in range(4):
                                    for h in range(H):
                                        c = 4 * k + j
                                        last = nc.scalar.activation(prod_a[:, a, j, h, :], ot[:, n, 1, c * T:(c + 1) * T], ACT.Copy,
                                                                    scale=shifted[:, n, c, h:h + 1])
                                last.then_inc(made_a, 1)

                        def weights(t, n, i):
                            after(act, below_, t, 2, n + 1, True)
                            nc.scalar.activation(w_edge[:, bass.ds(t * 2 + n, 1), :, :].rearrange("p a c h -> p (a c h)"),
                                                 diff[:, n, :, :].rearrange("p c h -> p (c h)"), ACT.Exp).then_inc(expd, 1)
                        skewed(act, 1, [(1, stage), (0, multiply), (-1, weights)])

                    @block.gpsimd
                    def _(pool):
                        def multiply(t, n, i):
                            after(pool, scored, t, 2, n + 1, True)
                            for a, k in enumerate(PK):
                                after(pool, folded, t, 2 * NG4, NG4 * (n - 1) + k + 1, True)
                                nc.gpsimd.tensor_tensor(prod_p[:, a, :, :, :], *factors(n, k), ALU.mult).then_inc(made_p, 1)
                        skewed(pool, 1, [(0, multiply)])

            def near(name, parts, extra, acc):
                spread_units(name, (OST, OD), D, parts, None, extra, acc, True)

            def spread(name, parts, first, w_edge, acc):
                spread_units(name, (ODT, OS), D if first else 2 * D, parts, w_edge, "weight" if first else "heads", acc, False)

            networks("f_", near, attention, spread, [T, NT, SC, H])

        over = nc.values_load(overfull_i[0:1, 0:1], min_val=0, max_val=1)
        with nc.If(over > 0):
            general_path()
        with nc.Else():
            fast_path()


_INS = ["x", "src", "dst", "edge_attr_64", "edge_type_500", "L0_gnn_W1", "L0_gnn_b1", "L0_gnn_W2", "L0_gnn_b2",
        "L1_gnn_relation_embed", "L1_gnn_ln_gamma", "L1_gnn_ln_beta", "L1_gnn_W_h", "L1_gnn_W_t", "L1_gnn_W_r",
        "L1_gnn_att_h", "L1_gnn_att_t", "L1_gnn_att_r", "L1_gnn_W_o"]


def kernel(**inputs):
    import numpy as np
    import concourse.bacc as bacc
    from concourse.bass_utils import run_bass_kernel_spmd as run

    nc = bacc.Bacc("TRN2", target_bir_lowering=False, num_devices=1)
    arrays, args = {}, []
    for name in _INS:
        a = np.ascontiguousarray(inputs[name])
        arrays[f"in_{name}"] = a
        args.append(nc.dram_tensor(f"in_{name}", a.shape, mybir.dt.from_np(a.dtype), kind="ExternalInput").ap())
    out = nc.dram_tensor("out_nodes", (N, D), F32, kind="ExternalOutput").ap()
    gnn_program(nc, *args, out)
    return run(nc, [arrays], core_ids=[0]).results[0]["out_nodes"]
```
